# Optimizing a Trainium2 kernel written in Bass

```python
import numpy as np
import jax
import jax.numpy as jnp

def _softmax(x, axis=-1):
    return jax.nn.softmax(x, axis=axis)

def _gelu(x):
    return jax.nn.gelu(x, approximate=True)

def _silu(x):
    return jax.nn.silu(x)

def _sigmoid(x):
    return jax.nn.sigmoid(x)

def _layernorm(x, axis=-1, eps=1e-05):
    m = jnp.mean(x, axis=axis, keepdims=True)
    v = jnp.var(x, axis=axis, keepdims=True)
    return (x - m) / jnp.sqrt(v + eps)

def _scatter_add(tgt, idx, src, axis=0):
    return tgt.at[idx].add(src)

def _segment_sum(src, seg, n):
    return jax.ops.segment_sum(src, seg, n)
kernel_name = 'mk_vit_tower_d1_tok_img1024_r4_da4367'

def setup_inputs(seed: int=0):
    np.random.seed(seed)
    _w = jnp.asarray

    def _rec_inputs():
        import jax
        import jax.numpy as jnp
        _rk = jax.random.key(seed)
        x = 7.22013e-05 + 1.00017 * jax.random.normal(jax.random.fold_in(_rk, 1), (64, 64, 256, 4), jnp.float32)
        return x
    x = _rec_inputs()

    def _L0_tok_setup():
        import jax, jax.numpy as jnp
        import numpy as np
        B, F, L, H, D = (8, 64, 256, 4, 64)
        MODEL = H * F
        WIN = 128

        def _local_mask():
            m = np.ones((L, L), dtype=bool)
            m = np.tril(m, WIN - 1)
            m = np.triu(m, -(WIN - 1))
            return jnp.asarray(m)

        def _flatten(y):
            n = y.shape[0]
            return y.transpose(0, 2, 3, 1).reshape(n, L, -1)
        key = jax.random.key(seed)
        ks = jax.random.split(key, 12)
        s = lambda n: 1.0 / np.sqrt(n)
        xav = np.sqrt(6.0 / (L + L))
        return {'x': jax.random.normal(ks[0], (B, F, L, H), jnp.float32), 'Wq_w': jax.random.normal(ks[1], (D, F), jnp.float32) * s(F), 'Wq_b': jnp.zeros((D,), jnp.float32), 'Wk_w': jax.random.normal(ks[2], (D, F), jnp.float32) * s(F), 'Wk_b': jnp.zeros((D,), jnp.float32), 'Wv_w': jax.random.normal(ks[3], (D, F), jnp.float32) * s(F), 'Wv_b': jnp.zeros((D,), jnp.float32), 'w_bias': jax.random.uniform(ks[4], (L, L), jnp.float32, -xav, xav), 'out_w': jax.random.normal(ks[5], (H * D, MODEL), jnp.float32) * s(H * D), 'out_b': jnp.zeros((MODEL,), jnp.float32), 'ln_g': jnp.ones((MODEL,), jnp.float32), 'ln_b': jnp.zeros((MODEL,), jnp.float32), 'local_mask': _local_mask()}
    _L0_tok_all = _L0_tok_setup()
    _L0_tok_in = {k: v for k, v in _L0_tok_all.items() if k in ('Wq_w', 'Wq_b', 'Wk_w', 'Wk_b', 'Wv_w', 'Wv_b', 'w_bias', 'out_w', 'out_b', 'ln_g', 'ln_b', 'local_mask')}
    del _L0_tok_all

    def _L0_attn_setup():
        import jax, jax.numpy as jnp
        import numpy as np
        H = 16
        LN_EPS = 1e-05
        key = jax.random.key(seed)
        ks = jax.random.split(key, 10)
        B, N, D = (2, 512, 256)
        s = 1.0 / np.sqrt(D).astype(np.float32)
        x = jax.random.normal(ks[0], (B, N, D), jnp.float32)
        Wq = jax.random.normal(ks[1], (D, D), jnp.float32) * s
        Wk = jax.random.normal(ks[2], (D, D), jnp.float32) * s
        Wv = jax.random.normal(ks[3], (D, D), jnp.float32) * s
        Wo = jax.random.normal(ks[4], (D, D), jnp.float32) * s
        bq = jnp.zeros((D,), jnp.float32)
        bk = jnp.zeros((D,), jnp.float32)
        bv = jnp.zeros((D,), jnp.float32)
        bo = jnp.zeros((D,), jnp.float32)
        beta = jnp.ones((H,), jnp.float32)
        t = jnp.ones((H,), jnp.float32)
        ln_w = jnp.ones((D,), jnp.float32)
        ln_b = jnp.zeros((D,), jnp.float32)
        return {'x': x, 'Wq': Wq, 'bq': bq, 'Wk': Wk, 'bk': bk, 'Wv': Wv, 'bv': bv, 'Wo': Wo, 'bo': bo, 'beta': beta, 't': t, 'ln_w': ln_w, 'ln_b': ln_b}
    _L0_attn_all = _L0_attn_setup()
    _L0_attn_in = {k: v for k, v in _L0_attn_all.items() if k in ('Wq', 'bq', 'Wk', 'bk', 'Wv', 'bv', 'Wo', 'bo', 'beta', 't', 'ln_w', 'ln_b')}
    del _L0_attn_all

    def _L0_ffn_setup():
        import jax, jax.numpy as jnp
        import numpy as np
        B, S, D, E, F = (4, 512, 256, 8, 1024)
        key = jax.random.key(seed)
        k0, k1, k2, k3 = jax.random.split(key, 4)
        x = jax.random.normal(k0, (B, S, D), dtype=jnp.float32)
        wg = jax.random.normal(k1, (D, E), dtype=jnp.float32) * 0.02
        w_gate = jax.random.normal(k2, (E, D, F), dtype=jnp.float32) * 0.02
        w_down = jax.random.normal(k3, (E, F, D), dtype=jnp.float32) * 0.02
        return {'x': x, 'wg': wg, 'w_gate': w_gate, 'w_down': w_down}
    _L0_ffn_all = _L0_ffn_setup()
    _L0_ffn_in = {k: v for k, v in _L0_ffn_all.items() if k in ('wg', 'w_gate', 'w_down')}
    del _L0_ffn_all
    return {'x': x, 'L0_tok_Wq_w': _L0_tok_in['Wq_w'], 'L0_tok_Wq_b': _L0_tok_in['Wq_b'], 'L0_tok_Wk_w': _L0_tok_in['Wk_w'], 'L0_tok_Wk_b': _L0_tok_in['Wk_b'], 'L0_tok_Wv_w': _L0_tok_in['Wv_w'], 'L0_tok_Wv_b': _L0_tok_in['Wv_b'], 'L0_tok_w_bias': _L0_tok_in['w_bias'], 'L0_tok_out_w': _L0_tok_in['out_w'], 'L0_tok_out_b': _L0_tok_in['out_b'], 'L0_tok_ln_g': _L0_tok_in['ln_g'], 'L0_tok_ln_b': _L0_tok_in['ln_b'], 'L0_tok_local_mask': _L0_tok_in['local_mask'], 'L0_attn_Wq': _L0_attn_in['Wq'], 'L0_attn_bq': _L0_attn_in['bq'], 'L0_attn_Wk': _L0_attn_in['Wk'], 'L0_attn_bk': _L0_attn_in['bk'], 'L0_attn_Wv': _L0_attn_in['Wv'], 'L0_attn_bv': _L0_attn_in['bv'], 'L0_attn_Wo': _L0_attn_in['Wo'], 'L0_attn_bo': _L0_attn_in['bo'], 'L0_attn_beta': _L0_attn_in['beta'], 'L0_attn_t': _L0_attn_in['t'], 'L0_attn_ln_w': _L0_attn_in['ln_w'], 'L0_attn_ln_b': _L0_attn_in['ln_b'], 'L0_ffn_wg': _L0_ffn_in['wg'], 'L0_ffn_w_gate': _L0_ffn_in['w_gate'], 'L0_ffn_w_down': _L0_ffn_in['w_down']}

def reference(x, L0_tok_Wq_w, L0_tok_Wq_b, L0_tok_Wk_w, L0_tok_Wk_b, L0_tok_Wv_w, L0_tok_Wv_b, L0_tok_w_bias, L0_tok_out_w, L0_tok_out_b, L0_tok_ln_g, L0_tok_ln_b, L0_tok_local_mask, L0_attn_Wq, L0_attn_bq, L0_attn_Wk, L0_attn_bk, L0_attn_Wv, L0_attn_bv, L0_attn_Wo, L0_attn_bo, L0_attn_beta, L0_attn_t, L0_attn_ln_w, L0_attn_ln_b, L0_ffn_wg, L0_ffn_w_gate, L0_ffn_w_down):
    import jax
    import jax.numpy as jnp

    def _L0_tok_ref(x, Wq_w, Wq_b, Wk_w, Wk_b, Wv_w, Wv_b, w_bias, out_w, out_b, ln_g, ln_b, local_mask):
        import jax, jax.numpy as jnp
        import numpy as np
        B, F, L, H, D = (8, 64, 256, 4, 64)
        MODEL = H * F
        WIN = 128

        def _local_mask():
            m = np.ones((L, L), dtype=bool)
            m = np.tril(m, WIN - 1)
            m = np.triu(m, -(WIN - 1))
            return jnp.asarray(m)

        def _flatten(y):
            n = y.shape[0]
            return y.transpose(0, 2, 3, 1).reshape(n, L, -1)

        def proj(w, b):
            y = jnp.einsum('nclh,dc->ndlh', x, w) + b[None, :, None, None]
            return _flatten(y)
        q = proj(Wq_w, Wq_b)
        k = proj(Wk_w, Wk_b)
        v = proj(Wv_w, Wv_b)
        wb = w_bias * local_mask.astype(w_bias.dtype)
        ew = jnp.exp(wb)
        ek = jnp.exp(k)
        num = jnp.einsum('ts,nsd->ntd', ew, ek * v)
        den = jnp.einsum('ts,nsd->ntd', ew, ek)
        y = jax.nn.sigmoid(q) * num / den
        h = y @ out_w + out_b + _flatten(x)
        mu = jnp.mean(h, axis=-1, keepdims=True)
        var = jnp.mean(jnp.square(h - mu), axis=-1, keepdims=True)
        return (h - mu) * jax.lax.rsqrt(var + 1e-05) * ln_g + ln_b

    def _L0_attn_ref(x, Wq, bq, Wk, bk, Wv, bv, Wo, bo, beta, t, ln_w, ln_b):
        import jax, jax.numpy as jnp
        import numpy as np
        H = 16
        LN_EPS = 1e-05
        B, N, D = x.shape
        dh = D // H

        def proj(W, b):
            return (x @ W.T + b).reshape(B, N, H, dh).transpose(0, 2, 1, 3)
        Q, K, V = (proj(Wq, bq), proj(Wk, bk), proj(Wv, bv))
        S = jnp.einsum('bhnd,bhmd->bhnm', Q, K) / dh ** 0.5
        W_tau = jax.nn.softmax(S, axis=-1)
        b_ = beta.reshape(1, H, 1, 1)
        t_ = t.reshape(1, H, 1, 1)
        W_sigma = 1.0 / ((1.0 + jnp.abs(S) / b_) ** 2 + t_ ** 2)
        W_sigma = W_sigma / W_sigma.sum(axis=-1, keepdims=True)
        tau = jnp.einsum('bhnm,bhmd->bhnd', W_tau, V).transpose(0, 2, 1, 3).reshape(B, N, D)
        sigma = jnp.einsum('bhnm,bhmd->bhnd', W_sigma, V).transpose(0, 2, 1, 3).reshape(B, N, D)
        f = 0.5 * tau + 0.5 * sigma
        y = f @ Wo.T + bo
        mu = y.mean(axis=-1, keepdims=True)
        var = jnp.mean((y - mu) ** 2, axis=-1, keepdims=True)
        out = x + ln_w * (y - mu) * jax.lax.rsqrt(var + LN_EPS) + ln_b
        return out

    def _L0_ffn_ref(x, wg, w_gate, w_down):
        import jax, jax.numpy as jnp
        import numpy as np
        B, S, D, E, F = (4, 512, 256, 8, 1024)
        Bb, Ss, Dd = x.shape
        Ee = wg.shape[1]
        T = Bb * Ss
        C = 2 * T // Ee
        tokens = x.reshape(T, Dd)
        logits = tokens.astype(jnp.float32) @ wg.astype(jnp.float32)
        gates = jax.nn.softmax(logits, axis=-1)
        idx1 = jnp.argmax(gates, axis=-1)
        mask1 = jax.nn.one_hot(idx1, Ee, dtype=jnp.int32)
        logits_no1 = jnp.where(mask1 > 0, -jnp.inf, logits)
        idx2 = jnp.argmax(logits_no1, axis=-1)
        mask2 = jax.nn.one_hot(idx2, Ee, dtype=jnp.int32)
        g1 = jnp.take_along_axis(gates, idx1[:, None], axis=-1)[:, 0]
        g2 = jnp.take_along_axis(gates, idx2[:, None], axis=-1)[:, 0]
        denom = jnp.clip(g1 + g2, 1e-09, None)
        g1, g2 = (g1 / denom, g2 / denom)
        loc1 = jnp.cumsum(mask1, axis=0) - mask1
        loc2 = jnp.cumsum(mask2, axis=0) - mask2 + jnp.sum(mask1, axis=0, keepdims=True)
        loc1_s = jnp.sum(loc1 * mask1, axis=-1)
        loc2_s = jnp.sum(loc2 * mask2, axis=-1)
        keep1 = (loc1_s < C).astype(x.dtype)
        keep2 = (loc2_s < C).astype(x.dtype)
        f1 = idx1 * C + jnp.minimum(loc1_s, C - 1)
        f2 = idx2 * C + jnp.minimum(loc2_s, C - 1)
        disp = jnp.zeros((Ee * C, Dd), dtype=x.dtype)
        disp = disp.at[f1].add(tokens * keep1[:, None])
        disp = disp.at[f2].add(tokens * keep2[:, None])
        disp = disp.reshape(Ee, C, Dd)
        h = jax.nn.gelu(jnp.einsum('ecd,edf->ecf', disp, w_gate), approximate=False)
        eo = jnp.einsum('ecf,efd->ecd', h, w_down).reshape(Ee * C, Dd)
        out = (g1 * keep1)[:, None].astype(x.dtype) * eo[f1] + (g2 * keep2)[:, None].astype(x.dtype) * eo[f2]
        return out.reshape(Bb, Ss, Dd)
    h = _L0_tok_ref(x, L0_tok_Wq_w, L0_tok_Wq_b, L0_tok_Wk_w, L0_tok_Wk_b, L0_tok_Wv_w, L0_tok_Wv_b, L0_tok_w_bias, L0_tok_out_w, L0_tok_out_b, L0_tok_ln_g, L0_tok_ln_b, L0_tok_local_mask)
    h = h + _L0_attn_ref(_layernorm(h, axis=-1), L0_attn_Wq, L0_attn_bq, L0_attn_Wk, L0_attn_bk, L0_attn_Wv, L0_attn_bv, L0_attn_Wo, L0_attn_bo, L0_attn_beta, L0_attn_t, L0_attn_ln_w, L0_attn_ln_b)
    h = h + _L0_ffn_ref(_layernorm(h, axis=-1), L0_ffn_wg, L0_ffn_w_gate, L0_ffn_w_down)
    return h

_drawn_inputs = setup_inputs


def setup_inputs(seed=0):
    import zlib

    import numpy as np

    out = dict(_drawn_inputs(seed))
    spreads = {'L0_tok_Wq_b': (0.0, 0.8),
     'L0_tok_Wk_b': (0.0, 0.8),
     'L0_tok_Wv_b': (0.0, 0.1),
     'L0_tok_out_b': (0.0, 0.1),
     'L0_tok_ln_g': (1.0, 0.2),
     'L0_tok_ln_b': (0.0, 0.1),
     'L0_attn_bq': (0.0, 0.646),
     'L0_attn_bk': (0.0, 0.8),
     'L0_attn_bv': (0.0, 0.1),
     'L0_attn_bo': (0.0, 0.1),
     'L0_attn_beta': (1.0, 0.6),
     'L0_attn_t': (1.0, 0.6),
     'L0_attn_ln_w': (1.0, 0.2),
     'L0_attn_ln_b': (0.0, 0.1)}
    factors = {'L0_tok_w_bias': 8.0}
    for name, (base, spread) in spreads.items():
        noise = np.random.default_rng([zlib.crc32(name.encode()), seed]).standard_normal(out[name].shape)
        drawn = base * np.exp(spread * noise) if base else spread * noise
        out[name] = jnp.asarray(drawn.astype(out[name].dtype))
    for name, factor in factors.items():
        out[name] = (out[name] * factor).astype(out[name].dtype)
    return out
```

```python
from contextlib import ExitStack

import concourse.bass as bass
from concourse import mybir

ALU = mybir.AluOpType
ACT = mybir.ActivationFunctionType
AX = mybir.AxisListType.X
F32 = mybir.dt.float32
BF16 = mybir.dt.bfloat16
U32 = mybir.dt.uint32
I32 = mybir.dt.int32
U8 = mybir.dt.uint8

P = 128
EPS = 1e-5
PARTS_Q = (0, 0, 0, 1, 1, 2)
PARTS_K = (0, 1, 2, 0, 1, 0)
SROWS = 16 * len(PARTS_Q)
NPART = 3
VW = 32
LOOP_FIRST = 2


class Batch:

    def __init__(self, c, reg=None):
        self.c, self.reg = c, reg

    def __add__(self, d):
        return Batch(self.c + d, self.reg)

    def before(self, per=1, k=0):
        return self.c * per + k if self.reg is None else self.reg * (2 * per) + (self.c * per + k)

    def landed(self, per=16):
        rounds = self.c // 2 + 1
        return rounds * per if self.reg is None else self.reg * per + rounds * per

    @property
    def par(self):
        return self.c % 2


def need(eng, sem, value):
    if isinstance(value, int) and value <= 0:
        return
    eng.wait_ge(sem, value)


def need_alone(eng, passed, sem, value):
    if isinstance(value, int) and value <= 0:
        return
    eng.wait_ge(sem, value)
    if not isinstance(value, int):
        eng.sem_inc(passed, 1)


def turns(eng, nb, step, ahead=2):
    last_full = nb - 1 - ahead
    trips = (last_full - LOOP_FIRST + 1) // 2
    for i in range(-2, LOOP_FIRST):
        step(Batch(i), nb)
    with eng.Fori(0, trips) as j:
        for c in range(2):
            step(Batch(LOOP_FIRST + c, j), nb)
    for i in range(LOOP_FIRST + 2 * trips, nb + 2):
        step(Batch(i), nb)


def pool_turns(eng, nb, step):
    last_full = nb - 3
    trips = (last_full - LOOP_FIRST + 1) // 2
    for i in range(-2, LOOP_FIRST):
        step(Batch(i), nb, i % 4)
    with eng.Fori(0, trips // 2) as j:
        for c in range(4):
            step(Batch4(LOOP_FIRST + c, j), nb, (LOOP_FIRST + c) % 4)
    first = LOOP_FIRST + 4 * (trips // 2)
    for i in range(first, nb + 2):
        step(Batch(i), nb, i % 4)


class Batch4(Batch):

    def __add__(self, d):
        return Batch4(self.c + d, self.reg)

    def before(self, per=1, k=0):
        return self.reg * (4 * per) + (self.c * per + k)

    def landed(self, per=16):
        return self.reg * (2 * per) + (self.c // 2 + 1) * per


def has(n, nb):
    return n.reg is not None or 0 <= n.c < nb


def tower_program(nc, x, wkv, wq, bkv, bq_tok, w_bias_t, mask_t, out_w, out_b, ln_g, ln_b,
                  wq_t, bq, wk_t, bk, wv_t, bv, wo_t, bo, beta, t_par, ln_w, ln_b2,
                  wg, w_gate, w_down, out):
    nb, cin, ltok, hm = 64, 64, 256, 4
    nb = x.shape[0]
    dm = 256
    nh, dh = 16, 16
    ne, ff = wg.shape[1], w_gate.shape[2]
    tokens = nb * ltok
    cap = 2 * tokens // ne
    tiles = tokens // P
    SC = 1.0 / dh ** 0.5

    h2_dram = nc.dram_tensor("h2_dram", (tokens, dm), F32, kind="Internal").ap()
    x2_dram = nc.dram_tensor("x2_dram", (tokens, dm), F32, kind="Internal").ap()
    eo_dram = nc.dram_tensor("eo_dram", (ne * cap, dm), F32, kind="Internal").ap()
    qk_dram = [nc.dram_tensor(f"qk_dram{b}", (NPART, 4, P, ltok), BF16, kind="Internal").ap() for b in range(2)]
    slot_dram = [nc.dram_tensor(f"slot_dram{c}", (ne * 2 * cap, 1), U32, kind="Internal").ap() for c in range(2)]

    outer = ExitStack()
    with outer:
        def keep(name, shape, dt=F32):
            return outer.enter_context(nc.sbuf_tensor(name, shape, dt))

        logits_all = keep("logits_all", [P, tiles, ne])
        top_all = keep("top_all", [P, tiles, 2])
        expert_all = keep("expert_all", [P, tiles, 2])
        place_all = keep("place_all", [P, tiles, 2])
        filled = keep("filled", [P, 2, 2, ne])
        iota_e = keep("iota_e", [P, ne])
        ident = keep("ident", [P, P])

        tower(nc, locals())
        routes = keep("routes", [P, 2, tiles], U32)
        gates = keep("gates", [P, 2, tiles])
        slot_tok = keep("slot_tok", [P, ne, cap // P], U32)
        finish_routes(nc, locals())
        experts(nc, locals())
        combine(nc, locals())


def tower(nc, g):
    x, out_w, wg = g["x"], g["out_w"], g["wg"]
    nb, ltok, dm, nh, dh, ne, cap, tiles, SC = (g[k] for k in "nb ltok dm nh dh ne cap tiles SC".split())
    qk_dram, slot_dram = g["qk_dram"], g["slot_dram"]
    ident, iota_e, filled = g["ident"], g["iota_e"], g["filled"]
    logits_all, top_all, expert_all, place_all = (g[k] for k in ("logits_all", "top_all", "expert_all", "place_all"))
    h2_dram = g["h2_dram"].rearrange("(n lt p) d -> n p lt d", p=P, lt=2)
    x2_dram = g["x2_dram"].rearrange("(n lt p) d -> n p lt d", p=P, lt=2)

    ctx = ExitStack()
    with ctx:
        def sb(name, shape, dt=F32):
            return ctx.enter_context(nc.sbuf_tensor(name, shape, dt))

        def bank(name, shape, dt=F32):
            return ctx.enter_context(nc.psum_tensor(name, shape, dt))

        def sem(name):
            return ctx.enter_context(nc.semaphore(name))

        wkv_sb = sb("wkv_sb", [65, 2, 64])
        wq_sb = sb("wq_sb", [65, 64])
        xid = sb("xid", [65, 4, 64])
        ew_t = sb("ew_t", [P, 2, 256])
        mask_sb = sb("mask_sb", [P, 2, 256], U8)
        outw_sb = sb("outw_sb", [P, 2, 256])
        wqa = sb("wqa", [P, 2, 256])
        wka = sb("wka", [P, 2, 256])
        wva = sb("wva", [P, 2, 256])
        woa = sb("woa", [P, 2, 256])
        wg_sb = sb("wg_sb", [P, 2, ne])
        rows = {k: sb(f"row_{k}", [P, 256]) for k in ("ln_g", "ln_b", "bv", "bo", "ln_w", "ln_b2")}
        bqk = sb("bqk", [P, 4])
        beta_sb = sb("beta_sb", [P, nh])
        t_sb = sb("t_sb", [P, nh])
        b8 = sb("b8", [P, nh])
        c16 = sb("c16", [P, nh])
        eps = sb("eps", [P, 1])
        identb = sb("identb", [P, P], BF16)
        before_b = sb("before_b", [P, P], BF16)
        ones_b = sb("ones_b", [P, P], BF16)
        tok_ids = sb("tok_ids", [P, tiles], I32)
        iota_i = sb("iota_i", [P, ne], I32)
        zero_i = sb("zero_i", [P, 2 * ne * cap // P], U32)

        xb = [sb(f"xb{b}", [65, ltok * 4]) for b in range(2)]
        ek = sb("ek", [P, 2, 256])
        ekv = sb("ekv", [P, 2, 256])
        eq = sb("eq", [P, 2, 256])
        dn = sb("dn", [P, 2, 256])
        rec = sb("rec", [P, 2, 256])
        y_t = sb("y_t", [P, 2, 256])
        hn = sb("hn", [P, 2, 256])
        hg = sb("hg", [P, 2, 256])
        h1 = sb("h1", [P, 2, 256])
        x1 = sb("x1", [P, 2, 256])
        hx0 = sb("hx0", [P, 2, 256])
        hx = [sb(f"hxr{b}", [P, 2, 256]) for b in range(4)]
        x1_t = sb("x1_t", [P, 2, 256])
        stat = [sb(f"stat{k}", [P, 2, 6]) for k in range(4)]
        mv = [sb(f"mv{k}", [P, 2, 2]) for k in range(4)]
        lnv = [sb(f"lnv{k}", [P, 2]) for k in range(4)]
        rs = [sb(f"rs{k}", [P, 2]) for k in range(4)]
        qkf = sb("qkf", [P, 4, 256])
        qkr = sb("qkr", [P, 4, 256])
        qkp = sb("qkp", [P, NPART, 4, 256], BF16)
        q_stack = [sb(f"q_stack{b}", [P, nh, ltok], BF16) for b in range(2)]
        k_stack = [sb(f"k_stack{b}", [P, nh, ltok], BF16) for b in range(2)]
        v_sb = [sb(f"v_sb{b}", [P, 2, nh, VW]) for b in range(2)]
        rmax = sb("rmax", [P, nh, 2])
        nmx = sb("nmx", [P, nh, 2])
        nmr = sb("nmr", [P, nh, 2])
        mparts = sb("mparts", [P, 2, NPART, nh], BF16)
        mrow = sb("mrow", [NPART * nh, ltok], BF16)
        z_sb = [sb(f"z_sb{b}", [P, 2, 512]) for b in range(2)]
        u_sb = [sb(f"u_sb{b}", [P, 2, 512]) for b in range(2)]
        zb = sb("zb", [P, 512])
        p_sb = [sb(f"p_sb{b}", [P, 4, 2, 256]) for b in range(2)]
        g_sb = [sb(f"g_sb{b}", [P, 4, 2, 256]) for b in range(2)]
        f_sb = sb("f_sb", [P, 512])
        rc = sb("rc", [P, 16])
        ntv = sb("ntv", [P, 2, 2, 4, 16])
        f_n = sb("f_n", [P, 2, 256])
        f_t = sb("f_t", [P, 2, 256])
        yb = sb("yb", [P, 2, 256])
        yn = sb("yn", [P, 2, 256])
        yw = sb("yw", [P, 2, 256])
        h2 = [sb(f"h2_{b}", [P, 2, 256]) for b in range(2)]
        x2 = [sb(f"x2_{b}", [P, 2, 256]) for b in range(2)]
        x2_t = sb("x2_t", [P, 2, 256])
        lgt = sb("lgt", [P, 2, ne])
        top8 = sb("top8", [P, 2, 8])
        idx8 = sb("idx8", [P, 2, 8], U32)
        idxf = sb("idxf", [P, 2, 2])
        hot = sb("hot", [P, 2, 2, ne], BF16)
        locb = sb("locb", [P, 2, 2, ne])
        lsel = sb("lsel", [P, 2, 2, ne])
        loc = sb("loc", [P, 2, 2])
        over = sb("over", [P, 2, 2])
        flat = sb("flat", [P, 2, 2])
        flat2 = sb("flat2", [P, 2, 2])
        slot_u = [sb(f"slot_u{b}", [P, 4], U32) for b in range(2)]
        tok_u = [sb(f"tok_u{b}", [P, 2], U32) for b in range(2)]

        raw_ps = bank("raw_ps", [P, 2, 2, 256])
        sh_ps = bank("sh_ps", [P, 2, 2, 256])
        pv_ps = bank("pv_ps", [P, 512])
        a_ps = bank("a_ps", [P, 512])
        b_ps = bank("b_ps", [P, 512])
        t_ps = bank("t_ps", [P, 512])
        b_bf = b_ps[:, :].bitcast(BF16)

        s_w = sem("s_w")
        s_c0 = sem("s_c0")
        s_c1 = sem("s_c1")
        s_d = sem("s_d")
        s_z = sem("s_z")
        s_zd = sem("s_zd")
        s_i = sem("s_i")
        with nc.Block() as block:
            @block.sync
            def _(sp):
                loads = [
                    (wkv_sb[0:64, :, :], g["wkv"].rearrange("k c d -> c k d")), (wkv_sb[64:65, :, :], g["bkv"].rearrange("k (a d) -> a k d", a=1)),
                    (wq_sb[0:64, :], g["wq"]), (wq_sb[64:65, :], g["bq_tok"].rearrange("(a d) -> a d", a=1)),
                    (xid[64:65, :, :], g["out_b"].rearrange("(a h c) -> a h c", a=1, c=64)),
                    (ew_t[:, :, :], g["w_bias_t"].rearrange("(s p) t -> p s t", p=P)),
                    (mask_sb[:, :, :], g["mask_t"].rearrange("(s p) t -> p s t", p=P)),
                    (wg_sb[:, :, :], wg.rearrange("(k p) e -> p k e", p=P)),
                    (bqk[:, 0:2], g["bq"].rearrange("(m p) -> p m", p=P)),
                    (bqk[:, 2:4], g["bk"].rearrange("(m p) -> p m", p=P)),
                    (beta_sb[:, :], g["beta"].partition_broadcast(P)),
                    (t_sb[:, :], g["t_par"].partition_broadcast(P)),
                ]
                loads += [(w[:, :, :], d.rearrange("(k p) n -> p k n", p=P)) for w, d in
                          ((outw_sb, out_w), (wqa, g["wq_t"]), (wka, g["wk_t"]), (wva, g["wv_t"]), (woa, g["wo_t"]))]
                loads += [(r[:, :], g[k].partition_broadcast(P)) for k, r in rows.items()]
                for dst, src in loads:
                    sp.dma_start(dst, src, allow_slow_non_contiguous=True).then_inc(s_w, 16)
                sp.wait_ge(s_w, 16 * len(loads))
                sp.wait_ge(s_z, 1)
                for c in range(2):
                    sp.dma_start(slot_dram[c].rearrange("(p m) o -> p (m o)", p=P), zero_i[:, :]).then_inc(s_zd, 16)
                sp.wait_ge(s_zd, 32)

            @block.gpsimd
            def _(pool):
                pool.memset(ident[:, :], 0.0).then_inc(s_c0, 1)
                pool.memset(before_b[:, :], 1.0).then_inc(s_c0, 1)
                pool.iota(iota_i[:, :], pattern=[[1, ne]], base=0, channel_multiplier=0).then_inc(s_c0, 1)
                pool.iota(tok_ids[:, :], pattern=[[P, tiles]], base=0, channel_multiplier=1).then_inc(s_c0, 1)
                pool.wait_ge(s_c0, 4)
                pool.affine_select(out=ident[:, :], in_=ident[:, :], compare_op=ALU.not_equal, fill=1.0,
                                   base=0, pattern=[[-1, P]], channel_multiplier=1).then_inc(s_c1, 1)
                pool.affine_select(out=before_b[:, :], in_=before_b[:, :], compare_op=ALU.is_ge, fill=0.0,
                                   base=-1, pattern=[[1, P]], channel_multiplier=-1).then_inc(s_c1, 1)

            @block.vector
            def _(dve):
                fills = [(zero_i[:, :], 0), (ones_b[:, :], 1.0), (eps[:, :], EPS), (filled[:, :, :, :], 0.0)]
                fills += [(v[:, :, :, :], 0.0) for v in v_sb]
                for b in range(2):
                    fills += [(xb[b][64:65, :], 1.0), (k_stack[b][96:128, :, :], 1.0), (q_stack[b][96:128, :, :], 0.0)]
                for n, (dst, value) in enumerate(fills):
                    dve.memset(dst, value).then_inc(s_z if n == 0 else s_i, 1)
                done = len(fills) - 1
                dve.wait_ge(s_i, done)
                for v in v_sb:
                    dve.memset(v[:, :, :, 16:17], 2.0).then_inc(s_d, 1)
                dve.wait_ge(s_c1, 2)
                dve.tensor_copy(identb[:, :], ident[:, :]).then_inc(s_d, 1)
                for h in range(4):
                    dve.tensor_copy(xid[0:64, h, :], ident[0:64, 0:64]).then_inc(s_d, 1)
                dve.tensor_copy(iota_e[:, :], iota_i[:, :]).then_inc(s_d, 1)
                dve.wait_ge(s_w, 16 * (12 + 5 + len(rows)))
                dve.tensor_tensor(ew_t[:, :, :], ew_t[:, :, :], mask_sb[:, :, :], ALU.mult).then_inc(s_d, 1)
                dve.tensor_scalar(b8[:, :], beta_sb[:, :], 8.0, None, ALU.mult).then_inc(s_d, 1)
                dve.tensor_tensor(c16[:, :], t_sb[:, :], t_sb[:, :], ALU.mult).then_inc(s_d, 1)
                dve.wait_ge(s_d, 11)
                dve.tensor_scalar(c16[:, :], c16[:, :], 1.0, 16.0, ALU.add, ALU.mult).then_inc(s_d, 1)
                dve.wait_ge(s_d, 12)
                dve.tensor_tensor(c16[:, :], c16[:, :], beta_sb[:, :], ALU.mult).then_inc(s_d, 1)
                dve.wait_ge(s_d, 13)
                dve.tensor_tensor(c16[:, :], c16[:, :], beta_sb[:, :], ALU.mult).then_inc(s_d, 1)

            @block.scalar
            def _(act):
                nc.scalar.preload_act_table_set("natural_log_exp_and_others")
                act.wait_ge(s_d, 14)
                act.activation(ew_t[:, :, :], ew_t[:, :, :], ACT.Exp).then_inc(s_c1, 1)

        names = """kv_full ek_ready ekv_ready q_full eq_ready den_full dn_ready rec_ready num_full yt_ready
            mix_full st0 ag0 lv0 rs0 hn_ready hg_ready h1_ready st1 ag1 lv1 rs1 x1_ready hx0_ready hx_ready
            x1t_full x1t_ready qk_full qk_copied part_h part_r part_m part_l v_full v_ready
            mx_full mx_ready nm_neg nm_h nm_r nm_m nm_r2 mparts_ready mt_full mt_ready
            raw_full z_ready u_dve zb_ready u_pool l_ready g_ready sh_full p_ready
            pv_full f_ready tr_full rc_ready nt_ready fn_ready
            ft_full ft_ready y_full yb_ready st2 ag2 lv2 rs2 yn_ready yw_ready h2_ready st3 ag3 lv3 rs3 x2_ready
            x2t_full x2t_ready lg_full lg_copied lg_kept top_ready idx_ready idxf_ready hot_ready kept
            lc_full locb_ready fill_ready lsel_ready loc_ready over_ready flat_ready flat2_ready slot_ready""".split()
        s = {k: sem(k) for k in names}
        passed = {k: sem(f"passed_{k}") for k in ("sp", "pe", "dve", "pool")}
        x_in = [sem(f"x_in{b}") for b in range(2)]
        qk_out = [sem(f"qk_out{b}") for b in range(2)]
        stack_in = [sem(f"stack_in{b}") for b in range(2)]
        maxrow_in = [sem(f"maxrow_in{b}") for b in range(2)]
        h2_out = [sem(f"h2_out{b}") for b in range(2)]
        x2_out = [sem(f"x2_out{b}") for b in range(2)]
        scat_out = [sem(f"scat_out{b}") for b in range(2)]

        def dyn(n, mul=1):
            return bass.ds(n.before(mul), mul)

        with nc.Block() as block:
            @block.sync
            def _(sp):
                def load_x(n):
                    b = n.par
                    need_alone(sp, passed["sp"], s["mix_full"], n.before(1, -1))
                    sp.dma_start(xb[b][0:64, :], x[dyn(n)].rearrange("a c m -> (a c) m")).then_inc(x_in[b], 16)

                def store_qk(n):
                    need_alone(sp, passed["sp"], s["part_l"], n.before(1, 1))
                    need_alone(sp, passed["sp"], stack_in[n.par], (n + -2).landed(16 * 2 * len(PARTS_Q)) if has(n + -2, nb) else 0)
                    sp.dma_start(qk_dram[n.par].rearrange("a m p n -> p a m n"), qkp[:, :, :, :]).then_inc(qk_out[n.par], 16)

                def load_stacks(n):
                    b = n.par
                    need_alone(sp, passed["sp"], qk_out[b], n.landed())
                    need_alone(sp, passed["sp"], s["sh_full"], (n + -1).before(8))
                    for c, (stack, parts) in enumerate(((q_stack[b], PARTS_Q), (k_stack[b], PARTS_K))):
                        for blk, part in enumerate(parts):
                            sp.dma_start(stack[dh * blk:dh * blk + dh, :, :].rearrange("r (m h) n -> r m h n", m=2),
                                         qk_dram[b][part, 2 * c:2 * c + 2].rearrange("m (h r) n -> r m h n", r=dh))\
                                .then_inc(stack_in[b], 16)

                def load_maxrow(n):
                    need_alone(sp, passed["sp"], s["mt_ready"], n.before(1, 1))
                    for part in range(NPART):
                        sp.dma_start(q_stack[n.par][SROWS + part:SROWS + part + 1, :, :],
                                     mrow[part * nh:part * nh + nh, :]).then_inc(maxrow_in[n.par], 16)

                def store_rows(n):
                    b = n.par
                    need_alone(sp, passed["sp"], s["h2_ready"], n.before(1, 1))
                    sp.dma_start(h2_dram[dyn(n)].rearrange("a p l d -> (a p) l d"), h2[b][:, :, :]).then_inc(h2_out[b], 16)
                    need_alone(sp, passed["sp"], s["x2_ready"], n.before(2, 2))
                    sp.dma_start(x2_dram[dyn(n)].rearrange("a p l d -> (a p) l d"), x2[b][:, :, :]).then_inc(x2_out[b], 16)

                def step(i, nb):
                    if has(i + 1, nb):
                        store_qk(i + 1)
                        load_stacks(i + 1)
                    if has(i + 3, nb) and i.c + 3 >= 2:
                        load_x(i + 3)
                    if has(i + -1, nb):
                        store_rows(i + -1)
                    if has(i + 1, nb):
                        load_maxrow(i + 1)

                load_x(Batch(0))
                turns(sp, nb, lambda i, nb: (load_x(Batch(1)) if i.reg is None and i.c == -2 else None, step(i, nb)), ahead=3)
                for sems in (h2_out, x2_out):
                    for b in range(2):
                        sp.wait_ge(sems[b], 16 * (nb // 2))

            @block.tensor
            def _(pe):
                def kv(n, lt):
                    if lt == 0:
                        pe.wait_ge(x_in[n.par], n.landed())
                        need(pe, s["x1t_ready"], n.before(1))
                    else:
                        need(pe, s["ekv_ready"], n.before(2, 1))
                    xv = xb[n.par][:, :].rearrange("c (l h) -> c l h", h=4)
                    for h in range(4):
                        mm = pe.matmul(a_ps[:, h * P:(h + 1) * P], xv[:, lt * P:lt * P + P, h],
                                       wkv_sb[:, :, :].rearrange("c k d -> c (k d)"), start=True, stop=True)
                    mm.then_inc(s["kv_full"], 1)

                def q_tok(n):
                    need(pe, s["ekv_ready"], n.before(2, 2))
                    xv = xb[n.par][:, :].rearrange("c (l h) -> c l h", h=4)
                    for h in range(4):
                        mm = pe.matmul(a_ps[64 * (h % 2):64 * (h % 2) + 64, (h // 2) * 256:(h // 2) * 256 + 256],
                                       wq_sb[:, :], xv[:, :, h], start=True, stop=True)
                    mm.then_inc(s["q_full"], 1)

                def mixed(n, src, ready, bank_free, full):
                    need(pe, s[ready[0]], n.before(*ready[1:]))
                    need(pe, s[bank_free], n.before(1, 1))
                    for m in range(2):
                        for st in range(2):
                            mm = pe.matmul(a_ps[:, m * 256:m * 256 + 256], src[:, st, m * P:m * P + P], ew_t[:, st, :],
                                           start=(st == 0), stop=(st == 1))
                    mm.then_inc(s[full], 1)

                def mix_out(n):
                    need(pe, s["yt_ready"], n.before(1, 1))
                    xv = xb[n.par][:, :].rearrange("c (l h) -> c l h", h=4)
                    for lt in range(2):
                        for h in range(4):
                            pe.matmul(a_ps[:, lt * 256 + h * 64:lt * 256 + h * 64 + 64], xv[:, lt * P:lt * P + P, h],
                                      xid[:, h, :], start=(h == 0), stop=False)
                        for m in range(2):
                            mm = pe.matmul(a_ps[:, lt * 256:lt * 256 + 256], y_t[:, m, lt * P:lt * P + P], outw_sb[:, m, :],
                                           start=False, stop=(m == 1))
                    mm.then_inc(s["mix_full"], 1)

                def transposed(n, src, ps, full):
                    for dk in range(2):
                        for lt in range(2):
                            mm = pe.transpose(ps[:, dk * 256 + lt * P:dk * 256 + lt * P + P], src[:, lt, dk * P:dk * P + P],
                                              ident[:, :])
                    mm.then_inc(s[full], 1)

                def x1_transposed(n):
                    need(pe, s["x1_ready"], n.before(2, 2))
                    transposed(n, x1, a_ps, "x1t_full")

                def project(n, c):
                    if c == 0:
                        need(pe, s["x1t_ready"], n.before(1, 1))
                        need(pe, s["mt_ready"], n.before(1))
                    else:
                        need(pe, s["qk_copied"], n.before(4, 2))
                    w = (wqa, wka)[c]
                    for m in range(2):
                        for dk in range(2):
                            mm = pe.matmul(b_ps[:, m * 256:m * 256 + 256], w[:, dk, m * P:m * P + P], x1_t[:, dk, :],
                                           start=(dk == 0), stop=(dk == 1))
                    mm.then_inc(s["qk_full"], 1)

                def project_v(n):
                    need(pe, s["qk_copied"], n.before(4, 4))
                    for lt in range(2):
                        for dk in range(2):
                            mm = pe.matmul(b_ps[:, lt * 256:lt * 256 + 256], x1_t[:, dk, lt * P:lt * P + P], wva[:, dk, :],
                                           start=(dk == 0), stop=(dk == 1))
                    mm.then_inc(s["v_full"], 1)

                def max_scores(n, h):
                    b = n.par
                    if h == 0:
                        pe.wait_ge(stack_in[b], n.landed(16 * 2 * len(PARTS_Q)))
                        need(pe, s["v_ready"], n.before(1, 1))
                    else:
                        need(pe, s["mx_ready"], n.before(nh, h))
                    for lt in range(2):
                        mm = pe.matmul(b_ps[:, lt * 256:lt * 256 + 256], q_stack[b][0:SROWS, h, lt * P:lt * P + P],
                                       k_stack[b][0:SROWS, h, :], start=True, stop=True)
                    mm.then_inc(s["mx_full"], 1)

                def max_transposed(n):
                    need_alone(pe, passed["pe"], s["mparts_ready"], n.before(1, 1))
                    for lt in range(2):
                        mm = pe.transpose(b_bf[0:NPART * nh, lt * P:lt * P + P],
                                          mparts[:, lt, :, :].rearrange("p a h -> p (a h)"), identb[:, :])
                    mm.then_inc(s["mt_full"], 1)

                def scores(n, pair, ps, nrows, bank_sem, full):
                    b = n.par
                    need(pe, s[bank_sem], n.before(8, pair))
                    if nrows > SROWS and pair == 0:
                        pe.wait_ge(maxrow_in[b], n.landed(16 * NPART))
                    if nrows == SROWS and pair == 0:
                        pe.wait_ge(stack_in[b], n.landed(16 * 2 * len(PARTS_Q)))
                    for j in range(2):
                        for mt in range(2):
                            mm = pe.matmul(ps[:, j, mt, :], k_stack[b][0:nrows, 2 * pair + j, mt * P:mt * P + P],
                                           q_stack[b][0:nrows, 2 * pair + j, :], start=True, stop=True)
                    mm.then_inc(s[full], 1)

                def weighted(n, t):
                    need(pe, s["g_ready"], n.before(8, 2 * t + 2))
                    need(pe, s["p_ready"], n.before(8, 2 * t + 2))
                    need(pe, s["v_ready"], n.before(1, 1))
                    need(pe, s["nt_ready"], n.before(4, t))
                    for kind, w in enumerate((p_sb[t % 2], g_sb[t % 2])):
                        for mt in range(2):
                            for q in range(4):
                                mm = pe.matmul(pv_ps[32 * q:32 * q + 32, kind * 256:kind * 256 + 256],
                                               v_sb[n.par][:, mt, 4 * t + q, :], w[:, q, mt, :],
                                               start=(mt == 0), stop=(mt == 1))
                    mm.then_inc(s["pv_full"], 1)

                def weighted_transposed(n, t):
                    need(pe, s["f_ready"], n.before(4, t + 1))
                    for lt in range(2):
                        for kind in range(2):
                            mm = pe.transpose(pv_ps[:, (lt * 2 + kind) * P:(lt * 2 + kind) * P + P],
                                              f_sb[:, kind * 256 + lt * P:kind * 256 + lt * P + P], ident[:, :])
                    mm.then_inc(s["tr_full"], 1)

                def f_transposed(n):
                    need(pe, s["fn_ready"], n.before(4, 4))
                    need(pe, s["locb_ready"], n.before(1))
                    need(pe, s["fill_ready"], n.before(1))
                    transposed(n, f_n, t_ps, "ft_full")

                def y_proj(n):
                    need(pe, s["ft_ready"], n.before(1, 1))
                    for lt in range(2):
                        for dk in range(2):
                            mm = pe.matmul(t_ps[:, lt * 256:lt * 256 + 256], f_t[:, dk, lt * P:lt * P + P], woa[:, dk, :],
                                           start=(dk == 0), stop=(dk == 1))
                    mm.then_inc(s["y_full"], 1)

                def x2_transposed(n):
                    need(pe, s["x2_ready"], n.before(2, 2))
                    transposed(n, x2[n.par], t_ps, "x2t_full")

                def logits(n):
                    need(pe, s["x2t_ready"], n.before(1, 1))
                    for lt in range(2):
                        for dk in range(2):
                            mm = pe.matmul(t_ps[:, lt * ne:lt * ne + ne], x2_t[:, dk, lt * P:lt * P + P], wg_sb[:, dk, :],
                                           start=(dk == 0), stop=(dk == 1))
                    mm.then_inc(s["lg_full"], 1)

                def positions(n):
                    need(pe, s["hot_ready"], n.before(1, 1))
                    c = 2 * ne
                    h0 = hot[:, 0, :, :].rearrange("p c e -> p (c e)")
                    h1_ = hot[:, 1, :, :].rearrange("p c e -> p (c e)")
                    pe.matmul(t_ps[:, 0:c], before_b[:, :], h0, start=True, stop=True)
                    pe.matmul(t_ps[:, c:2 * c], before_b[:, :], h1_, start=True, stop=False)
                    pe.matmul(t_ps[:, c:2 * c], ones_b[:, :], h0, start=False, stop=True)
                    pe.matmul(t_ps[:, 2 * c:3 * c], ones_b[:, :], h0, start=True, stop=False)
                    pe.matmul(t_ps[:, 2 * c:3 * c], ones_b[:, :], h1_, start=False, stop=True).then_inc(s["lc_full"], 1)

                def step(i, nb):
                    A, B, M, C, D = (has(i + d, nb) for d in (2, 1, 0, -1, -2))
                    for st in range(8):
                        if M:
                            scores(i, st, raw_ps, SROWS, "z_ready", "raw_full")
                        if st == 0:
                            if C:
                                weighted_transposed(i + -1, 2)
                            if B:
                                project(i + 1, 0)
                            if A:
                                kv(i + 2, 0)
                        if M:
                            scores(i, st, sh_ps, SROWS + NPART, "p_ready", "sh_full")
                        if st == 1:
                            if B:
                                project(i + 1, 1)
                            if A:
                                kv(i + 2, 1)
                            if C:
                                weighted(i + -1, 3)
                            if A:
                                q_tok(i + 2)
                            if D:
                                positions(i + -2)
                        if st == 2:
                            if B:
                                project_v(i + 1)
                            if C:
                                weighted_transposed(i + -1, 3)
                            if A:
                                mixed(i + 2, ek, ("ek_ready", 2, 2), "eq_ready", "den_full")
                        if st == 3:
                            if C:
                                f_transposed(i + -1)
                            if A:
                                mixed(i + 2, ekv, ("ekv_ready", 2, 2), "dn_ready", "num_full")
                            if M:
                                weighted(i, 0)
                            if C:
                                y_proj(i + -1)
                        if B and st >= 4:
                            for h in range(4 * (st - 4), 4 * (st - 4) + 2):
                                max_scores(i + 1, h)
                        if st == 4:
                            if M:
                                weighted_transposed(i, 0)
                            if A:
                                mix_out(i + 2)
                        if st == 5 and M:
                            weighted(i, 1)
                        if st == 6 and M:
                            weighted_transposed(i, 1)
                        if st == 7:
                            if C:
                                x2_transposed(i + -1)
                            if M:
                                weighted(i, 2)
                        if B and st >= 4:
                            for h in range(4 * (st - 4) + 2, 4 * (st - 4) + 4):
                                max_scores(i + 1, h)
                        if st == 7:
                            if A:
                                x1_transposed(i + 2)
                            if C:
                                logits(i + -1)
                            if B:
                                max_transposed(i + 1)

                turns(pe, nb, step)

            @block.scalar
            def _(act):
                def ek_tile(n, lt):
                    need(act, s["kv_full"], n.before(2, lt + 1))
                    if lt == 0:
                        need(act, s["den_full"], n.before(1))
                    kvv = a_ps[:, :].rearrange("p (h k d) -> p h k d", h=4, k=2)
                    act.activation(ek[:, lt, :].rearrange("p (h d) -> p h d", h=4), kvv[:, :, 0, :], ACT.Exp)\
                        .then_inc(s["ek_ready"], 1)

                def exp_minus_q(n):
                    need(act, s["q_full"], n.before(1, 1))
                    need(act, s["dn_ready"], n.before(1))
                    act.activation(eq[:, :, :].rearrange("p m t -> p (m t)"), a_ps[:, :], ACT.Exp, scale=-1.0)\
                        .then_inc(s["eq_ready"], 1)

                def rsqrt(n, k, used, per):
                    need(act, s[f"ag{k}"], n.before(2, 2))
                    act.activation(lnv[k][:, :], mv[k][:, :, 1], ACT.Ln, bias=eps[:, 0:1]).then_inc(s[f"lv{k}"], 1)
                    need(act, s[f"lv{k}"], n.before(1, 1))
                    need(act, s[used], n.before(per))
                    act.activation(rs[k][:, :], lnv[k][:, :], ACT.Exp, scale=-0.5).then_inc(s[f"rs{k}"], 1)

                def copy_out(n, ps, dst, full, ready, used):
                    need(act, s[full], n.before(1, 1))
                    for sem_name, per in used:
                        need(act, s[sem_name], n.before(per))
                    act.activation(dst[:, :, :].rearrange("p a n -> p (a n)"), ps[:, :], ACT.Copy).then_inc(s[ready], 1)

                def qk_bias(n, c):
                    need(act, s["qk_full"], n.before(2, c + 1))
                    if c == 0:
                        need(act, s["part_h"], n.before(1))
                        need(act, s["part_r"], n.before(1))
                    for m in range(2):
                        act.activation(qkf[:, 2 * c + m, :], b_ps[:, m * 256:m * 256 + 256], ACT.Identity,
                                       bias=bqk[:, 2 * c + m:2 * c + m + 1]).then_inc(s["qk_copied"], 1)

                def maxrow_copy(n):
                    need(act, s["mt_full"], n.before(1, 1))
                    if has(n + -1, nb):
                        act.wait_ge(maxrow_in[(n.par + 1) % 2], (n + -1).landed(16 * NPART))
                    act.activation(mrow[:, :], b_bf[0:NPART * nh, 0:ltok], ACT.Copy).then_inc(s["mt_ready"], 1)

                def softmax_weights(n, pair):
                    need(act, s["sh_full"], n.before(8, pair + 1))
                    if pair % 2 == 0:
                        need(act, s["pv_full"], n.before(4, pair // 2 - 1))
                    dst = p_sb[(pair // 2) % 2][:, 2 * (pair % 2):2 * (pair % 2) + 2, :, :]
                    act.activation(dst.rearrange("p j m n -> p (j m n)"), sh_ps[:, :, :, :].rearrange("p j m n -> p (j m n)"),
                                   ACT.Exp, scale=SC).then_inc(s["p_ready"], 1)

                def cauchy_weights(n, pair):
                    b = pair % 2
                    for j, ready in enumerate(("u_dve", "u_pool")):
                        need(act, s[ready], n.before(8, pair + 1))
                        h = 2 * pair + j
                        act.activation(u_sb[b][:, j, :], u_sb[b][:, j, :], ACT.Ln, bias=c16[:, h:h + 1])\
                            .then_inc(s["l_ready"], 1)
                    need(act, s["l_ready"], n.before(16, 2 * pair + 2))
                    if pair % 2 == 0:
                        need(act, s["pv_full"], n.before(4, pair // 2 - 1))
                    dst = g_sb[(pair // 2) % 2][:, 2 * (pair % 2):2 * (pair % 2) + 2, :, :]
                    act.activation(dst.rearrange("p j m n -> p (j m n)"), u_sb[b][:, :, :].rearrange("p j n -> p (j n)"),
                                   ACT.Exp, scale=-1.0).then_inc(s["g_ready"], 1)

                def weighted_copy(n, t):
                    need(act, s["pv_full"], n.before(4, t + 1))
                    need(act, s["tr_full"], n.before(4, t))
                    act.activation(f_sb[:, :], pv_ps[:, :], ACT.Copy).then_inc(s["f_ready"], 1)

                def step(i, nb):
                    A, B, M, C = (has(i + d, nb) for d in (2, 1, 0, -1))
                    for st in range(8):
                        if st == 0 and C:
                            cauchy_weights(i + -1, 7)
                        if st == 0:
                            if B:
                                qk_bias(i + 1, 0)
                            if A:
                                ek_tile(i + 2, 0)
                        if M:
                            softmax_weights(i, st)
                        if st >= 1 and M:
                            cauchy_weights(i, st - 1)
                        if st == 1:
                            if B:
                                qk_bias(i + 1, 1)
                            if A:
                                ek_tile(i + 2, 1)
                                exp_minus_q(i + 2)
                            if C:
                                weighted_copy(i + -1, 3)
                        if st == 3:
                            if C:
                                copy_out(i + -1, t_ps, f_t, "ft_full", "ft_ready", (("y_full", 1),))
                            if M:
                                weighted_copy(i, 0)
                        if st == 4:
                            if C:
                                rsqrt(i + -1, 2, "yn_ready", 2)
                        if st == 5:
                            if A:
                                rsqrt(i + 2, 0, "hn_ready", 2)
                            if M:
                                weighted_copy(i, 1)
                        if st == 6:
                            if C:
                                rsqrt(i + -1, 3, "x2_ready", 2)
                            if A:
                                rsqrt(i + 2, 1, "x1_ready", 2)
                        if st == 7:
                            if C:
                                copy_out(i + -1, t_ps, x2_t, "x2t_full", "x2t_ready", (("lg_full", 1),))
                            if M:
                                weighted_copy(i, 2)
                            if A:
                                copy_out(i + 2, a_ps, x1_t, "x1t_full", "x1t_ready", (("v_full", 1),))
                            if B:
                                maxrow_copy(i + 1)

                nc.scalar.preload_act_table_set("natural_log_exp_and_others")
                turns(act, nb, step)

            @block.vector
            def _(dve):
                def ekv_tile(n, lt):
                    need(dve, s["ek_ready"], n.before(2, lt + 1))
                    if lt == 0:
                        need(dve, s["num_full"], n.before(1))
                    kvv = a_ps[:, :].rearrange("p (h k d) -> p h k d", h=4, k=2)
                    dve.tensor_tensor(ekv[:, lt, :].rearrange("p (h d) -> p h d", h=4), kvv[:, :, 1, :],
                                      ek[:, lt, :].rearrange("p (h d) -> p h d", h=4), ALU.mult).then_inc(s["ekv_ready"], 1)

                def fold(t):
                    return t[:, :, :].rearrange("p a n -> p (a n)")

                def denominators(n):
                    need(dve, s["den_full"], n.before(1, 1))
                    dve.scalar_tensor_tensor(out=fold(dn), in0=fold(eq), scalar=1.0, in1=a_ps[:, :],
                                             op0=ALU.add, op1=ALU.mult).then_inc(s["dn_ready"], 1)
                    need(dve, s["dn_ready"], n.before(1, 1))
                    dve.reciprocal(fold(rec), fold(dn)).then_inc(s["rec_ready"], 1)

                def mixed_values(n):
                    need(dve, s["rec_ready"], n.before(1, 1))
                    need(dve, s["num_full"], n.before(1, 1))
                    need(dve, s["mix_full"], n.before(1))
                    dve.tensor_tensor(fold(y_t), a_ps[:, :], fold(rec), ALU.mult).then_inc(s["yt_ready"], 1)

                def stats(n, k, src, ready, per, incs):
                    need(dve, s[ready], n.before(per, incs))
                    for lt in range(2):
                        dve.bn_stats(stat[k][:, lt, :], src(lt)).then_inc(s[f"st{k}"], 1)
                    need(dve, s[f"lv{k}"], n.before(1))
                    for lt in range(2):
                        need_alone(dve, passed["dve"], s[f"st{k}"], n.before(2, lt + 1))
                        dve.bn_aggr(mv[k][:, lt, :], stat[k][:, lt, :]).then_inc(s[f"ag{k}"], 1)

                def normalise(n, k, src, dst, ready, used):
                    need(dve, s[f"rs{k}"], n.before(1, 1))
                    for f in used:
                        need(dve, s[f], n.before(1))
                    for lt in range(2):
                        dve.tensor_scalar(dst[:, lt, :], src(lt), mv[k][:, lt, 0:1], rs[k][:, lt:lt + 1],
                                          ALU.subtract, ALU.mult).then_inc(s[ready], 1)

                def a_half(lt):
                    return a_ps[:, lt * 256:lt * 256 + 256]

                def part_high(n):
                    need(dve, s["qk_copied"], n.before(4, 4))
                    if has(n + -1, nb):
                        dve.wait_ge(qk_out[(n.par + 1) % 2], (n + -1).landed())
                    dve.tensor_copy(qkp[:, 0, :, :], qkf[:, :, :]).then_inc(s["part_h"], 1)

                def part_mid(n):
                    need(dve, s["part_r"], n.before(1, 1))
                    dve.tensor_copy(qkp[:, 1, :, :], qkr[:, :, :]).then_inc(s["part_m"], 1)

                def v_bias(n):
                    need(dve, s["v_full"], n.before(1, 1))
                    need(dve, s["pv_full"], (n + -1).before(4))
                    for_v = rows["bv"][:, :].rearrange("p (a h d) -> p a h d", a=1, d=dh).broadcast_to((P, 2, nh, dh))
                    dve.tensor_tensor(v_sb[n.par][:, :, :, 0:dh], b_ps[:, :].rearrange("p (l h d) -> p l h d", l=2, d=dh),
                                      for_v, ALU.add).then_inc(s["v_ready"], 1)

                def head_max(n, h):
                    need(dve, s["mx_full"], n.before(nh, h + 1))
                    if h == 0:
                        need(dve, s["nm_neg"], n.before(1))
                    dve.tensor_reduce(rmax[:, h, :], b_ps[:, :].rearrange("p (l m) -> p l m", l=2), AX, ALU.max)\
                        .then_inc(s["mx_ready"], 1)

                def max_parts(n):
                    def part(k):
                        return mparts[:, :, k, :].rearrange("p l h -> p h l")
                    need(dve, s["mx_ready"], n.before(nh, nh))
                    need(dve, s["mparts_ready"], n.before(1))
                    dve.tensor_scalar(nmx[:, :, :], rmax[:, :, :], -1.0, None, ALU.mult).then_inc(s["nm_neg"], 1)
                    need(dve, s["nm_neg"], n.before(1, 1))
                    need(dve, s["mt_full"], n.before(1))
                    dve.tensor_copy(part(0), nmx[:, :, :]).then_inc(s["nm_h"], 1)
                    need(dve, s["nm_h"], n.before(1, 1))
                    dve.tensor_tensor(nmr[:, :, :], nmx[:, :, :], part(0), ALU.subtract).then_inc(s["nm_r"], 1)
                    need(dve, s["nm_r"], n.before(1, 1))
                    dve.tensor_copy(part(1), nmr[:, :, :]).then_inc(s["nm_m"], 1)
                    need(dve, s["nm_m"], n.before(1, 1))
                    dve.tensor_tensor(part(2), nmr[:, :, :], part(1), ALU.subtract).then_inc(s["mparts_ready"], 1)

                def magnitudes(n, pair):
                    b = pair % 2
                    need(dve, s["raw_full"], n.before(8, pair + 1))
                    need(dve, s["u_dve"], n.before(8, pair - 1))
                    need(dve, s["u_pool"], n.before(8, pair - 1))
                    dve.tensor_scalar(z_sb[b][:, :, :].rearrange("p j n -> p (j n)").bitcast(I32),
                                      raw_ps[:, :, :, :].rearrange("p j m n -> p (j m n)").bitcast(I32),
                                      0x7FFFFFFF, None, ALU.bitwise_and).then_inc(s["z_ready"], 1)

                def polynomial(n, pair):
                    b, h = pair % 2, 2 * pair
                    need(dve, s["z_ready"], n.before(8, pair + 1))
                    need(dve, s["g_ready"], n.before(8, pair - 1))
                    dve.scalar_tensor_tensor(out=u_sb[b][:, 0, :], in0=z_sb[b][:, 0, :], scalar=b8[:, h:h + 1],
                                             in1=z_sb[b][:, 0, :], op0=ALU.add, op1=ALU.mult).then_inc(s["u_dve"], 1)

                def norm_quad(n, t):
                    need(dve, s["tr_full"], n.before(4, t + 1))
                    need(dve, s["nt_ready"], n.before(4, t))
                    v = pv_ps[:, :].rearrange("p (g d) -> p g d", d=VW)
                    dve.reciprocal(rc[:, :], v[:, :, dh]).then_inc(s["rc_ready"], 1)
                    need(dve, s["rc_ready"], n.before(4, t + 1))
                    need(dve, s["fn_ready"], n.before(4, t))
                    dve.tensor_tensor(ntv[:, :, :, :, :].rearrange("p l k h d -> p (l k h) d"), v[:, :, 0:dh],
                                      rc[:, :].rearrange("p (g a) -> p g a", a=1).broadcast_to((P, 16, dh)), ALU.mult)\
                        .then_inc(s["nt_ready"], 1)
                    need(dve, s["nt_ready"], n.before(4, t + 1))
                    if t == 0:
                        need(dve, s["ft_full"], n.before(1))
                    nv = ntv[:, :, :, :, :].rearrange("p l k h d -> p l k (h d)")
                    dve.tensor_tensor(f_n[:, :, t * 64:t * 64 + 64], nv[:, :, 0, :], nv[:, :, 1, :], ALU.add)\
                        .then_inc(s["fn_ready"], 1)

                def y_bias(n):
                    need(dve, s["y_full"], n.before(1, 1))
                    dve.tensor_tensor(yb[:, :, :], t_ps[:, :].rearrange("p (l d) -> p l d", l=2),
                                      rows["bo"][:, :].rearrange("p (a d) -> p a d", a=1).broadcast_to((P, 2, dm)), ALU.add)\
                        .then_inc(s["yb_ready"], 1)

                def choose(n):
                    need(dve, s["lg_full"], n.before(1, 1))
                    dve.tensor_copy(fold(lgt), t_ps[:, 0:2 * ne]).then_inc(s["lg_copied"], 1)
                    need(dve, s["lg_copied"], n.before(1, 1))
                    dve.tensor_copy(logits_all[:, dyn(n, 2), :], lgt[:, :, :]).then_inc(s["lg_kept"], 1)
                    for lt in range(2):
                        need_alone(dve, passed["dve"], s["idx_ready"], n.before(2))
                        dve.max(top8[:, lt, :], lgt[:, lt, :]).then_inc(s["top_ready"], 1)
                    for lt in range(2):
                        need_alone(dve, passed["dve"], s["top_ready"], n.before(2, lt + 1))
                        dve.max_index(idx8[:, lt, :], top8[:, lt, :], lgt[:, lt, :]).then_inc(s["idx_ready"], 1)
                    need(dve, s["idx_ready"], n.before(2, 2))
                    dve.tensor_copy(top_all[:, dyn(n, 2), :], top8[:, :, 0:2]).then_inc(s["kept"], 1)
                    dve.tensor_copy(idxf[:, :, :], idx8[:, :, 0:2]).then_inc(s["idxf_ready"], 1)
                    need(dve, s["idxf_ready"], n.before(1, 1))
                    dve.tensor_copy(expert_all[:, dyn(n, 2), :], idxf[:, :, :]).then_inc(s["kept"], 1)
                    dve.tensor_tensor(hot[:, :, :, :].rearrange("p l c e -> p (l c) e"),
                                      idxf[:, :, :].rearrange("p l (c a) -> p (l c) a", a=1).broadcast_to((P, 4, ne)),
                                      iota_e[:, :].rearrange("p (a e) -> p a e", a=1).broadcast_to((P, 4, ne)), ALU.is_equal)\
                        .then_inc(s["hot_ready"], 1)

                def place(n):
                    b, c = n.par, 2 * ne
                    need(dve, s["lc_full"], n.before(1, 1))
                    need(dve, s["fill_ready"], n.before(1))
                    run = filled[:, b, :, :].rearrange("p c e -> p (c e)")
                    dve.tensor_tensor(locb[:, :, :, :].rearrange("p l c e -> p l (c e)"),
                                      t_ps[:, 0:2 * c].rearrange("p (l k) -> p l k", l=2),
                                      run.rearrange("p (a k) -> p a k", a=1).broadcast_to((P, 2, c)), ALU.add)\
                        .then_inc(s["locb_ready"], 1)
                    dve.tensor_tensor(filled[:, 1 - b, :, :].rearrange("p c e -> p (c e)"), t_ps[:, 2 * c:3 * c], run, ALU.add)\
                        .then_inc(s["fill_ready"], 1)
                    need(dve, s["locb_ready"], n.before(1, 1))
                    dve.tensor_tensor(lsel[:, :, :, :].rearrange("p l c e -> p (l c e)"),
                                      locb[:, :, :, :].rearrange("p l c e -> p (l c e)"),
                                      hot[:, :, :, :].rearrange("p l c e -> p (l c e)"), ALU.mult).then_inc(s["lsel_ready"], 1)
                    need(dve, s["lsel_ready"], n.before(1, 1))
                    dve.tensor_reduce(loc[:, :, :].rearrange("p l c -> p (l c)"),
                                      lsel[:, :, :, :].rearrange("p l c e -> p (l c) e"), AX, ALU.add).then_inc(s["loc_ready"], 1)
                    need(dve, s["loc_ready"], n.before(1, 1))
                    dve.tensor_copy(place_all[:, dyn(n, 2), :], loc[:, :, :]).then_inc(s["kept"], 1)
                    dve.tensor_scalar(fold(over), fold(loc), float(cap), float(4 * ne * cap), ALU.is_ge, ALU.mult)\
                        .then_inc(s["over_ready"], 1)
                    dve.scalar_tensor_tensor(out=fold(flat), in0=fold(idxf), scalar=float(2 * cap), in1=fold(loc),
                                             op0=ALU.mult, op1=ALU.add).then_inc(s["flat_ready"], 1)
                    need(dve, s["over_ready"], n.before(1, 1))
                    need(dve, s["flat_ready"], n.before(1, 1))
                    dve.tensor_tensor(fold(flat2), fold(flat), fold(over), ALU.add).then_inc(s["flat2_ready"], 1)
                    need(dve, s["flat2_ready"], n.before(1, 1))
                    if has(n + -2, nb):
                        dve.wait_ge(scat_out[b], (n + -2).landed(64))
                    dve.tensor_copy(slot_u[b][:, :], fold(flat2)).then_inc(s["slot_ready"], 1)
                    dve.tensor_copy(tok_u[b][:, :], tok_ids[:, dyn(n, 2)]).then_inc(s["slot_ready"], 1)

                def step(i, nb):
                    A, B, M, C, D = (has(i + d, nb) for d in (2, 1, 0, -1, -2))
                    for st in range(8):
                        if M:
                            magnitudes(i, st)
                        if st == 0:
                            if C:
                                norm_quad(i + -1, 2)
                            if A:
                                ekv_tile(i + 2, 0)
                        if M:
                            polynomial(i, st)
                        if st == 1:
                            if A:
                                ekv_tile(i + 2, 1)
                            if B:
                                part_high(i + 1)
                        if st == 2:
                            if D:
                                place(i + -2)
                            if B:
                                v_bias(i + 1)
                            if C:
                                norm_quad(i + -1, 3)
                            if A:
                                denominators(i + 2)
                            if B:
                                part_mid(i + 1)
                        if st == 3:
                            if A:
                                mixed_values(i + 2)
                        if st == 4:
                            if C:
                                y_bias(i + -1)
                                stats(i + -1, 2, lambda lt: yb[:, lt, :], "yb_ready", 1, 1)
                        if B and st >= 4:
                            for h in range(4 * (st - 4), 4 * (st - 4) + 2):
                                head_max(i + 1, h)
                        if st == 4 and M:
                            norm_quad(i, 0)
                        if st == 5:
                            if A:
                                stats(i + 2, 0, a_half, "mix_full", 1, 1)
                            if C:
                                normalise(i + -1, 2, lambda lt: yb[:, lt, :], yn, "yn_ready", ("yw_ready",))
                            if A:
                                normalise(i + 2, 0, a_half, hn, "hn_ready", ("hg_ready",))
                        if st == 6:
                            if C:
                                stats(i + -1, 3, lambda lt: h2[(i.par + 1) % 2][:, lt, :], "h2_ready", 1, 1)
                            if A:
                                stats(i + 2, 1, lambda lt: h1[:, lt, :], "h1_ready", 1, 1)
                            if M:
                                norm_quad(i, 1)
                            if C:
                                if has(i + -3, nb):
                                    dve.wait_ge(x2_out[(i.par + 1) % 2], (i + -3).landed())
                                normalise(i + -1, 3, lambda lt: h2[(i.par + 1) % 2][:, lt, :], x2[(i.par + 1) % 2], "x2_ready", ("x2t_full",))
                            if A:
                                normalise(i + 2, 1, lambda lt: h1[:, lt, :], x1, "x1_ready", ("hx0_ready", "x1t_full"))
                        if B and st >= 4:
                            for h in range(4 * (st - 4) + 2, 4 * (st - 4) + 4):
                                head_max(i + 1, h)
                        if st == 7:
                            if B:
                                max_parts(i + 1)
                            if C:
                                choose(i + -1)

                turns(dve, nb, step)

            @block.gpsimd
            def _(pool):
                def over_rows(dst, a, row):
                    r = rows[row][:, :].rearrange("p (a d) -> p a d", a=1).broadcast_to((P, 2, dm))
                    return a[:, :, :], r

                def scale_row(n, dst, src, row, op, ready, per, k, done, free=()):
                    need_alone(pool, passed["pool"], s[ready], n.before(per, k))
                    for f in free:
                        need_alone(pool, passed["pool"], s[f], n.before(1))
                    a, r = over_rows(dst, src, row)
                    pool.tensor_tensor(dst[:, :, :], a, r, op).then_inc(s[done], 1)

                def sum_rows(n, dst, a, b_, done):
                    pool.tensor_tensor(dst[:, :, :], a[:, :, :], b_[:, :, :], ALU.add).then_inc(s[done], 1)

                def mixer_norm(n):
                    scale_row(n, hg, hn, "ln_g", ALU.mult, "hn_ready", 2, 2, "hg_ready", ("h1_ready",))
                    need_alone(pool, passed["pool"], s["x1_ready"], n.before(2))
                    scale_row(n, h1, hg, "ln_b", ALU.add, "hg_ready", 1, 1, "h1_ready", ("hx0_ready",))

                def residual(n, b):
                    need_alone(pool, passed["pool"], s["x1_ready"], n.before(2, 2))
                    need_alone(pool, passed["pool"], s["hx_ready"], n.before(1))
                    sum_rows(n, hx0, h1, x1, "hx0_ready")
                    need_alone(pool, passed["pool"], s["h2_ready"], (n + -3).before(1) if has(n + -4, nb) else 0)
                    scale_row(n, hx[b], hx0, "ln_b2", ALU.add, "hx0_ready", 1, 1, "hx_ready")

                def remainder(n):
                    need_alone(pool, passed["pool"], s["part_h"], n.before(1, 1))
                    need_alone(pool, passed["pool"], s["part_l"], n.before(1))
                    pool.tensor_tensor(qkr[:, :, :], qkf[:, :, :], qkp[:, 0, :, :], ALU.subtract).then_inc(s["part_r"], 1)

                def part_low(n):
                    need_alone(pool, passed["pool"], s["part_m"], n.before(1, 1))
                    if has(n + -1, nb):
                        need_alone(pool, passed["pool"], qk_out[(n.par + 1) % 2], (n + -1).landed())
                    pool.tensor_tensor(qkp[:, 2, :, :], qkr[:, :, :], qkp[:, 1, :, :], ALU.subtract).then_inc(s["part_l"], 1)

                def polynomial(n, pair):
                    b, h = pair % 2, 2 * pair + 1
                    need_alone(pool, passed["pool"], s["z_ready"], n.before(8, pair + 1))
                    need_alone(pool, passed["pool"], s["u_pool"], n.before(8, pair))
                    pool.tensor_tensor(zb[:, :], z_sb[b][:, 1, :], b8[:, h:h + 1].broadcast_to((P, 512)), ALU.add)\
                        .then_inc(s["zb_ready"], 1)
                    need_alone(pool, passed["pool"], s["zb_ready"], n.before(8, pair + 1))
                    need_alone(pool, passed["pool"], s["g_ready"], n.before(8, pair - 1))
                    pool.tensor_tensor(u_sb[b][:, 1, :], zb[:, :], z_sb[b][:, 1, :], ALU.mult).then_inc(s["u_pool"], 1)

                def attention_norm(n, b):
                    scale_row(n, yw, yn, "ln_w", ALU.mult, "yn_ready", 2, 2, "yw_ready", ("h2_ready",))
                    need_alone(pool, passed["pool"], s["yw_ready"], n.before(1, 1))
                    need_alone(pool, passed["pool"], s["x2_ready"], (n + -1).before(2) if has(n + -2, nb) else 0)
                    if has(n + -2, nb):
                        need_alone(pool, passed["pool"], h2_out[n.par], (n + -2).landed())
                    sum_rows(n, h2[n.par], yw, hx[b], "h2_ready")

                def scatter(n):
                    b = n.par
                    need_alone(pool, passed["pool"], s["slot_ready"], n.before(2, 2))
                    for lt in range(2):
                        for c in range(2):
                            pool.indirect_dma_start(
                                out=slot_dram[c], out_offset=bass.IndirectOffsetOnAxis(ap=slot_u[b][:, 2 * lt + c:2 * lt + c + 1], axis=0),
                                in_=tok_u[b][:, lt:lt + 1], in_offset=None,
                                bounds_check=2 * ne * cap - 1, oob_is_err=False).then_inc(scat_out[b], 16)

                def step4(i, nb, ring):
                    A, B, M, C, D = (has(i + d, nb) for d in (2, 1, 0, -1, -2))
                    for st in range(8):
                        if M:
                            polynomial(i, st)
                        if st == 1 and B:
                            remainder(i + 1)
                        if st == 2 and B:
                            part_low(i + 1)
                        if st == 3 and D:
                            scatter(i + -2)
                        if st == 5:
                            if C:
                                attention_norm(i + -1, (ring + 3) % 4)
                            if A:
                                mixer_norm(i + 2)
                        if st == 6 and A:
                            residual(i + 2, (ring + 2) % 4)

                pool_turns(pool, nb, step4)
                for b in range(2):
                    pool.wait_ge(scat_out[b], 64 * (nb // 2))


def finish_routes(nc, g):
    ne, cap, tiles = g["ne"], g["cap"], g["tiles"]
    filled, iota_e = g["filled"], g["iota_e"]
    logits_all, top_all, expert_all, place_all = (g[k] for k in ("logits_all", "top_all", "expert_all", "place_all"))
    routes, gates, slot_tok, slot_dram = g["routes"], g["gates"], g["slot_tok"], g["slot_dram"]
    with ExitStack() as ctx:
        def sb(name, shape, dt=F32):
            return ctx.enter_context(nc.sbuf_tensor(name, shape, dt))

        def sem(name):
            return ctx.enter_context(nc.semaphore(name))

        big = [sb(f"big{b}", [P, tiles, ne]) for b in range(2)]
        soft = sb("soft", [P, tiles, ne])
        n1f = sb("n1f", [P, ne])
        n1i = sb("n1i", [P, ne], I32)
        col = {k: sb(f"col_{k}", [P, tiles]) for k in "off pos kept0 kept1 posm row z rz d2 e2 g2 sum rd w".split()}
        r_chain = sem("r_chain")
        r_counts = sem("r_counts")
        r_shift = sem("r_shift")
        r_exp = sem("r_exp")
        r_joined = sem("r_joined")
        r_table = sem("r_table")
        n1 = filled[:, 0, 0, :]

        def wide(a):
            return a.rearrange("p (t a) -> p t a", a=1).broadcast_to((P, tiles, ne))

        def tall(a):
            return a.rearrange("p (a e) -> p a e", a=1).broadcast_to((P, tiles, ne))

        with nc.Block() as block:
            @block.vector
            def _(dve):
                count = [0]

                def link(ins):
                    count[0] += 1
                    ins.then_inc(r_chain, 1)
                    dve.wait_ge(r_chain, count[0])

                link(dve.tensor_scalar(n1f[:, :], n1, float(cap), None, ALU.min))
                dve.tensor_copy(n1i[:, :], n1f[:, :]).then_inc(r_counts, 1)
                dve.tensor_tensor(soft[:, :, :], logits_all[:, :, :], wide(top_all[:, :, 0]), ALU.subtract).then_inc(r_shift, 1)
                dve.tensor_tensor(col["d2"][:, :], top_all[:, :, 1], top_all[:, :, 0], ALU.subtract).then_inc(r_shift, 1)
                link(dve.tensor_tensor(big[0][:, :, :], wide(expert_all[:, :, 1]), tall(iota_e[:, :]), ALU.is_equal))
                link(dve.tensor_tensor(big[1][:, :, :], big[0][:, :, :], tall(n1), ALU.mult))
                link(dve.tensor_reduce(col["off"][:, :], big[1][:, :, :], AX, ALU.add))
                link(dve.tensor_tensor(place_all[:, :, 1], place_all[:, :, 1], col["off"][:, :], ALU.add))
                for c in range(2):
                    link(dve.tensor_scalar(col[f"kept{c}"][:, :], place_all[:, :, c], float(cap), None, ALU.is_lt))
                    link(dve.tensor_scalar(col["posm"][:, :], place_all[:, :, c], float(cap - 1), None, ALU.min))
                    link(dve.scalar_tensor_tensor(out=col["row"][:, :], in0=expert_all[:, :, c], scalar=float(cap),
                                                  in1=col["posm"][:, :], op0=ALU.mult, op1=ALU.add))
                    link(dve.tensor_copy(routes[:, c, :], col["row"][:, :]))
                dve.wait_ge(r_exp, 2)
                link(dve.tensor_reduce(col["z"][:, :], soft[:, :, :], AX, ALU.add))
                link(dve.reciprocal(col["rz"][:, :], col["z"][:, :]))
                link(dve.tensor_tensor(col["g2"][:, :], col["e2"][:, :], col["rz"][:, :], ALU.mult))
                link(dve.tensor_tensor(col["sum"][:, :], col["g2"][:, :], col["rz"][:, :], ALU.add))
                link(dve.tensor_scalar(col["w"][:, :], col["sum"][:, :], 1e-9, None, ALU.max))
                link(dve.reciprocal(col["rd"][:, :], col["w"][:, :]))
                for c, gate in enumerate((col["rz"], col["g2"])):
                    link(dve.tensor_tensor(col["sum"][:, :], gate[:, :], col["rd"][:, :], ALU.mult))
                    link(dve.tensor_tensor(gates[:, c, :], col["sum"][:, :], col[f"kept{c}"][:, :], ALU.mult))

            @block.scalar
            def _(act):
                act.wait_ge(r_shift, 2)
                act.activation(soft[:, :, :], soft[:, :, :], ACT.Exp).then_inc(r_exp, 1)
                act.activation(col["e2"][:, :], col["d2"][:, :], ACT.Exp).then_inc(r_exp, 1)

            @block.sync
            def _(sp):
                sp.wait_ge(r_counts, 1)
                for e in range(ne):
                    n = sp.value_load(n1i[0:1, e:e + 1], min_val=0, max_val=cap)
                    base = e * 2 * cap
                    sp.dma_start(slot_dram[0][bass.ds(n + base, cap), :].rearrange("(a m) o -> a (m o)", a=16),
                                 slot_dram[1][base:base + cap, :].rearrange("(a m) o -> a (m o)", a=16)).then_inc(r_joined, 16)
                    sp.wait_ge(r_joined, 16 * (e + 1))
                for e in range(ne):
                    base = e * 2 * cap
                    sp.dma_start(slot_tok[:, e, :], slot_dram[0][base:base + cap, :].rearrange("(p j) o -> p (j o)", p=P))\
                        .then_inc(r_table, 16)
                sp.wait_ge(r_table, 16 * ne)


def experts(nc, g):
    ne, cap, tiles, ff = g["ne"], g["cap"], g["tiles"], g["ff"]
    x2_dram, w_gate, w_down = g["x2_dram"], g["w_gate"], g["w_down"]
    ident, slot_tok = g["ident"], g["slot_tok"]
    gpe = cap // (4 * P)
    fts = ff // P
    eo_view = g["eo_dram"].rearrange("(e p j) d -> e p j d", e=ne, p=P)
    with ExitStack() as ctx:
        def sb(name, shape, dt=F32):
            return ctx.enter_context(nc.sbuf_tensor(name, shape, dt))

        def bank(name, shape, dt=F32):
            return ctx.enter_context(nc.psum_tensor(name, shape, dt))

        def sem(name):
            return ctx.enter_context(nc.semaphore(name))

        wg_e = [sb(f"wg_e{b}", [P, 2, ff]) for b in range(2)]
        wd_e = [sb(f"wd_e{b}", [P, fts, 256]) for b in range(2)]
        idc = [sb(f"idc{b}", [P, 4], U32) for b in range(2)]
        xg = [sb(f"xg{b}", [P, 4, 256]) for b in range(2)]
        xt = [sb(f"xt{b}", [P, 2, 512]) for b in range(2)]
        ht = [sb(f"ht{b}", [P, fts, 512]) for b in range(2)]
        eo = [sb(f"eo{b}", [P, 4, 256]) for b in range(2)]
        tr_ps = [bank(f"tr_ps{k}", [P, 512]) for k in range(2)]
        h_ps = [bank(f"h_ps{k}", [P, 512]) for k in range(4)]
        o_ps = bank("o_ps", [P, 4, 256])
        w_in = [sem(f"w_in{b}") for b in range(2)]
        rows_in = [sem(f"rows_in{b}") for b in range(2)]
        eo_out = [sem(f"eo_out{b}") for b in range(2)]
        ids_ready = sem("ids_ready")
        xtr_full = sem("xtr_full")
        xt_ready = sem("xt_ready")
        h_full = sem("h_full")
        h_ready = sem("h_ready")
        o_full = sem("o_full")
        eo_ready = sem("eo_ready")
        passed = {k: sem(f"x_passed_{k}") for k in ("sp", "pe", "pool")}
        PER = {ids_ready: 1, xtr_full: 2, xt_ready: 2, h_full: fts, h_ready: fts, o_full: 4, eo_ready: 2}

        class Group:

            def __init__(self, ep, par, gi, b):
                self.e, self.par, self.b = ep * 2 + par, par, b
                self.j = gi * 8 + b * 4
                self.ep, self.gi = ep, gi

            def number(self, mul, add=0):
                return self.ep * (2 * gpe * mul) + self.gi * (2 * mul) + ((self.par * gpe + self.b) * mul + add)

            def past(self, sem_, k=0):
                per = PER[sem_]
                return self.number(per, 2 * per + k)

            def landed(self, per, extra=0):
                return self.ep * (gpe * per) + self.gi * per + (self.par * gpe // 2 + 1 + extra) * per

        def groups(eng, body, head=None, tail=None, pairs=None):
            with eng.Fori(0, pairs or ne // 2) as ep:
                pair(eng, ep, body, head, tail)

        def pair(eng, ep, body, head=None, tail=None):
            for par in range(2):
                if head:
                    head(ep, par)
                with eng.Fori(0, gpe // 2) as gi:
                    for b in range(2):
                        body(Group(ep, par, gi, b))
                if tail:
                    tail(ep, par)

        def start_past(eng, sem_):
            eng.sem_inc(sem_, 2 * PER[sem_])

        with nc.Block() as block:
            @block.sync
            def _(sp):
                def load_weights(e, par):
                    sp.dma_start(wg_e[par][:, :, :], w_gate[bass.ds(e, 1)].rearrange("a (k p) f -> p (a k) f", p=P)).then_inc(w_in[par], 16)
                    sp.dma_start(wd_e[par][:, :, :], w_down[bass.ds(e, 1)].rearrange("a (k p) d -> p (a k) d", p=P)).then_inc(w_in[par], 16)

                def store(q):
                    need_alone(sp, passed["sp"], eo_ready, q.past(eo_ready, 2))
                    sp.dma_start(eo_view[bass.ds(q.e, 1), :, bass.ds(q.j, 4), :].rearrange("a p j d -> (a p) j d"),
                                 eo[q.b][:, :, :]).then_inc(eo_out[q.b], 16)

                load_weights(0, 0)
                load_weights(1, 1)
                groups(sp, store, tail=lambda ep, par: load_weights(ep * 2 + (par + 2), par), pairs=ne // 2 - 1)
                pair(sp, ne // 2 - 1, store)
                for b in range(2):
                    sp.wait_ge(eo_out[b], 16 * ne * gpe // 2)

            @block.gpsimd
            def _(pool):
                ids = slot_tok[:, :, :].rearrange("p e j -> p (e j)")

                def gather(q):
                    need_alone(pool, passed["pool"], xtr_full, q.past(xtr_full, -2))
                    pool.tensor_copy(idc[q.b][:, :], ids[:, bass.ds(q.number(4), 4)]).then_inc(ids_ready, 1)
                    need_alone(pool, passed["pool"], ids_ready, q.past(ids_ready, 1))
                    for j in range(4):
                        pool.indirect_dma_start(out=xg[q.b][:, j, :], out_offset=None, in_=x2_dram,
                                                in_offset=bass.IndirectOffsetOnAxis(ap=idc[q.b][:, j:j + 1], axis=0))\
                            .then_inc(rows_in[q.b], 16)

                start_past(pool, ids_ready)
                groups(pool, gather)

            @block.tensor
            def _(pe):
                def group(q):
                    pe.wait_ge(rows_in[q.b], q.landed(64))
                    for dk in range(2):
                        pe.wait_ge(xt_ready, q.past(xt_ready, dk - 1))
                        for j in range(4):
                            mm = pe.transpose(tr_ps[dk][:, j * P:j * P + P], xg[q.b][:, j, dk * P:dk * P + P], ident[:, :])
                        mm.then_inc(xtr_full, 1)
                    pe.wait_ge(xt_ready, q.past(xt_ready, 2))
                    for f in range(fts):
                        pe.wait_ge(h_ready, q.past(h_ready, f - 3))
                        for dk in range(2):
                            mm = pe.matmul(h_ps[f % 4][:, :], wg_e[q.par][:, dk, f * P:f * P + P], xt[q.b][:, dk, :],
                                           start=(dk == 0), stop=(dk == 1))
                        mm.then_inc(h_full, 1)
                    for j in range(4):
                        pe.wait_ge(eo_ready, q.past(eo_ready, j // 2 - 1))
                        for f in range(fts):
                            if j == 0:
                                pe.wait_ge(h_ready, q.past(h_ready, f + 1))
                            mm = pe.matmul(o_ps[:, j, :], ht[q.b][:, f, j * P:j * P + P], wd_e[q.par][:, f, :],
                                           start=(f == 0), stop=(f == fts - 1))
                        mm.then_inc(o_full, 1)

                start_past(pe, xtr_full)
                start_past(pe, h_full)
                start_past(pe, o_full)
                groups(pe, group, head=lambda ep, par: need_alone(pe, passed["pe"], w_in[par], ep * 32 + 32))

            @block.scalar
            def _(act):
                def gelu(q):
                    act.wait_ge(o_full, q.past(o_full, -4))
                    for f in range(fts):
                        act.wait_ge(h_full, q.past(h_full, f + 1))
                        act.activation(ht[q.b][:, f, :], h_ps[f % 4][:, :], ACT.Gelu).then_inc(h_ready, 1)

                start_past(act, h_ready)
                groups(act, gelu)

            @block.vector
            def _(dve):
                def copies(q):
                    for dk in range(2):
                        dve.wait_ge(xtr_full, q.past(xtr_full, dk + 1))
                        if dk == 0:
                            dve.wait_ge(h_full, q.past(h_full, -fts))
                        dve.tensor_copy(xt[q.b][:, dk, :], tr_ps[dk][:, :]).then_inc(xt_ready, 1)
                    for half in range(2):
                        dve.wait_ge(o_full, q.past(o_full, 2 * half + 2))
                        if half == 0:
                            dve.wait_ge(eo_out[q.b], q.landed(16, -1))
                        dve.tensor_copy(eo[q.b][:, 2 * half:2 * half + 2, :], o_ps[:, 2 * half:2 * half + 2, :]).then_inc(eo_ready, 1)

                start_past(dve, xt_ready)
                start_past(dve, eo_ready)
                groups(dve, copies)


def combine(nc, g):
    tiles, routes, gates = g["tiles"], g["routes"], g["gates"]
    eo_dram = g["eo_dram"]
    h2_dram = g["h2_dram"].rearrange("(q l p) d -> q p l d", l=2, p=P)
    out = g["out"].rearrange("q (l p) d -> q p l d", l=2)
    with ExitStack() as ctx:
        def sb(name, shape, dt=F32):
            return ctx.enter_context(nc.sbuf_tensor(name, shape, dt))

        def sem(name):
            return ctx.enter_context(nc.semaphore(name))

        idx = [sb(f"cidx{b}", [P, 2, 2], U32) for b in range(2)]
        gate = [sb(f"cgate{b}", [P, 2, 2]) for b in range(2)]
        got = [sb(f"got{b}", [P, 2, 2, 256]) for b in range(2)]
        res = [sb(f"res{b}", [P, 2, 256]) for b in range(2)]
        acc = [sb(f"acc{b}", [P, 2, 256]) for b in range(2)]
        sums = [sb(f"sums{b}", [P, 2, 256]) for b in range(2)]
        got_in = [sem(f"got_in{b}") for b in range(2)]
        res_in = [sem(f"res_in{b}") for b in range(2)]
        sum_out = [sem(f"sum_out{b}") for b in range(2)]
        idx_ready = sem("idx2_ready")
        gate_ready = sem("gate_ready")
        first_done = sem("first_done")
        sums_done = sem("sums_done")
        passed = {k: sem(f"c_passed_{k}") for k in ("sp", "pool")}
        rounds = tiles // 4

        with nc.Block() as block:
            @block.sync
            def _(sp):
                def load(j, b):
                    sp.dma_start(res[b][:, :, :], h2_dram[bass.ds(j * 2 + b, 1)].rearrange("a p l d -> (a p) l d")).then_inc(res_in[b], 16)

                for b in range(2):
                    load(0, b)
                with sp.Fori(0, rounds - 1) as j:
                    for b in range(2):
                        need_alone(sp, passed["sp"], sums_done, j * 4 + (2 * b + 4))
                        sp.dma_start(out[bass.ds(j * 2 + b, 1)].rearrange("a p l d -> (a p) l d"), sums[b][:, :, :]).then_inc(sum_out[b], 16)
                        load(j + 1, b)
                for b in range(2):
                    sp.wait_ge(sums_done, (rounds - 1) * 4 + 2 * b + 4)
                    sp.dma_start(out[2 * rounds - 2 + b], sums[b][:, :, :]).then_inc(sum_out[b], 16)
                for b in range(2):
                    sp.wait_ge(sum_out[b], 16 * rounds)

            @block.gpsimd
            def _(pool):
                with pool.Fori(0, rounds) as j:
                    for b in range(2):
                        need_alone(pool, passed["pool"], sums_done, j * 4 + 2 * b)
                        pool.tensor_copy(idx[b][:, :, :], routes[:, :, bass.ds(j * 4 + 2 * b, 2)]).then_inc(idx_ready, 1)
                        need_alone(pool, passed["pool"], idx_ready, j * 2 + (b + 1))
                        for c in range(2):
                            for l in range(2):
                                pool.indirect_dma_start(out=got[b][:, c, l, :], out_offset=None, in_=eo_dram,
                                                        in_offset=bass.IndirectOffsetOnAxis(ap=idx[b][:, c, l:l + 1], axis=0))\
                                    .then_inc(got_in[b], 16)

            @block.vector
            def _(dve):
                dve.sem_inc(sums_done, 2)
                with dve.Fori(0, rounds) as j:
                    for b in range(2):
                        dve.tensor_copy(gate[b][:, :, :], gates[:, :, bass.ds(j * 4 + 2 * b, 2)]).then_inc(gate_ready, 1)
                        dve.wait_ge(gate_ready, j * 2 + (b + 1))
                        dve.wait_ge(got_in[b], j * 64 + 64)
                        dve.wait_ge(res_in[b], j * 16 + 16)
                        for l in range(2):
                            dve.scalar_tensor_tensor(out=acc[b][:, l, :], in0=got[b][:, 0, l, :], scalar=gate[b][:, 0, l:l + 1],
                                                     in1=res[b][:, l, :], op0=ALU.mult, op1=ALU.add).then_inc(first_done, 1)
                        dve.wait_ge(sum_out[b], j * 16)
                        for l in range(2):
                            dve.wait_ge(first_done, j * 4 + (2 * b + l + 1))
                            dve.scalar_tensor_tensor(out=sums[b][:, l, :], in0=got[b][:, 1, l, :], scalar=gate[b][:, 1, l:l + 1],
                                                     in1=acc[b][:, l, :], op0=ALU.mult, op1=ALU.add).then_inc(sums_done, 1)


_NAMES = ["x", "wkv", "wq", "bkv", "bq_tok", "w_bias_t", "mask_t", "out_w", "out_b", "ln_g", "ln_b",
          "wq_t", "bq", "wk_t", "bk", "wv_t", "bv", "wo_t", "bo", "beta", "t_par", "ln_w", "ln_b2",
          "wg", "w_gate", "w_down"]


def kernel(**inputs):
    import numpy as _np
    import concourse.bacc as _bacc
    from concourse import mybir as _mybir
    from concourse.bass_utils import run_bass_kernel_spmd as _run

    a = {k: _np.asarray(v) for k, v in inputs.items()}
    n, c, l, h = a["x"].shape
    tok, att, ffn = "L0_tok_", "L0_attn_", "L0_ffn_"
    host = {
        "x": a["x"].reshape(n, c, l * h),
        "wkv": _np.stack([a[tok + "Wk_w"].T, a[tok + "Wv_w"].T]), "wq": a[tok + "Wq_w"].T,
        "bkv": _np.stack([a[tok + "Wk_b"], a[tok + "Wv_b"]]), "bq_tok": a[tok + "Wq_b"],
        "w_bias_t": a[tok + "w_bias"].T, "mask_t": a[tok + "local_mask"].T,
        "out_w": a[tok + "out_w"], "out_b": a[tok + "out_b"], "ln_g": a[tok + "ln_g"], "ln_b": a[tok + "ln_b"],
        "wq_t": a[att + "Wq"].T, "bq": a[att + "bq"], "wk_t": a[att + "Wk"].T, "bk": a[att + "bk"],
        "wv_t": a[att + "Wv"].T, "bv": a[att + "bv"], "wo_t": a[att + "Wo"].T, "bo": a[att + "bo"],
        "beta": a[att + "beta"], "t_par": a[att + "t"], "ln_w": a[att + "ln_w"], "ln_b2": a[att + "ln_b"],
        "wg": a[ffn + "wg"], "w_gate": a[ffn + "w_gate"], "w_down": a[ffn + "w_down"],
    }
    nc = _bacc.Bacc("TRN2", target_bir_lowering=False, num_devices=1)
    arrays, args = {}, []
    for name in _NAMES:
        v = _np.ascontiguousarray(host[name])
        arrays[f"in_{name}"] = v
        args.append(nc.dram_tensor(f"in_{name}", v.shape, _mybir.dt.from_np(v.dtype), kind="ExternalInput").ap())
    args.append(nc.dram_tensor("out_0", (n, l, c * h), _mybir.dt.from_np(_np.dtype("float32")), kind="ExternalOutput").ap())
    tower_program(nc, *args)
    r = _run(nc, [arrays], core_ids=[0])
    return r.results[0]["out_0"]
```

```python
from contextlib import ExitStack

import concourse.bass as bass
from concourse import mybir

ALU = mybir.AluOpType
ACT = mybir.ActivationFunctionType
AX = mybir.AxisListType.X
F32 = mybir.dt.float32
BF16 = mybir.dt.bfloat16
U32 = mybir.dt.uint32
I32 = mybir.dt.int32
U8 = mybir.dt.uint8

P = 128
EPS = 1e-5
PARTS_Q = (0, 0, 0, 1, 1, 2)
PARTS_K = (0, 1, 2, 0, 1, 0)
RUNS_Q = ((0, 1, 3), (1, 1, 2), (2, 1, 1))
RUNS_K = ((0, 3, 1), (0, 2, 1), (0, 1, 1))
STACK_DMAS = len(RUNS_Q + RUNS_K)
SPLIT_DMAS = 2 * 3
SROWS = 16 * len(PARTS_Q)
NPART = 3
VW = 32
LOOP_FIRST = 2


class Batch:

    def __init__(self, c, reg=None):
        self.c, self.reg = c, reg

    def __add__(self, d):
        return Batch(self.c + d, self.reg)

    def before(self, per=1, k=0):
        return self.c * per + k if self.reg is None else self.reg * (2 * per) + (self.c * per + k)

    def landed(self, per=16):
        rounds = self.c // 2 + 1
        return rounds * per if self.reg is None else self.reg * per + rounds * per

    @property
    def par(self):
        return self.c % 2


def need(eng, sem, value):
    if isinstance(value, int) and value <= 0:
        return
    eng.wait_ge(sem, value)


def need_alone(eng, passed, sem, value):
    if isinstance(value, int) and value <= 0:
        return
    eng.wait_ge(sem, value)
    if not isinstance(value, int):
        eng.sem_inc(passed, 1)


def turns(eng, nb, step, ahead=3):
    last_full = nb - 1 - ahead
    trips = (last_full - LOOP_FIRST + 1) // 2
    for i in range(-3, LOOP_FIRST):
        step(Batch(i), nb)
    with eng.Fori(0, trips) as j:
        for c in range(2):
            step(Batch(LOOP_FIRST + c, j), nb)
    for i in range(LOOP_FIRST + 2 * trips, nb + 2):
        step(Batch(i), nb)


def pool_turns(eng, nb, step):
    last_full = nb - 4
    trips = (last_full - LOOP_FIRST + 1) // 2
    for i in range(-3, LOOP_FIRST):
        step(Batch(i), nb, i % 4)
    with eng.Fori(0, trips // 2) as j:
        for c in range(4):
            step(Batch4(LOOP_FIRST + c, j), nb, (LOOP_FIRST + c) % 4)
    first = LOOP_FIRST + 4 * (trips // 2)
    for i in range(first, nb + 2):
        step(Batch(i), nb, i % 4)


class Batch4(Batch):

    def __add__(self, d):
        return Batch4(self.c + d, self.reg)

    def before(self, per=1, k=0):
        return self.reg * (4 * per) + (self.c * per + k)

    def landed(self, per=16):
        return self.reg * (2 * per) + (self.c // 2 + 1) * per


def slot(h):
    return 2 * (h % 8) + h // 8


def has(n, nb):
    return n.reg is not None or 0 <= n.c < nb


def tower_program(nc, x, wkv, wq, bkv, bq_tok, w_bias_t, mask_t, out_w, out_b, ln_g, ln_b,
                  wq_t, bq, wk_t, bk, wv_t, bv, wo_t, bo, beta, t_par, ln_w, ln_b2,
                  wg, w_gate, w_down, out):
    nb, cin, ltok, hm = 64, 64, 256, 4
    nb = x.shape[0]
    dm = 256
    nh, dh = 16, 16
    ne, ff = wg.shape[1], w_gate.shape[2]
    tokens = nb * ltok
    cap = 2 * tokens // ne
    tiles = tokens // P
    SC = 1.0 / dh ** 0.5

    h2_dram = nc.dram_tensor("h2_dram", (tokens, dm), F32, kind="Internal").ap()
    x2_dram = nc.dram_tensor("x2_dram", (tokens, dm), F32, kind="Internal").ap()
    eo_dram = nc.dram_tensor("eo_dram", (ne * cap, dm), F32, kind="Internal").ap()
    qk_dram = [nc.dram_tensor(f"qk_dram{b}", (2, NPART, dh, nh * ltok), BF16, kind="Internal").ap() for b in range(2)]
    slot_dram = [nc.dram_tensor(f"slot_dram{c}", (ne * 2 * cap, 1), U32, kind="Internal").ap() for c in range(2)]

    outer = ExitStack()
    with outer:
        def keep(name, shape, dt=F32):
            return outer.enter_context(nc.sbuf_tensor(name, shape, dt))

        logits_all = keep("logits_all", [P, tiles, ne])
        top_all = keep("top_all", [P, tiles, 2])
        expert_all = keep("expert_all", [P, tiles, 2])
        place_all = keep("place_all", [P, tiles, 2])
        filled = keep("filled", [P, 2, 2, ne])
        iota_e = keep("iota_e", [P, ne])
        ident = keep("ident", [P, P])

        tower(nc, locals())
        routes = keep("routes", [P, 2, tiles], U32)
        gates = keep("gates", [P, 2, tiles])
        slot_tok = keep("slot_tok", [P, ne, cap // P], U32)
        finish_routes(nc, locals())
        experts(nc, locals())
        combine(nc, locals())


def tower(nc, g):
    x, out_w, wg = g["x"], g["out_w"], g["wg"]
    nb, ltok, dm, nh, dh, ne, cap, tiles, SC = (g[k] for k in "nb ltok dm nh dh ne cap tiles SC".split())
    qk_dram, slot_dram = g["qk_dram"], g["slot_dram"]
    ident, iota_e, filled = g["ident"], g["iota_e"], g["filled"]
    logits_all, top_all, expert_all, place_all = (g[k] for k in ("logits_all", "top_all", "expert_all", "place_all"))
    h2_dram = g["h2_dram"].rearrange("(n lt p) d -> n p lt d", p=P, lt=2)
    x2_dram = g["x2_dram"].rearrange("(n lt p) d -> n p lt d", p=P, lt=2)

    ctx = ExitStack()
    with ctx:
        def sb(name, shape, dt=F32):
            return ctx.enter_context(nc.sbuf_tensor(name, shape, dt))

        def bank(name, shape, dt=F32):
            return ctx.enter_context(nc.psum_tensor(name, shape, dt))

        def sem(name):
            return ctx.enter_context(nc.semaphore(name))

        wkv_sb = sb("wkv_sb", [65, 2, 64])
        wq_sb = sb("wq_sb", [65, 64])
        xid = sb("xid", [65, 4, 64])
        ew_t = sb("ew_t", [P, 2, 256])
        mask_sb = sb("mask_sb", [P, 2, 256], U8)
        outw_sb = sb("outw_sb", [P, 2, 256])
        wqa = sb("wqa", [P, 2, 256])
        wka = sb("wka", [P, 2, 256])
        wva = sb("wva", [P, 2, 256])
        woa = sb("woa", [P, 2, 256])
        wg_sb = sb("wg_sb", [P, 2, ne])
        rows = {k: sb(f"row_{k}", [P, 256]) for k in ("ln_g", "ln_b", "bv", "bo", "ln_w", "ln_b2")}
        bqk = sb("bqk", [P, 4])
        beta_sb = sb("beta_sb", [P, nh])
        t_sb = sb("t_sb", [P, nh])
        b8 = sb("b8", [P, nh])
        c16 = sb("c16", [P, nh])
        eps = sb("eps", [P, 1])
        identb = sb("identb", [P, P], BF16)
        before_b = sb("before_b", [P, P], BF16)
        ones_b = sb("ones_b", [P, P], BF16)
        tok_ids = sb("tok_ids", [P, tiles], I32)
        iota_i = sb("iota_i", [P, ne], I32)
        zero_i = sb("zero_i", [P, 2 * ne * cap // P], U32)

        xb = [sb(f"xb{b}", [65, ltok * 4]) for b in range(2)]
        ek = sb("ek", [P, 2, 256])
        ekv = sb("ekv", [P, 2, 256])
        eq = sb("eq", [P, 2, 256])
        dn = sb("dn", [P, 2, 256])
        rec = sb("rec", [P, 2, 256])
        y_t = sb("y_t", [P, 2, 256])
        hn = sb("hn", [P, 2, 256])
        hg = sb("hg", [P, 2, 256])
        h1 = sb("h1", [P, 2, 256])
        x1 = sb("x1", [P, 2, 256])
        hx0 = sb("hx0", [P, 2, 256])
        hx = [sb(f"hxr{b}", [P, 2, 256]) for b in range(4)]
        x1_t = [sb(f"x1_t{b}", [P, 2, 256]) for b in range(2)]
        stat = [sb(f"stat{k}", [P, 2, 6]) for k in range(4)]
        mv = [sb(f"mv{k}", [P, 2, 2]) for k in range(4)]
        lnv = [sb(f"lnv{k}", [P, 2]) for k in range(4)]
        rs = [sb(f"rs{k}", [P, 2]) for k in range(4)]
        qkf = sb("qkf", [P, 4, 256])
        qkr = sb("qkr", [P, 4, 256])
        qkp = sb("qkp", [P, NPART, 4, 256], BF16)
        q_stack = [sb(f"q_stack{b}", [P, nh, ltok], BF16) for b in range(2)]
        k_stack = [sb(f"k_stack{b}", [P, nh, ltok], BF16) for b in range(2)]
        v_sb = [sb(f"v_sb{b}", [P, 2, nh, VW]) for b in range(2)]
        rmax = sb("rmax", [P, nh, 2])
        nmx = sb("nmx", [P, nh, 2])
        nmr = sb("nmr", [P, nh, 2])
        mparts = sb("mparts", [P, 2, NPART, nh], BF16)
        mrow = sb("mrow", [NPART * nh, ltok], BF16)
        z_sb = [sb(f"z_sb{b}", [P, 2, 512]) for b in range(2)]
        u_sb = [sb(f"u_sb{b}", [P, 2, 512]) for b in range(2)]
        zb = sb("zb", [P, 512])
        p_sb = [sb(f"p_sb{b}", [P, 4, 2, 256]) for b in range(2)]
        g_sb = [sb(f"g_sb{b}", [P, 4, 2, 256]) for b in range(2)]
        f_sb = sb("f_sb", [P, 512])
        rc = sb("rc", [P, 16])
        ntv = sb("ntv", [P, 2, 2, 4, 16])
        f_n = sb("f_n", [P, 2, 256])
        f_t = sb("f_t", [P, 2, 256])
        yb = sb("yb", [P, 2, 256])
        yn = sb("yn", [P, 2, 256])
        yw = sb("yw", [P, 2, 256])
        h2 = [sb(f"h2_{b}", [P, 2, 256]) for b in range(2)]
        x2 = [sb(f"x2_{b}", [P, 2, 256]) for b in range(2)]
        x2_t = sb("x2_t", [P, 2, 256])
        lgt = sb("lgt", [P, 2, ne])
        top8 = sb("top8", [P, 2, 8])
        idx8 = sb("idx8", [P, 2, 8], U32)
        idxf = sb("idxf", [P, 2, 2])
        hot = sb("hot", [P, 2, 2, ne], BF16)
        locb = sb("locb", [P, 2, 2, ne])
        lsel = sb("lsel", [P, 2, 2, ne])
        loc = sb("loc", [P, 2, 2])
        over = sb("over", [P, 2, 2])
        flat = sb("flat", [P, 2, 2])
        flat2 = sb("flat2", [P, 2, 2])
        slot_u = [sb(f"slot_u{b}", [P, 4], U32) for b in range(2)]
        tok_u = [sb(f"tok_u{b}", [P, 2], U32) for b in range(2)]

        raw_ps = bank("raw_ps", [P, 2, 2, 256])
        sh_ps = bank("sh_ps", [P, 2, 2, 256])
        pv_ps = bank("pv_ps", [P, 512])
        a_ps = bank("a_ps", [P, 512])
        b_ps = bank("b_ps", [P, 512])
        t_ps = bank("t_ps", [P, 512])
        b_bf = b_ps[:, :].bitcast(BF16)

        s_w = sem("s_w")
        s_c0 = sem("s_c0")
        s_c1 = sem("s_c1")
        s_d = sem("s_d")
        s_z = sem("s_z")
        s_zd = sem("s_zd")
        s_i = sem("s_i")
        with nc.Block() as block:
            @block.sync
            def _(sp):
                loads = [
                    (wkv_sb[0:64, :, :], g["wkv"].rearrange("k c d -> c k d")), (wkv_sb[64:65, :, :], g["bkv"].rearrange("k (a d) -> a k d", a=1)),
                    (wq_sb[0:64, :], g["wq"]), (wq_sb[64:65, :], g["bq_tok"].rearrange("(a d) -> a d", a=1)),
                    (xid[64:65, :, :], g["out_b"].rearrange("(a h c) -> a h c", a=1, c=64)),
                    (ew_t[:, :, :], g["w_bias_t"].rearrange("(s p) t -> p s t", p=P)),
                    (mask_sb[:, :, :], g["mask_t"].rearrange("(s p) t -> p s t", p=P)),
                    (wg_sb[:, :, :], wg.rearrange("(k p) e -> p k e", p=P)),
                    (bqk[:, 0:2], g["bq"].rearrange("(m p) -> p m", p=P)),
                    (bqk[:, 2:4], g["bk"].rearrange("(m p) -> p m", p=P)),
                    (beta_sb[:, :], g["beta"].partition_broadcast(P)),
                    (t_sb[:, :], g["t_par"].partition_broadcast(P)),
                ]
                loads += [(w[:, :, :], d.rearrange("(k p) n -> p k n", p=P)) for w, d in
                          ((outw_sb, out_w), (wqa, g["wq_t"]), (wka, g["wk_t"]), (wva, g["wv_t"]), (woa, g["wo_t"]))]
                loads += [(r[:, :], g[k].partition_broadcast(P)) for k, r in rows.items()]
                for dst, src in loads:
                    sp.dma_start(dst, src, allow_slow_non_contiguous=True).then_inc(s_w, 16)
                sp.wait_ge(s_w, 16 * len(loads))
                sp.wait_ge(s_z, 1)
                for c in range(2):
                    sp.dma_start(slot_dram[c].rearrange("(p m) o -> p (m o)", p=P), zero_i[:, :]).then_inc(s_zd, 16)
                sp.wait_ge(s_zd, 32)

            @block.gpsimd
            def _(pool):
                pool.memset(ident[:, :], 0.0).then_inc(s_c0, 1)
                pool.memset(before_b[:, :], 1.0).then_inc(s_c0, 1)
                pool.iota(iota_i[:, :], pattern=[[1, ne]], base=0, channel_multiplier=0).then_inc(s_c0, 1)
                pool.iota(tok_ids[:, :], pattern=[[P, tiles]], base=0, channel_multiplier=1).then_inc(s_c0, 1)
                pool.wait_ge(s_c0, 4)
                pool.affine_select(out=ident[:, :], in_=ident[:, :], compare_op=ALU.not_equal, fill=1.0,
                                   base=0, pattern=[[-1, P]], channel_multiplier=1).then_inc(s_c1, 1)
                pool.affine_select(out=before_b[:, :], in_=before_b[:, :], compare_op=ALU.is_ge, fill=0.0,
                                   base=-1, pattern=[[1, P]], channel_multiplier=-1).then_inc(s_c1, 1)

            @block.vector
            def _(dve):
                fills = [(zero_i[:, :], 0), (ones_b[:, :], 1.0), (eps[:, :], EPS), (filled[:, :, :, :], 0.0)]
                fills += [(v[:, :, :, :], 0.0) for v in v_sb]
                for b in range(2):
                    fills += [(xb[b][64:65, :], 1.0), (k_stack[b][96:128, :, :], 1.0), (q_stack[b][96:128, :, :], 0.0)]
                for n, (dst, value) in enumerate(fills):
                    dve.memset(dst, value).then_inc(s_z if n == 0 else s_i, 1)
                done = len(fills) - 1
                dve.wait_ge(s_i, done)
                for v in v_sb:
                    dve.memset(v[:, :, :, 16:17], 2.0).then_inc(s_d, 1)
                dve.wait_ge(s_c1, 2)
                dve.tensor_copy(identb[:, :], ident[:, :]).then_inc(s_d, 1)
                for h in range(4):
                    dve.tensor_copy(xid[0:64, h, :], ident[0:64, 0:64]).then_inc(s_d, 1)
                dve.tensor_copy(iota_e[:, :], iota_i[:, :]).then_inc(s_d, 1)
                dve.wait_ge(s_w, 16 * (12 + 5 + len(rows)))
                dve.tensor_tensor(ew_t[:, :, :], ew_t[:, :, :], mask_sb[:, :, :], ALU.mult).then_inc(s_d, 1)
                dve.tensor_scalar(b8[:, :], beta_sb[:, :], 8.0, None, ALU.mult).then_inc(s_d, 1)
                dve.tensor_tensor(c16[:, :], t_sb[:, :], t_sb[:, :], ALU.mult).then_inc(s_d, 1)
                dve.wait_ge(s_d, 11)
                dve.tensor_scalar(c16[:, :], c16[:, :], 1.0, 16.0, ALU.add, ALU.mult).then_inc(s_d, 1)
                dve.wait_ge(s_d, 12)
                dve.tensor_tensor(c16[:, :], c16[:, :], beta_sb[:, :], ALU.mult).then_inc(s_d, 1)
                dve.wait_ge(s_d, 13)
                dve.tensor_tensor(c16[:, :], c16[:, :], beta_sb[:, :], ALU.mult).then_inc(s_d, 1)

            @block.scalar
            def _(act):
                nc.scalar.preload_act_table_set("natural_log_exp_and_others")
                act.wait_ge(s_d, 14)
                act.activation(ew_t[:, :, :], ew_t[:, :, :], ACT.Exp).then_inc(s_c1, 1)

        names = """kv_full ek_ready ekv_ready q_full eq_ready den_full dn_ready ldn_ready rec_ready num_full yt_ready
            mix_full st0 ag0 lv0 rs0 hn_ready hg_ready h1_ready st1 ag1 lv1 rs1 x1_ready hx0_ready hx_ready
            x1t_full x1t_ready qk_full qk_copied part_h part_r part_m part_l v_full v_ready
            mx_full mx_ready nm_neg nm_h nm_r nm_m nm_r2 mparts_ready mt_full mt_ready
            raw_full z_ready u_dve zb_ready u_pool l_ready g_ready sh_full p_ready
            pv_full f_ready tr_full rc_ready nt_ready fn_ready
            ft_full ft_ready y_full yb_ready st2 ag2 lv2 rs2 yn_ready yw_ready h2_ready st3 ag3 lv3 rs3 x2_ready
            x2t_full x2t_ready lg_full lg_copied lg_kept top_ready idx_ready idxf_ready hot_ready kept
            lc_full locb_ready fill_ready lsel_ready loc_ready over_ready flat_ready flat2_ready slot_ready""".split()
        s = {k: sem(k) for k in names}
        passed = {k: sem(f"passed_{k}") for k in ("sp", "pe", "dve", "pool")}
        x_in = [sem(f"x_in{b}") for b in range(2)]
        qk_out = [sem(f"qk_out{b}") for b in range(2)]
        stack_in = [sem(f"stack_in{b}") for b in range(2)]
        maxrow_in = [sem(f"maxrow_in{b}") for b in range(2)]
        h2_out = [sem(f"h2_out{b}") for b in range(2)]
        x2_out = [sem(f"x2_out{b}") for b in range(2)]
        scat_out = [sem(f"scat_out{b}") for b in range(2)]

        def dyn(n, mul=1):
            return bass.ds(n.before(mul), mul)

        with nc.Block() as block:
            @block.sync
            def _(sp):
                def load_x(n):
                    b = n.par
                    need_alone(sp, passed["sp"], s["mix_full"], n.before(1, -1))
                    sp.dma_start(xb[b][0:64, :], x[dyn(n)].rearrange("a c m -> (a c) m")).then_inc(x_in[b], 16)

                def store_qk(n):
                    need_alone(sp, passed["sp"], s["part_l"], n.before(1, 1))
                    need_alone(sp, passed["sp"], stack_in[n.par], (n + -2).landed(16 * STACK_DMAS) if has(n + -2, nb) else 0)
                    for c in range(2):
                        for part in range(NPART):
                            sp.dma_start(qk_dram[n.par][c, part].rearrange("r (h m) -> h r m", h=8), qkp[:, part, 2 * c:2 * c + 2, :])\
                                .then_inc(qk_out[n.par], 16)

                def load_stacks(n):
                    b = n.par
                    need_alone(sp, passed["sp"], qk_out[b], n.landed(16 * SPLIT_DMAS))
                    need_alone(sp, passed["sp"], s["sh_full"], (n + -1).before(8))
                    for c, (stack, runs) in enumerate(((q_stack[b], RUNS_Q), (k_stack[b], RUNS_K))):
                        row = 0
                        for part, parts, times in runs:
                            src = qk_dram[b][c, part:part + parts].rearrange("a r m -> (a r) m")
                            if times > 1:
                                src = src.rearrange("(t r) m -> t r m", t=1).broadcast_to((times, dh, nh * ltok))
                            width = dh * parts * times
                            sp.dma_start(stack[row:row + width, :, :].rearrange("r h n -> r (h n)"), src).then_inc(stack_in[b], 16)
                            row += width

                def load_maxrow(n):
                    need_alone(sp, passed["sp"], s["mt_ready"], n.before(1, 1))
                    for part in range(NPART):
                        sp.dma_start(q_stack[n.par][SROWS + part:SROWS + part + 1, :, :],
                                     mrow[part * nh:part * nh + nh, :]).then_inc(maxrow_in[n.par], 16)

                def store_h2(n):
                    need_alone(sp, passed["sp"], s["h2_ready"], n.before(1, 1))
                    sp.dma_start(h2_dram[dyn(n)].rearrange("a p l d -> (a p) l d"), h2[n.par][:, :, :]).then_inc(h2_out[n.par], 16)

                def store_x2(n):
                    need_alone(sp, passed["sp"], s["x2_ready"], n.before(2, 2))
                    sp.dma_start(x2_dram[dyn(n)].rearrange("a p l d -> (a p) l d"), x2[n.par][:, :, :]).then_inc(x2_out[n.par], 16)

                def step(i, nb):
                    if has(i + 1, nb):
                        load_stacks(i + 1)
                    if has(i + 4, nb) and i.c + 4 >= 2:
                        load_x(i + 4)
                    if has(i + 2, nb):
                        store_qk(i + 2)
                    if has(i + -1, nb):
                        store_h2(i + -1)
                    if has(i + 1, nb):
                        load_maxrow(i + 1)
                    if has(i + -1, nb):
                        store_x2(i + -1)

                load_x(Batch(0))
                load_x(Batch(1))
                turns(sp, nb, step, ahead=4)
                for sems in (h2_out, x2_out):
                    for b in range(2):
                        sp.wait_ge(sems[b], 16 * (nb // 2))

            @block.tensor
            def _(pe):
                def kv(n, lt):
                    if lt == 0:
                        pe.wait_ge(x_in[n.par], n.landed())
                        need(pe, s["x1t_ready"], n.before(1))
                    else:
                        need(pe, s["ekv_ready"], n.before(2, 1))
                    xv = xb[n.par][:, :].rearrange("c (l h) -> c l h", h=4)
                    for h in range(4):
                        mm = pe.matmul(a_ps[:, h * P:(h + 1) * P], xv[:, lt * P:lt * P + P, h],
                                       wkv_sb[:, :, :].rearrange("c k d -> c (k d)"), start=True, stop=True)
                    mm.then_inc(s["kv_full"], 1)

                def q_tok(n):
                    need(pe, s["ekv_ready"], n.before(2, 2))
                    xv = xb[n.par][:, :].rearrange("c (l h) -> c l h", h=4)
                    for h in range(4):
                        mm = pe.matmul(a_ps[64 * (h % 2):64 * (h % 2) + 64, (h // 2) * 256:(h // 2) * 256 + 256],
                                       wq_sb[:, :], xv[:, :, h], start=True, stop=True)
                    mm.then_inc(s["q_full"], 1)

                def den(n, m):
                    if m == 0:
                        need(pe, s["ek_ready"], n.before(2, 2))
                        need(pe, s["eq_ready"], n.before(1, 1))
                    for st in range(2):
                        mm = pe.matmul(a_ps[:, m * 256:m * 256 + 256], ek[:, st, m * P:m * P + P], ew_t[:, st, :],
                                       start=(st == 0), stop=(st == 1))
                    if m == 1:
                        mm.then_inc(s["den_full"], 1)

                def num(n, m):
                    if m == 0:
                        need(pe, s["ekv_ready"], n.before(2, 2))
                        need(pe, s["dn_ready"], n.before(1, 1))
                    for st in range(2):
                        mm = pe.matmul(a_ps[:, m * 256:m * 256 + 256], ekv[:, st, m * P:m * P + P], ew_t[:, st, :],
                                       start=(st == 0), stop=(st == 1))
                    if m == 1:
                        mm.then_inc(s["num_full"], 1)

                def mix_out(n, lt):
                    if lt == 0:
                        need(pe, s["yt_ready"], n.before(1, 1))
                    xv = xb[n.par][:, :].rearrange("c (l h) -> c l h", h=4)
                    for h in range(4):
                        pe.matmul(a_ps[:, lt * 256 + h * 64:lt * 256 + h * 64 + 64], xv[:, lt * P:lt * P + P, h],
                                  xid[:, h, :], start=(h == 0), stop=False)
                    for m in range(2):
                        mm = pe.matmul(a_ps[:, lt * 256:lt * 256 + 256], y_t[:, m, lt * P:lt * P + P], outw_sb[:, m, :],
                                       start=False, stop=(m == 1))
                    if lt == 1:
                        mm.then_inc(s["mix_full"], 1)

                def transposed(n, src, ps, full):
                    for dk in range(2):
                        for lt in range(2):
                            mm = pe.transpose(ps[:, dk * 256 + lt * P:dk * 256 + lt * P + P], src[:, lt, dk * P:dk * P + P],
                                              ident[:, :])
                    mm.then_inc(s[full], 1)

                def x1_transposed(n):
                    need(pe, s["x1_ready"], n.before(2, 2))
                    transposed(n, x1, a_ps, "x1t_full")

                def project(n, c):
                    if c == 0:
                        need(pe, s["x1t_ready"], n.before(1, 1))
                        if has(n + -4, nb):
                            need(pe, s["lg_copied"], (n + -3).before(1))
                        else:
                            need(pe, s["qk_copied"], n.before(4))
                    else:
                        need(pe, s["qk_copied"], n.before(4, 2))
                    w = (wqa, wka)[c]
                    for m in range(2):
                        for dk in range(2):
                            mm = pe.matmul(t_ps[:, m * 256:m * 256 + 256], w[:, dk, m * P:m * P + P], x1_t[n.par][:, dk, :],
                                           start=(dk == 0), stop=(dk == 1))
                    mm.then_inc(s["qk_full"], 1)

                def project_v(n):
                    need(pe, s["mt_ready"], n.before(1))
                    for lt in range(2):
                        for dk in range(2):
                            mm = pe.matmul(b_ps[:, lt * 256:lt * 256 + 256], x1_t[n.par][:, dk, lt * P:lt * P + P], wva[:, dk, :],
                                           start=(dk == 0), stop=(dk == 1))
                    mm.then_inc(s["v_full"], 1)

                def max_scores(n, h):
                    b = n.par
                    if h == 0:
                        pe.wait_ge(stack_in[b], n.landed(16 * STACK_DMAS))
                        need(pe, s["v_ready"], n.before(1, 1))
                    else:
                        need(pe, s["mx_ready"], n.before(nh, h))
                    for lt in range(2):
                        mm = pe.matmul(b_ps[:, lt * 256:lt * 256 + 256], q_stack[b][0:SROWS, slot(h), lt * P:lt * P + P],
                                       k_stack[b][0:SROWS, slot(h), :], start=True, stop=True)
                    mm.then_inc(s["mx_full"], 1)

                def max_transposed(n):
                    need_alone(pe, passed["pe"], s["mparts_ready"], n.before(1, 1))
                    for lt in range(2):
                        mm = pe.transpose(b_bf[0:NPART * nh, lt * P:lt * P + P],
                                          mparts[:, lt, :, :].rearrange("p a h -> p (a h)"), identb[:, :])
                    mm.then_inc(s["mt_full"], 1)

                def scores(n, pair, ps, nrows, bank_sem, full):
                    b = n.par
                    need(pe, s[bank_sem], n.before(8, pair))
                    if nrows > SROWS and pair == 0:
                        pe.wait_ge(maxrow_in[b], n.landed(16 * NPART))
                    if nrows == SROWS and pair == 0:
                        pe.wait_ge(stack_in[b], n.landed(16 * STACK_DMAS))
                    for j in range(2):
                        for mt in range(2):
                            mm = pe.matmul(ps[:, j, mt, :], k_stack[b][0:nrows, slot(2 * pair + j), mt * P:mt * P + P],
                                           q_stack[b][0:nrows, slot(2 * pair + j), :], start=True, stop=True)
                    mm.then_inc(s[full], 1)

                def weighted(n, t, kind):
                    if kind == 0:
                        need(pe, s["p_ready"], n.before(8, 2 * t + 2))
                        need(pe, s["v_ready"], n.before(1, 1))
                        need(pe, s["nt_ready"], n.before(4, t))
                    else:
                        need(pe, s["g_ready"], n.before(8, 2 * t + 2))
                    w = (p_sb, g_sb)[kind][t % 2]
                    for mt in range(2):
                        for q in range(4):
                            mm = pe.matmul(pv_ps[32 * q:32 * q + 32, kind * 256:kind * 256 + 256],
                                           v_sb[n.par][:, mt, 4 * t + q, :], w[:, q, mt, :],
                                           start=(mt == 0), stop=(mt == 1))
                    if kind == 1:
                        mm.then_inc(s["pv_full"], 1)

                def weighted_transposed(n, t):
                    need(pe, s["f_ready"], n.before(4, t + 1))
                    for lt in range(2):
                        for kind in range(2):
                            mm = pe.transpose(pv_ps[:, (lt * 2 + kind) * P:(lt * 2 + kind) * P + P],
                                              f_sb[:, kind * 256 + lt * P:kind * 256 + lt * P + P], ident[:, :])
                    mm.then_inc(s["tr_full"], 1)

                def f_transposed(n):
                    need(pe, s["fn_ready"], n.before(4, 4))
                    if has(n + -1, nb):
                        need(pe, s["locb_ready"], n.before(1))
                        need(pe, s["fill_ready"], n.before(1))
                    else:
                        need(pe, s["qk_copied"], (n + 3).before(4, 4))
                    transposed(n, f_n, t_ps, "ft_full")

                def y_proj(n, lt):
                    if lt == 0:
                        need(pe, s["ft_ready"], n.before(1, 1))
                    for dk in range(2):
                        mm = pe.matmul(t_ps[:, lt * 256:lt * 256 + 256], f_t[:, dk, lt * P:lt * P + P], woa[:, dk, :],
                                       start=(dk == 0), stop=(dk == 1))
                    if lt == 1:
                        mm.then_inc(s["y_full"], 1)

                def x2_transposed(n):
                    need(pe, s["x2_ready"], n.before(2, 2))
                    transposed(n, x2[n.par], t_ps, "x2t_full")

                def logits(n):
                    need(pe, s["x2t_ready"], n.before(1, 1))
                    for lt in range(2):
                        for dk in range(2):
                            mm = pe.matmul(t_ps[:, lt * ne:lt * ne + ne], x2_t[:, dk, lt * P:lt * P + P], wg_sb[:, dk, :],
                                           start=(dk == 0), stop=(dk == 1))
                    mm.then_inc(s["lg_full"], 1)

                def positions(n):
                    need(pe, s["hot_ready"], n.before(1, 1))
                    if has(n + 4, nb):
                        need(pe, s["qk_copied"], (n + 4).before(4, 4))
                    c = 2 * ne
                    h0 = hot[:, 0, :, :].rearrange("p c e -> p (c e)")
                    h1_ = hot[:, 1, :, :].rearrange("p c e -> p (c e)")
                    pe.matmul(t_ps[:, 0:c], before_b[:, :], h0, start=True, stop=True)
                    pe.matmul(t_ps[:, c:2 * c], before_b[:, :], h1_, start=True, stop=False)
                    pe.matmul(t_ps[:, c:2 * c], ones_b[:, :], h0, start=False, stop=True)
                    pe.matmul(t_ps[:, 2 * c:3 * c], ones_b[:, :], h0, start=True, stop=False)
                    pe.matmul(t_ps[:, 2 * c:3 * c], ones_b[:, :], h1_, start=False, stop=True).then_inc(s["lc_full"], 1)

                def step(i, nb):
                    A, B, X, M, C, D = (has(i + d, nb) for d in (3, 2, 1, 0, -1, -2))

                    def maxima(*heads):
                        for h in heads:
                            if X:
                                max_scores(i + 1, h)

                    def raw(pair):
                        if M:
                            scores(i, pair, raw_ps, SROWS, "z_ready", "raw_full")

                    def shifted(pair):
                        if M:
                            scores(i, pair, sh_ps, SROWS + NPART, "p_ready", "sh_full")

                    def on(there, d, what, *args):
                        if there:
                            what(i + d, *args)

                    raw(0)
                    on(X, 1, project_v)
                    shifted(0)
                    on(C, -1, weighted_transposed, 2)
                    on(D, -2, x2_transposed)
                    on(B, 2, x1_transposed)

                    raw(1)
                    on(D, -2, logits)
                    on(A, 3, kv, 0)
                    shifted(1)
                    on(B, 2, project, 0)
                    on(C, -1, weighted, 3, 0)
                    on(C, -1, weighted, 3, 1)

                    raw(2)
                    on(A, 3, kv, 1)
                    on(B, 2, project, 1)
                    shifted(2)
                    on(C, -1, weighted_transposed, 3)
                    maxima(0)
                    on(A, 3, q_tok)
                    maxima(1)

                    raw(3)
                    on(A, 3, den, 0)
                    maxima(2)
                    on(A, 3, den, 1)
                    shifted(3)
                    maxima(3)
                    on(M, 0, weighted, 0, 0)
                    maxima(4)
                    on(M, 0, weighted, 0, 1)
                    on(D, -2, positions)
                    maxima(5)

                    raw(4)
                    on(C, -1, f_transposed)
                    on(A, 3, num, 0)
                    maxima(6)
                    on(A, 3, num, 1)
                    shifted(4)
                    maxima(7)
                    on(M, 0, weighted_transposed, 0)
                    on(C, -1, y_proj, 0)
                    maxima(8)
                    on(C, -1, y_proj, 1)

                    raw(5)
                    maxima(9)
                    on(A, 3, mix_out, 0)
                    maxima(10)
                    shifted(5)
                    on(A, 3, mix_out, 1)
                    maxima(11)
                    on(M, 0, weighted, 1, 0)
                    maxima(12)
                    on(M, 0, weighted, 1, 1)

                    raw(6)
                    maxima(13)
                    shifted(6)
                    on(M, 0, weighted_transposed, 1)
                    maxima(14, 15)

                    raw(7)
                    on(X, 1, max_transposed)
                    shifted(7)
                    on(M, 0, weighted, 2, 0)
                    on(M, 0, weighted, 2, 1)

                turns(pe, nb, step)

            @block.scalar
            def _(act):
                def ek_tile(n, lt):
                    need(act, s["kv_full"], n.before(2, lt + 1))
                    if lt == 0:
                        need(act, s["den_full"], n.before(1))
                    kvv = a_ps[:, :].rearrange("p (h k d) -> p h k d", h=4, k=2)
                    act.activation(ek[:, lt, :].rearrange("p (h d) -> p h d", h=4), kvv[:, :, 0, :], ACT.Exp)\
                        .then_inc(s["ek_ready"], 1)

                def exp_minus_q(n):
                    need(act, s["q_full"], n.before(1, 1))
                    need(act, s["dn_ready"], n.before(1))
                    act.activation(eq[:, :, :].rearrange("p m t -> p (m t)"), a_ps[:, :], ACT.Exp, scale=-1.0)\
                        .then_inc(s["eq_ready"], 1)

                def rsqrt(n, k, used, per):
                    need(act, s[f"ag{k}"], n.before(2, 2))
                    act.activation(lnv[k][:, :], mv[k][:, :, 1], ACT.Ln, bias=eps[:, 0:1]).then_inc(s[f"lv{k}"], 1)
                    need(act, s[f"lv{k}"], n.before(1, 1))
                    need(act, s[used], n.before(per))
                    act.activation(rs[k][:, :], lnv[k][:, :], ACT.Exp, scale=-0.5).then_inc(s[f"rs{k}"], 1)

                def copy_out(n, ps, dst, full, ready, used):
                    need(act, s[full], n.before(1, 1))
                    for sem_name, back in used:
                        need(act, s[sem_name], (n + back).before(1))
                    act.activation(dst[:, :, :].rearrange("p a n -> p (a n)"), ps[:, :], ACT.Copy).then_inc(s[ready], 1)

                def reciprocal(n):
                    need(act, s["dn_ready"], n.before(1, 1))
                    act.activation(dn[:, :, :], dn[:, :, :], ACT.Ln).then_inc(s["ldn_ready"], 1)
                    need(act, s["ldn_ready"], n.before(1, 1))
                    need(act, s["yt_ready"], n.before(1))
                    act.activation(rec[:, :, :], dn[:, :, :], ACT.Exp, scale=-1.0).then_inc(s["rec_ready"], 1)

                def qk_bias(n, c):
                    need(act, s["qk_full"], n.before(2, c + 1))
                    if c == 0:
                        need(act, s["part_h"], n.before(1))
                        need(act, s["part_r"], n.before(1))
                    for m in range(2):
                        act.activation(qkf[:, 2 * c + m, :], t_ps[:, m * 256:m * 256 + 256], ACT.Identity,
                                       bias=bqk[:, 2 * c + m:2 * c + m + 1]).then_inc(s["qk_copied"], 1)

                def maxrow_copy(n):
                    need(act, s["mt_full"], n.before(1, 1))
                    if has(n + -1, nb):
                        act.wait_ge(maxrow_in[(n.par + 1) % 2], (n + -1).landed(16 * NPART))
                    act.activation(mrow[:, :], b_bf[0:NPART * nh, 0:ltok], ACT.Copy).then_inc(s["mt_ready"], 1)

                def softmax_weights(n, pair):
                    need(act, s["sh_full"], n.before(8, pair + 1))
                    if pair % 2 == 0:
                        need(act, s["pv_full"], n.before(4, pair // 2 - 1))
                    dst = p_sb[(pair // 2) % 2][:, 2 * (pair % 2):2 * (pair % 2) + 2, :, :]
                    act.activation(dst.rearrange("p j m n -> p (j m n)"), sh_ps[:, :, :, :].rearrange("p j m n -> p (j m n)"),
                                   ACT.Exp, scale=SC).then_inc(s["p_ready"], 1)

                def cauchy_weights(n, pair):
                    b = pair % 2
                    for j, ready in enumerate(("u_dve", "u_pool")):
                        need(act, s[ready], n.before(8, pair + 1))
                        h = 2 * pair + j
                        act.activation(u_sb[b][:, j, :], u_sb[b][:, j, :], ACT.Ln, bias=c16[:, h:h + 1])\
                            .then_inc(s["l_ready"], 1)
                    need(act, s["l_ready"], n.before(16, 2 * pair + 2))
                    if pair % 2 == 0:
                        need(act, s["pv_full"], n.before(4, pair // 2 - 1))
                    dst = g_sb[(pair // 2) % 2][:, 2 * (pair % 2):2 * (pair % 2) + 2, :, :]
                    act.activation(dst.rearrange("p j m n -> p (j m n)"), u_sb[b][:, :, :].rearrange("p j n -> p (j n)"),
                                   ACT.Exp, scale=-1.0).then_inc(s["g_ready"], 1)

                def weighted_copy(n, t):
                    need(act, s["pv_full"], n.before(4, t + 1))
                    need(act, s["tr_full"], n.before(4, t))
                    act.activation(f_sb[:, :], pv_ps[:, :], ACT.Copy).then_inc(s["f_ready"], 1)

                def step(i, nb):
                    A, B, X, M, C, D = (has(i + d, nb) for d in (3, 2, 1, 0, -1, -2))

                    def on(there, d, what, *args):
                        if there:
                            what(i + d, *args)

                    on(C, -1, cauchy_weights, 7)
                    on(M, 0, softmax_weights, 0)
                    if D:
                        copy_out(i + -2, t_ps, x2_t, "x2t_full", "x2t_ready", (("lg_full", 0),))
                    if B:
                        copy_out(i + 2, a_ps, x1_t[i.par], "x1t_full", "x1t_ready", (("v_full", -1),))

                    on(A, 3, ek_tile, 0)
                    on(M, 0, softmax_weights, 1)
                    on(M, 0, cauchy_weights, 0)
                    on(B, 2, qk_bias, 0)
                    on(C, -1, weighted_copy, 3)

                    on(A, 3, ek_tile, 1)
                    on(M, 0, cauchy_weights, 1)
                    on(B, 2, qk_bias, 1)
                    on(M, 0, softmax_weights, 2)
                    on(A, 3, exp_minus_q)

                    on(M, 0, softmax_weights, 3)
                    on(M, 0, cauchy_weights, 2)
                    on(A, 3, reciprocal)
                    on(M, 0, weighted_copy, 0)

                    if C:
                        copy_out(i + -1, t_ps, f_t, "ft_full", "ft_ready", (("y_full", 0),))
                    on(M, 0, softmax_weights, 4)
                    on(M, 0, cauchy_weights, 3)

                    on(M, 0, softmax_weights, 5)
                    on(C, -1, rsqrt, 2, "yn_ready", 2)
                    on(M, 0, cauchy_weights, 4)
                    on(M, 0, weighted_copy, 1)

                    on(M, 0, softmax_weights, 6)
                    on(A, 3, rsqrt, 0, "hn_ready", 2)
                    on(M, 0, cauchy_weights, 5)

                    on(X, 1, maxrow_copy)
                    on(M, 0, softmax_weights, 7)
                    on(C, -1, rsqrt, 3, "x2_ready", 2)
                    on(M, 0, cauchy_weights, 6)
                    on(A, 3, rsqrt, 1, "x1_ready", 2)
                    on(M, 0, weighted_copy, 2)

                nc.scalar.preload_act_table_set("natural_log_exp_and_others")
                turns(act, nb, step)

            @block.vector
            def _(dve):
                def ekv_tile(n, lt):
                    need(dve, s["ek_ready"], n.before(2, lt + 1))
                    if lt == 0:
                        need(dve, s["num_full"], n.before(1))
                    kvv = a_ps[:, :].rearrange("p (h k d) -> p h k d", h=4, k=2)
                    dve.tensor_tensor(ekv[:, lt, :].rearrange("p (h d) -> p h d", h=4), kvv[:, :, 1, :],
                                      ek[:, lt, :].rearrange("p (h d) -> p h d", h=4), ALU.mult).then_inc(s["ekv_ready"], 1)

                def fold(t):
                    return t[:, :, :].rearrange("p a n -> p (a n)")

                def denominators(n):
                    need(dve, s["den_full"], n.before(1, 1))
                    need(dve, s["rec_ready"], n.before(1))
                    dve.scalar_tensor_tensor(out=fold(dn), in0=fold(eq), scalar=1.0, in1=a_ps[:, :],
                                             op0=ALU.add, op1=ALU.mult).then_inc(s["dn_ready"], 1)

                def mixed_values(n):
                    need(dve, s["rec_ready"], n.before(1, 1))
                    need(dve, s["num_full"], n.before(1, 1))
                    need(dve, s["mix_full"], n.before(1))
                    dve.tensor_tensor(fold(y_t), a_ps[:, :], fold(rec), ALU.mult).then_inc(s["yt_ready"], 1)

                def stats(n, k, src, ready, per, incs):
                    need(dve, s[ready], n.before(per, incs))
                    for lt in range(2):
                        dve.bn_stats(stat[k][:, lt, :], src(lt)).then_inc(s[f"st{k}"], 1)
                    need(dve, s[f"lv{k}"], n.before(1))
                    for lt in range(2):
                        need_alone(dve, passed["dve"], s[f"st{k}"], n.before(2, lt + 1))
                        dve.bn_aggr(mv[k][:, lt, :], stat[k][:, lt, :]).then_inc(s[f"ag{k}"], 1)

                def normalise(n, k, src, dst, ready, used):
                    need(dve, s[f"rs{k}"], n.before(1, 1))
                    for f in used:
                        need(dve, s[f], n.before(1))
                    for lt in range(2):
                        dve.tensor_scalar(dst[:, lt, :], src(lt), mv[k][:, lt, 0:1], rs[k][:, lt:lt + 1],
                                          ALU.subtract, ALU.mult).then_inc(s[ready], 1)

                def a_half(lt):
                    return a_ps[:, lt * 256:lt * 256 + 256]

                def part_high(n):
                    need(dve, s["qk_copied"], n.before(4, 4))
                    if has(n + -1, nb):
                        dve.wait_ge(qk_out[(n.par + 1) % 2], (n + -1).landed(16 * SPLIT_DMAS))
                    dve.tensor_copy(qkp[:, 0, :, :], qkf[:, :, :]).then_inc(s["part_h"], 1)

                def part_mid(n):
                    need(dve, s["part_r"], n.before(1, 1))
                    dve.tensor_copy(qkp[:, 1, :, :], qkr[:, :, :]).then_inc(s["part_m"], 1)

                def v_bias(n):
                    need(dve, s["v_full"], n.before(1, 1))
                    need(dve, s["pv_full"], (n + -1).before(4))
                    for_v = rows["bv"][:, :].rearrange("p (a h d) -> p a h d", a=1, d=dh).broadcast_to((P, 2, nh, dh))
                    dve.tensor_tensor(v_sb[n.par][:, :, :, 0:dh], b_ps[:, :].rearrange("p (l h d) -> p l h d", l=2, d=dh),
                                      for_v, ALU.add).then_inc(s["v_ready"], 1)

                def head_max(n, h):
                    need(dve, s["mx_full"], n.before(nh, h + 1))
                    if h == 0:
                        need(dve, s["nm_neg"], n.before(1))
                    dve.tensor_reduce(rmax[:, slot(h), :], b_ps[:, :].rearrange("p (l m) -> p l m", l=2), AX, ALU.max)\
                        .then_inc(s["mx_ready"], 1)

                def max_parts(n):
                    def part(k):
                        return mparts[:, :, k, :].rearrange("p l h -> p h l")
                    need(dve, s["mx_ready"], n.before(nh, nh))
                    need(dve, s["mparts_ready"], n.before(1))
                    dve.tensor_scalar(nmx[:, :, :], rmax[:, :, :], -1.0, None, ALU.mult).then_inc(s["nm_neg"], 1)
                    need(dve, s["nm_neg"], n.before(1, 1))
                    need(dve, s["mt_full"], n.before(1))
                    dve.tensor_copy(part(0), nmx[:, :, :]).then_inc(s["nm_h"], 1)
                    need(dve, s["nm_h"], n.before(1, 1))
                    dve.tensor_tensor(nmr[:, :, :], nmx[:, :, :], part(0), ALU.subtract).then_inc(s["nm_r"], 1)
                    need(dve, s["nm_r"], n.before(1, 1))
                    dve.tensor_copy(part(1), nmr[:, :, :]).then_inc(s["nm_m"], 1)
                    need(dve, s["nm_m"], n.before(1, 1))
                    dve.tensor_tensor(part(2), nmr[:, :, :], part(1), ALU.subtract).then_inc(s["mparts_ready"], 1)

                def magnitudes(n, pair):
                    b = pair % 2
                    need(dve, s["raw_full"], n.before(8, pair + 1))
                    need(dve, s["u_dve"], n.before(8, pair - 1))
                    need(dve, s["u_pool"], n.before(8, pair - 1))
                    dve.tensor_scalar(z_sb[b][:, :, :].rearrange("p j n -> p (j n)").bitcast(I32),
                                      raw_ps[:, :, :, :].rearrange("p j m n -> p (j m n)").bitcast(I32),
                                      0x7FFFFFFF, None, ALU.bitwise_and).then_inc(s["z_ready"], 1)

                def polynomial(n, pair):
                    b, h = pair % 2, 2 * pair
                    need(dve, s["z_ready"], n.before(8, pair + 1))
                    need(dve, s["g_ready"], n.before(8, pair - 1))
                    dve.scalar_tensor_tensor(out=u_sb[b][:, 0, :], in0=z_sb[b][:, 0, :], scalar=b8[:, h:h + 1],
                                             in1=z_sb[b][:, 0, :], op0=ALU.add, op1=ALU.mult).then_inc(s["u_dve"], 1)

                def norm_quad(n, t):
                    need(dve, s["tr_full"], n.before(4, t + 1))
                    need(dve, s["nt_ready"], n.before(4, t))
                    v = pv_ps[:, :].rearrange("p (g d) -> p g d", d=VW)
                    dve.reciprocal(rc[:, :], v[:, :, dh]).then_inc(s["rc_ready"], 1)
                    need(dve, s["rc_ready"], n.before(4, t + 1))
                    need(dve, s["fn_ready"], n.before(4, t))
                    dve.tensor_tensor(ntv[:, :, :, :, :].rearrange("p l k h d -> p (l k h) d"), v[:, :, 0:dh],
                                      rc[:, :].rearrange("p (g a) -> p g a", a=1).broadcast_to((P, 16, dh)), ALU.mult)\
                        .then_inc(s["nt_ready"], 1)
                    need(dve, s["nt_ready"], n.before(4, t + 1))
                    if t == 0:
                        need(dve, s["ft_full"], n.before(1))
                    nv = ntv[:, :, :, :, :].rearrange("p l k h d -> p l k (h d)")
                    dve.tensor_tensor(f_n[:, :, t * 64:t * 64 + 64], nv[:, :, 0, :], nv[:, :, 1, :], ALU.add)\
                        .then_inc(s["fn_ready"], 1)

                def y_bias(n):
                    need(dve, s["y_full"], n.before(1, 1))
                    dve.tensor_tensor(yb[:, :, :], t_ps[:, :].rearrange("p (l d) -> p l d", l=2),
                                      rows["bo"][:, :].rearrange("p (a d) -> p a d", a=1).broadcast_to((P, 2, dm)), ALU.add)\
                        .then_inc(s["yb_ready"], 1)

                def choose(n):
                    need(dve, s["lg_full"], n.before(1, 1))
                    dve.tensor_copy(fold(lgt), t_ps[:, 0:2 * ne]).then_inc(s["lg_copied"], 1)
                    need(dve, s["lg_copied"], n.before(1, 1))
                    dve.tensor_copy(logits_all[:, dyn(n, 2), :], lgt[:, :, :]).then_inc(s["lg_kept"], 1)
                    for lt in range(2):
                        need_alone(dve, passed["dve"], s["idx_ready"], n.before(2))
                        dve.max(top8[:, lt, :], lgt[:, lt, :]).then_inc(s["top_ready"], 1)
                    for lt in range(2):
                        need_alone(dve, passed["dve"], s["top_ready"], n.before(2, lt + 1))
                        dve.max_index(idx8[:, lt, :], top8[:, lt, :], lgt[:, lt, :]).then_inc(s["idx_ready"], 1)
                    need(dve, s["idx_ready"], n.before(2, 2))
                    dve.tensor_copy(top_all[:, dyn(n, 2), :], top8[:, :, 0:2]).then_inc(s["kept"], 1)
                    dve.tensor_copy(idxf[:, :, :], idx8[:, :, 0:2]).then_inc(s["idxf_ready"], 1)
                    need(dve, s["idxf_ready"], n.before(1, 1))
                    dve.tensor_copy(expert_all[:, dyn(n, 2), :], idxf[:, :, :]).then_inc(s["kept"], 1)
                    dve.tensor_tensor(hot[:, :, :, :].rearrange("p l c e -> p (l c) e"),
                                      idxf[:, :, :].rearrange("p l (c a) -> p (l c) a", a=1).broadcast_to((P, 4, ne)),
                                      iota_e[:, :].rearrange("p (a e) -> p a e", a=1).broadcast_to((P, 4, ne)), ALU.is_equal)\
                        .then_inc(s["hot_ready"], 1)

                def place(n):
                    b, c = n.par, 2 * ne
                    need(dve, s["lc_full"], n.before(1, 1))
                    need(dve, s["fill_ready"], n.before(1))
                    run = filled[:, b, :, :].rearrange("p c e -> p (c e)")
                    dve.tensor_tensor(locb[:, :, :, :].rearrange("p l c e -> p l (c e)"),
                                      t_ps[:, 0:2 * c].rearrange("p (l k) -> p l k", l=2),
                                      run.rearrange("p (a k) -> p a k", a=1).broadcast_to((P, 2, c)), ALU.add)\
                        .then_inc(s["locb_ready"], 1)
                    dve.tensor_tensor(filled[:, 1 - b, :, :].rearrange("p c e -> p (c e)"), t_ps[:, 2 * c:3 * c], run, ALU.add)\
                        .then_inc(s["fill_ready"], 1)
                    need(dve, s["locb_ready"], n.before(1, 1))
                    dve.tensor_tensor(lsel[:, :, :, :].rearrange("p l c e -> p (l c e)"),
                                      locb[:, :, :, :].rearrange("p l c e -> p (l c e)"),
                                      hot[:, :, :, :].rearrange("p l c e -> p (l c e)"), ALU.mult).then_inc(s["lsel_ready"], 1)
                    need(dve, s["lsel_ready"], n.before(1, 1))
                    dve.tensor_reduce(loc[:, :, :].rearrange("p l c -> p (l c)"),
                                      lsel[:, :, :, :].rearrange("p l c e -> p (l c) e"), AX, ALU.add).then_inc(s["loc_ready"], 1)
                    need(dve, s["loc_ready"], n.before(1, 1))
                    dve.tensor_copy(place_all[:, dyn(n, 2), :], loc[:, :, :]).then_inc(s["kept"], 1)
                    dve.tensor_scalar(fold(over), fold(loc), float(cap), float(4 * ne * cap), ALU.is_ge, ALU.mult)\
                        .then_inc(s["over_ready"], 1)
                    dve.scalar_tensor_tensor(out=fold(flat), in0=fold(idxf), scalar=float(2 * cap), in1=fold(loc),
                                             op0=ALU.mult, op1=ALU.add).then_inc(s["flat_ready"], 1)
                    need(dve, s["over_ready"], n.before(1, 1))
                    need(dve, s["flat_ready"], n.before(1, 1))
                    dve.tensor_tensor(fold(flat2), fold(flat), fold(over), ALU.add).then_inc(s["flat2_ready"], 1)
                    need(dve, s["flat2_ready"], n.before(1, 1))
                    if has(n + -2, nb):
                        dve.wait_ge(scat_out[b], (n + -2).landed(64))
                    dve.tensor_copy(slot_u[b][:, :], fold(flat2)).then_inc(s["slot_ready"], 1)
                    dve.tensor_copy(tok_u[b][:, :], tok_ids[:, dyn(n, 2)]).then_inc(s["slot_ready"], 1)

                def step(i, nb):
                    A, B, X, M, C, D = (has(i + d, nb) for d in (3, 2, 1, 0, -1, -2))
                    last = (i.par + 1) % 2

                    def maxima(*heads):
                        for h in heads:
                            if X:
                                head_max(i + 1, h)

                    def on(there, d, what, *args):
                        if there:
                            what(i + d, *args)

                    on(M, 0, magnitudes, 0)
                    on(M, 0, polynomial, 0)
                    on(C, -1, norm_quad, 2)

                    on(M, 0, magnitudes, 1)
                    on(A, 3, ekv_tile, 0)
                    on(M, 0, polynomial, 1)
                    on(D, -2, choose)

                    on(M, 0, magnitudes, 2)
                    on(A, 3, ekv_tile, 1)
                    on(M, 0, polynomial, 2)
                    on(X, 1, v_bias)
                    on(B, 2, part_high)
                    on(C, -1, norm_quad, 3)
                    maxima(0, 1)

                    on(M, 0, magnitudes, 3)
                    maxima(2)
                    on(A, 3, denominators)
                    maxima(3)
                    on(M, 0, polynomial, 3)
                    maxima(4)
                    on(B, 2, part_mid)
                    on(D, -2, place)
                    maxima(5)

                    on(M, 0, magnitudes, 4)
                    maxima(6)
                    on(M, 0, polynomial, 4)
                    maxima(7)
                    on(A, 3, mixed_values)
                    on(M, 0, norm_quad, 0)
                    maxima(8)

                    on(M, 0, magnitudes, 5)
                    maxima(9)
                    if C:
                        y_bias(i + -1)
                    maxima(10)
                    if C:
                        stats(i + -1, 2, lambda lt: yb[:, lt, :], "yb_ready", 1, 1)
                    on(M, 0, polynomial, 5)
                    maxima(11)
                    on(A, 3, stats, 0, a_half, "mix_full", 1, 1)
                    maxima(12)
                    if C:
                        normalise(i + -1, 2, lambda lt: yb[:, lt, :], yn, "yn_ready", ("yw_ready",))

                    on(M, 0, magnitudes, 6)
                    maxima(13)
                    on(A, 3, normalise, 0, a_half, hn, "hn_ready", ("hg_ready",))
                    on(M, 0, polynomial, 6)
                    maxima(14)
                    on(M, 0, norm_quad, 1)
                    maxima(15)
                    on(X, 1, max_parts)

                    on(M, 0, magnitudes, 7)
                    on(M, 0, polynomial, 7)
                    if C:
                        stats(i + -1, 3, lambda lt: h2[last][:, lt, :], "h2_ready", 1, 1)
                        if has(i + -3, nb):
                            dve.wait_ge(x2_out[last], (i + -3).landed())
                        normalise(i + -1, 3, lambda lt: h2[last][:, lt, :], x2[last], "x2_ready", ("x2t_full",))
                    if A:
                        stats(i + 3, 1, lambda lt: h1[:, lt, :], "h1_ready", 1, 1)
                        normalise(i + 3, 1, lambda lt: h1[:, lt, :], x1, "x1_ready", ("hx0_ready", "x1t_full"))

                turns(dve, nb, step)

            @block.gpsimd
            def _(pool):
                def over_rows(dst, a, row):
                    r = rows[row][:, :].rearrange("p (a d) -> p a d", a=1).broadcast_to((P, 2, dm))
                    return a[:, :, :], r

                def scale_row(n, dst, src, row, op, ready, per, k, done, free=()):
                    need_alone(pool, passed["pool"], s[ready], n.before(per, k))
                    for f in free:
                        need_alone(pool, passed["pool"], s[f], n.before(1))
                    a, r = over_rows(dst, src, row)
                    pool.tensor_tensor(dst[:, :, :], a, r, op).then_inc(s[done], 1)

                def sum_rows(n, dst, a, b_, done):
                    pool.tensor_tensor(dst[:, :, :], a[:, :, :], b_[:, :, :], ALU.add).then_inc(s[done], 1)

                def mixer_norm(n):
                    scale_row(n, hg, hn, "ln_g", ALU.mult, "hn_ready", 2, 2, "hg_ready", ("h1_ready",))
                    need_alone(pool, passed["pool"], s["x1_ready"], n.before(2))
                    scale_row(n, h1, hg, "ln_b", ALU.add, "hg_ready", 1, 1, "h1_ready", ("hx0_ready",))

                def residual(n, b):
                    need_alone(pool, passed["pool"], s["x1_ready"], n.before(2, 2))
                    need_alone(pool, passed["pool"], s["hx_ready"], n.before(1))
                    sum_rows(n, hx0, h1, x1, "hx0_ready")
                    need_alone(pool, passed["pool"], s["h2_ready"], (n + -3).before(1) if has(n + -4, nb) else 0)
                    scale_row(n, hx[b], hx0, "ln_b2", ALU.add, "hx0_ready", 1, 1, "hx_ready")

                def remainder(n):
                    need_alone(pool, passed["pool"], s["part_h"], n.before(1, 1))
                    need_alone(pool, passed["pool"], s["part_l"], n.before(1))
                    pool.tensor_tensor(qkr[:, :, :], qkf[:, :, :], qkp[:, 0, :, :], ALU.subtract).then_inc(s["part_r"], 1)

                def part_low(n):
                    need_alone(pool, passed["pool"], s["part_m"], n.before(1, 1))
                    if has(n + -1, nb):
                        need_alone(pool, passed["pool"], qk_out[(n.par + 1) % 2], (n + -1).landed(16 * SPLIT_DMAS))
                    pool.tensor_tensor(qkp[:, 2, :, :], qkr[:, :, :], qkp[:, 1, :, :], ALU.subtract).then_inc(s["part_l"], 1)

                def polynomial(n, pair):
                    b, h = pair % 2, 2 * pair + 1
                    need_alone(pool, passed["pool"], s["z_ready"], n.before(8, pair + 1))
                    need_alone(pool, passed["pool"], s["u_pool"], n.before(8, pair))
                    pool.tensor_tensor(zb[:, :], z_sb[b][:, 1, :], b8[:, h:h + 1].broadcast_to((P, 512)), ALU.add)\
                        .then_inc(s["zb_ready"], 1)
                    need_alone(pool, passed["pool"], s["zb_ready"], n.before(8, pair + 1))
                    need_alone(pool, passed["pool"], s["g_ready"], n.before(8, pair - 1))
                    pool.tensor_tensor(u_sb[b][:, 1, :], zb[:, :], z_sb[b][:, 1, :], ALU.mult).then_inc(s["u_pool"], 1)

                def attention_norm(n, b):
                    scale_row(n, yw, yn, "ln_w", ALU.mult, "yn_ready", 2, 2, "yw_ready", ("h2_ready",))
                    need_alone(pool, passed["pool"], s["yw_ready"], n.before(1, 1))
                    need_alone(pool, passed["pool"], s["x2_ready"], (n + -1).before(2) if has(n + -2, nb) else 0)
                    if has(n + -2, nb):
                        need_alone(pool, passed["pool"], h2_out[n.par], (n + -2).landed())
                    sum_rows(n, h2[n.par], yw, hx[b], "h2_ready")

                def scatter(n):
                    b = n.par
                    need_alone(pool, passed["pool"], s["slot_ready"], n.before(2, 2))
                    for lt in range(2):
                        for c in range(2):
                            pool.indirect_dma_start(
                                out=slot_dram[c], out_offset=bass.IndirectOffsetOnAxis(ap=slot_u[b][:, 2 * lt + c:2 * lt + c + 1], axis=0),
                                in_=tok_u[b][:, lt:lt + 1], in_offset=None,
                                bounds_check=2 * ne * cap - 1, oob_is_err=False).then_inc(scat_out[b], 16)

                def step4(i, nb, ring):
                    A, B, M, C, D = (has(i + d, nb) for d in (3, 2, 0, -1, -2))
                    for pair in range(nh // 2):
                        if M:
                            polynomial(i, pair)
                        if pair == 0 and B:
                            residual(i + 2, (ring + 2) % 4)
                        if pair == 2 and B:
                            remainder(i + 2)
                        if pair == 3 and D:
                            scatter(i + -2)
                        if pair == 4 and B:
                            part_low(i + 2)
                        if pair == 5 and C:
                            attention_norm(i + -1, (ring + 3) % 4)
                        if pair == 6 and A:
                            mixer_norm(i + 3)

                pool_turns(pool, nb, step4)
                for b in range(2):
                    pool.wait_ge(scat_out[b], 64 * (nb // 2))


def finish_routes(nc, g):
    ne, cap, tiles = g["ne"], g["cap"], g["tiles"]
    filled, iota_e = g["filled"], g["iota_e"]
    logits_all, top_all, expert_all, place_all = (g[k] for k in ("logits_all", "top_all", "expert_all", "place_all"))
    routes, gates, slot_tok, slot_dram = g["routes"], g["gates"], g["slot_tok"], g["slot_dram"]
    with ExitStack() as ctx:
        def sb(name, shape, dt=F32):
            return ctx.enter_context(nc.sbuf_tensor(name, shape, dt))

        def sem(name):
            return ctx.enter_context(nc.semaphore(name))

        big = [sb(f"big{b}", [P, tiles, ne]) for b in range(2)]
        soft = sb("soft", [P, tiles, ne])
        n1f = sb("n1f", [P, ne])
        n1i = sb("n1i", [P, ne], I32)
        col = {k: sb(f"col_{k}", [P, tiles]) for k in "off pos kept0 kept1 posm row z rz d2 e2 g2 sum rd w".split()}
        r_chain = sem("r_chain")
        r_counts = sem("r_counts")
        r_shift = sem("r_shift")
        r_exp = sem("r_exp")
        r_joined = sem("r_joined")
        r_table = sem("r_table")
        n1 = filled[:, 0, 0, :]

        def wide(a):
            return a.rearrange("p (t a) -> p t a", a=1).broadcast_to((P, tiles, ne))

        def tall(a):
            return a.rearrange("p (a e) -> p a e", a=1).broadcast_to((P, tiles, ne))

        with nc.Block() as block:
            @block.vector
            def _(dve):
                count = [0]

                def link(ins):
                    count[0] += 1
                    ins.then_inc(r_chain, 1)
                    dve.wait_ge(r_chain, count[0])

                link(dve.tensor_scalar(n1f[:, :], n1, float(cap), None, ALU.min))
                dve.tensor_copy(n1i[:, :], n1f[:, :]).then_inc(r_counts, 1)
                dve.tensor_tensor(soft[:, :, :], logits_all[:, :, :], wide(top_all[:, :, 0]), ALU.subtract).then_inc(r_shift, 1)
                dve.tensor_tensor(col["d2"][:, :], top_all[:, :, 1], top_all[:, :, 0], ALU.subtract).then_inc(r_shift, 1)
                link(dve.tensor_tensor(big[0][:, :, :], wide(expert_all[:, :, 1]), tall(iota_e[:, :]), ALU.is_equal))
                link(dve.tensor_tensor(big[1][:, :, :], big[0][:, :, :], tall(n1), ALU.mult))
                link(dve.tensor_reduce(col["off"][:, :], big[1][:, :, :], AX, ALU.add))
                link(dve.tensor_tensor(place_all[:, :, 1], place_all[:, :, 1], col["off"][:, :], ALU.add))
                for c in range(2):
                    link(dve.tensor_scalar(col[f"kept{c}"][:, :], place_all[:, :, c], float(cap), None, ALU.is_lt))
                    link(dve.tensor_scalar(col["posm"][:, :], place_all[:, :, c], float(cap - 1), None, ALU.min))
                    link(dve.scalar_tensor_tensor(out=col["row"][:, :], in0=expert_all[:, :, c], scalar=float(cap),
                                                  in1=col["posm"][:, :], op0=ALU.mult, op1=ALU.add))
                    link(dve.tensor_copy(routes[:, c, :], col["row"][:, :]))
                dve.wait_ge(r_exp, 2)
                link(dve.tensor_reduce(col["z"][:, :], soft[:, :, :], AX, ALU.add))
                link(dve.reciprocal(col["rz"][:, :], col["z"][:, :]))
                link(dve.tensor_tensor(col["g2"][:, :], col["e2"][:, :], col["rz"][:, :], ALU.mult))
                link(dve.tensor_tensor(col["sum"][:, :], col["g2"][:, :], col["rz"][:, :], ALU.add))
                link(dve.tensor_scalar(col["w"][:, :], col["sum"][:, :], 1e-9, None, ALU.max))
                link(dve.reciprocal(col["rd"][:, :], col["w"][:, :]))
                for c, gate in enumerate((col["rz"], col["g2"])):
                    link(dve.tensor_tensor(col["sum"][:, :], gate[:, :], col["rd"][:, :], ALU.mult))
                    link(dve.tensor_tensor(gates[:, c, :], col["sum"][:, :], col[f"kept{c}"][:, :], ALU.mult))

            @block.scalar
            def _(act):
                act.wait_ge(r_shift, 2)
                act.activation(soft[:, :, :], soft[:, :, :], ACT.Exp).then_inc(r_exp, 1)
                act.activation(col["e2"][:, :], col["d2"][:, :], ACT.Exp).then_inc(r_exp, 1)

            @block.sync
            def _(sp):
                sp.wait_ge(r_counts, 1)
                for e in range(ne):
                    n = sp.value_load(n1i[0:1, e:e + 1], min_val=0, max_val=cap)
                    base = e * 2 * cap
                    sp.dma_start(slot_dram[0][bass.ds(n + base, cap), :].rearrange("(a m) o -> a (m o)", a=16),
                                 slot_dram[1][base:base + cap, :].rearrange("(a m) o -> a (m o)", a=16)).then_inc(r_joined, 16)
                    sp.wait_ge(r_joined, 16 * (e + 1))
                for e in range(ne):
                    base = e * 2 * cap
                    sp.dma_start(slot_tok[:, e, :], slot_dram[0][base:base + cap, :].rearrange("(p j) o -> p (j o)", p=P))\
                        .then_inc(r_table, 16)
                sp.wait_ge(r_table, 16 * ne)


def experts(nc, g):
    ne, cap, tiles, ff = g["ne"], g["cap"], g["tiles"], g["ff"]
    x2_dram, w_gate, w_down = g["x2_dram"], g["w_gate"], g["w_down"]
    ident, slot_tok = g["ident"], g["slot_tok"]
    gpe = cap // (4 * P)
    fts = ff // P
    eo_view = g["eo_dram"].rearrange("(e p j) d -> e p j d", e=ne, p=P)
    with ExitStack() as ctx:
        def sb(name, shape, dt=F32):
            return ctx.enter_context(nc.sbuf_tensor(name, shape, dt))

        def bank(name, shape, dt=F32):
            return ctx.enter_context(nc.psum_tensor(name, shape, dt))

        def sem(name):
            return ctx.enter_context(nc.semaphore(name))

        wg_e = [sb(f"wg_e{b}", [P, 2, ff]) for b in range(2)]
        wd_e = [sb(f"wd_e{b}", [P, fts, 256]) for b in range(2)]
        idc = [sb(f"idc{b}", [P, 4], U32) for b in range(2)]
        xg = [sb(f"xg{b}", [P, 4, 256]) for b in range(2)]
        xt = [sb(f"xt{b}", [P, 2, 512]) for b in range(2)]
        ht = [sb(f"ht{b}", [P, fts, 512]) for b in range(2)]
        eo = [sb(f"eo{b}", [P, 4, 256]) for b in range(2)]
        tr_ps = [bank(f"tr_ps{k}", [P, 512]) for k in range(2)]
        h_ps = [bank(f"h_ps{k}", [P, 512]) for k in range(4)]
        o_ps = bank("o_ps", [P, 4, 256])
        w_in = [sem(f"w_in{b}") for b in range(2)]
        rows_in = [sem(f"rows_in{b}") for b in range(2)]
        eo_out = [sem(f"eo_out{b}") for b in range(2)]
        ids_ready = sem("ids_ready")
        xtr_full = sem("xtr_full")
        xt_ready = sem("xt_ready")
        h_full = sem("h_full")
        h_ready = sem("h_ready")
        o_full = sem("o_full")
        eo_ready = sem("eo_ready")
        passed = {k: sem(f"x_passed_{k}") for k in ("sp", "pe", "pool")}
        PER = {ids_ready: 1, xtr_full: 2, xt_ready: 2, h_full: fts, h_ready: fts, o_full: 4, eo_ready: 2}

        class Group:

            def __init__(self, ep, par, gi, b):
                self.e, self.par, self.b = ep * 2 + par, par, b
                self.j = gi * 8 + b * 4
                self.ep, self.gi = ep, gi

            def number(self, mul, add=0):
                return self.ep * (2 * gpe * mul) + self.gi * (2 * mul) + ((self.par * gpe + self.b) * mul + add)

            def past(self, sem_, k=0):
                per = PER[sem_]
                return self.number(per, 2 * per + k)

            def landed(self, per, extra=0):
                return self.ep * (gpe * per) + self.gi * per + (self.par * gpe // 2 + 1 + extra) * per

        def groups(eng, body, head=None, tail=None, pairs=None):
            with eng.Fori(0, pairs or ne // 2) as ep:
                pair(eng, ep, body, head, tail)

        def pair(eng, ep, body, head=None, tail=None):
            for par in range(2):
                if head:
                    head(ep, par)
                with eng.Fori(0, gpe // 2) as gi:
                    for b in range(2):
                        body(Group(ep, par, gi, b))
                if tail:
                    tail(ep, par)

        def start_past(eng, sem_):
            eng.sem_inc(sem_, 2 * PER[sem_])

        with nc.Block() as block:
            @block.sync
            def _(sp):
                def load_weights(e, par):
                    sp.dma_start(wg_e[par][:, :, :], w_gate[bass.ds(e, 1)].rearrange("a (k p) f -> p (a k) f", p=P)).then_inc(w_in[par], 16)
                    sp.dma_start(wd_e[par][:, :, :], w_down[bass.ds(e, 1)].rearrange("a (k p) d -> p (a k) d", p=P)).then_inc(w_in[par], 16)

                def store(q):
                    need_alone(sp, passed["sp"], eo_ready, q.past(eo_ready, 2))
                    sp.dma_start(eo_view[bass.ds(q.e, 1), :, bass.ds(q.j, 4), :].rearrange("a p j d -> (a p) j d"),
                                 eo[q.b][:, :, :]).then_inc(eo_out[q.b], 16)

                load_weights(0, 0)
                load_weights(1, 1)
                groups(sp, store, tail=lambda ep, par: load_weights(ep * 2 + (par + 2), par), pairs=ne // 2 - 1)
                pair(sp, ne // 2 - 1, store)
                for b in range(2):
                    sp.wait_ge(eo_out[b], 16 * ne * gpe // 2)

            @block.gpsimd
            def _(pool):
                ids = slot_tok[:, :, :].rearrange("p e j -> p (e j)")

                def gather(q):
                    need_alone(pool, passed["pool"], xtr_full, q.past(xtr_full, -2))
                    pool.tensor_copy(idc[q.b][:, :], ids[:, bass.ds(q.number(4), 4)]).then_inc(ids_ready, 1)
                    need_alone(pool, passed["pool"], ids_ready, q.past(ids_ready, 1))
                    for j in range(4):
                        pool.indirect_dma_start(out=xg[q.b][:, j, :], out_offset=None, in_=x2_dram,
                                                in_offset=bass.IndirectOffsetOnAxis(ap=idc[q.b][:, j:j + 1], axis=0))\
                            .then_inc(rows_in[q.b], 16)

                start_past(pool, ids_ready)
                groups(pool, gather)

            @block.tensor
            def _(pe):
                def group(q):
                    pe.wait_ge(rows_in[q.b], q.landed(64))
                    for dk in range(2):
                        pe.wait_ge(xt_ready, q.past(xt_ready, dk - 1))
                        for j in range(4):
                            mm = pe.transpose(tr_ps[dk][:, j * P:j * P + P], xg[q.b][:, j, dk * P:dk * P + P], ident[:, :])
                        mm.then_inc(xtr_full, 1)
                    pe.wait_ge(xt_ready, q.past(xt_ready, 2))
                    for f in range(fts):
                        pe.wait_ge(h_ready, q.past(h_ready, f - 3))
                        for dk in range(2):
                            mm = pe.matmul(h_ps[f % 4][:, :], wg_e[q.par][:, dk, f * P:f * P + P], xt[q.b][:, dk, :],
                                           start=(dk == 0), stop=(dk == 1))
                        mm.then_inc(h_full, 1)
                    for j in range(4):
                        pe.wait_ge(eo_ready, q.past(eo_ready, j // 2 - 1))
                        for f in range(fts):
                            if j == 0:
                                pe.wait_ge(h_ready, q.past(h_ready, f + 1))
                            mm = pe.matmul(o_ps[:, j, :], ht[q.b][:, f, j * P:j * P + P], wd_e[q.par][:, f, :],
                                           start=(f == 0), stop=(f == fts - 1))
                        mm.then_inc(o_full, 1)

                start_past(pe, xtr_full)
                start_past(pe, h_full)
                start_past(pe, o_full)
                groups(pe, group, head=lambda ep, par: need_alone(pe, passed["pe"], w_in[par], ep * 32 + 32))

            @block.scalar
            def _(act):
                def gelu(q):
                    act.wait_ge(o_full, q.past(o_full, -4))
                    for f in range(fts):
                        act.wait_ge(h_full, q.past(h_full, f + 1))
                        act.activation(ht[q.b][:, f, :], h_ps[f % 4][:, :], ACT.Gelu).then_inc(h_ready, 1)

                start_past(act, h_ready)
                groups(act, gelu)

            @block.vector
            def _(dve):
                def copies(q):
                    for dk in range(2):
                        dve.wait_ge(xtr_full, q.past(xtr_full, dk + 1))
                        if dk == 0:
                            dve.wait_ge(h_full, q.past(h_full, -fts))
                        dve.tensor_copy(xt[q.b][:, dk, :], tr_ps[dk][:, :]).then_inc(xt_ready, 1)
                    for half in range(2):
                        dve.wait_ge(o_full, q.past(o_full, 2 * half + 2))
                        if half == 0:
                            dve.wait_ge(eo_out[q.b], q.landed(16, -1))
                        dve.tensor_copy(eo[q.b][:, 2 * half:2 * half + 2, :], o_ps[:, 2 * half:2 * half + 2, :]).then_inc(eo_ready, 1)

                start_past(dve, xt_ready)
                start_past(dve, eo_ready)
                groups(dve, copies)


def combine(nc, g):
    tiles, routes, gates = g["tiles"], g["routes"], g["gates"]
    eo_dram = g["eo_dram"]
    h2_dram = g["h2_dram"].rearrange("(q l p) d -> q p l d", l=2, p=P)
    out = g["out"].rearrange("q (l p) d -> q p l d", l=2)
    with ExitStack() as ctx:
        def sb(name, shape, dt=F32):
            return ctx.enter_context(nc.sbuf_tensor(name, shape, dt))

        def sem(name):
            return ctx.enter_context(nc.semaphore(name))

        idx = [sb(f"cidx{b}", [P, 2, 2], U32) for b in range(2)]
        gate = [sb(f"cgate{b}", [P, 2, 2]) for b in range(2)]
        got = [sb(f"got{b}", [P, 2, 2, 256]) for b in range(2)]
        res = [sb(f"res{b}", [P, 2, 256]) for b in range(2)]
        acc = [sb(f"acc{b}", [P, 2, 256]) for b in range(2)]
        sums = [sb(f"sums{b}", [P, 2, 256]) for b in range(2)]
        got_in = [sem(f"got_in{b}") for b in range(2)]
        res_in = [sem(f"res_in{b}") for b in range(2)]
        sum_out = [sem(f"sum_out{b}") for b in range(2)]
        idx_ready = sem("idx2_ready")
        gate_ready = sem("gate_ready")
        first_done = sem("first_done")
        sums_done = sem("sums_done")
        passed = {k: sem(f"c_passed_{k}") for k in ("sp", "pool")}
        rounds = tiles // 4

        with nc.Block() as block:
            @block.sync
            def _(sp):
                def load(j, b):
                    sp.dma_start(res[b][:, :, :], h2_dram[bass.ds(j * 2 + b, 1)].rearrange("a p l d -> (a p) l d")).then_inc(res_in[b], 16)

                for b in range(2):
                    load(0, b)
                with sp.Fori(0, rounds - 1) as j:
                    for b in range(2):
                        need_alone(sp, passed["sp"], sums_done, j * 4 + (2 * b + 4))
                        sp.dma_start(out[bass.ds(j * 2 + b, 1)].rearrange("a p l d -> (a p) l d"), sums[b][:, :, :]).then_inc(sum_out[b], 16)
                        load(j + 1, b)
                for b in range(2):
                    sp.wait_ge(sums_done, (rounds - 1) * 4 + 2 * b + 4)
                    sp.dma_start(out[2 * rounds - 2 + b], sums[b][:, :, :]).then_inc(sum_out[b], 16)
                for b in range(2):
                    sp.wait_ge(sum_out[b], 16 * rounds)

            @block.gpsimd
            def _(pool):
                with pool.Fori(0, rounds) as j:
                    for b in range(2):
                        need_alone(pool, passed["pool"], sums_done, j * 4 + 2 * b)
                        pool.tensor_copy(idx[b][:, :, :], routes[:, :, bass.ds(j * 4 + 2 * b, 2)]).then_inc(idx_ready, 1)
                        need_alone(pool, passed["pool"], idx_ready, j * 2 + (b + 1))
                        for c in range(2):
                            for l in range(2):
                                pool.indirect_dma_start(out=got[b][:, c, l, :], out_offset=None, in_=eo_dram,
                                                        in_offset=bass.IndirectOffsetOnAxis(ap=idx[b][:, c, l:l + 1], axis=0))\
                                    .then_inc(got_in[b], 16)

            @block.vector
            def _(dve):
                dve.sem_inc(sums_done, 2)
                with dve.Fori(0, rounds) as j:
                    for b in range(2):
                        dve.tensor_copy(gate[b][:, :, :], gates[:, :, bass.ds(j * 4 + 2 * b, 2)]).then_inc(gate_ready, 1)
                        dve.wait_ge(gate_ready, j * 2 + (b + 1))
                        dve.wait_ge(got_in[b], j * 64 + 64)
                        dve.wait_ge(res_in[b], j * 16 + 16)
                        for l in range(2):
                            dve.scalar_tensor_tensor(out=acc[b][:, l, :], in0=got[b][:, 0, l, :], scalar=gate[b][:, 0, l:l + 1],
                                                     in1=res[b][:, l, :], op0=ALU.mult, op1=ALU.add).then_inc(first_done, 1)
                        dve.wait_ge(sum_out[b], j * 16)
                        for l in range(2):
                            dve.wait_ge(first_done, j * 4 + (2 * b + l + 1))
                            dve.scalar_tensor_tensor(out=sums[b][:, l, :], in0=got[b][:, 1, l, :], scalar=gate[b][:, 1, l:l + 1],
                                                     in1=acc[b][:, l, :], op0=ALU.mult, op1=ALU.add).then_inc(sums_done, 1)


_NAMES = ["x", "wkv", "wq", "bkv", "bq_tok", "w_bias_t", "mask_t", "out_w", "out_b", "ln_g", "ln_b",
          "wq_t", "bq", "wk_t", "bk", "wv_t", "bv", "wo_t", "bo", "beta", "t_par", "ln_w", "ln_b2",
          "wg", "w_gate", "w_down"]


def kernel(**inputs):
    import numpy as _np
    import concourse.bacc as _bacc
    from concourse import mybir as _mybir
    from concourse.bass_utils import run_bass_kernel_spmd as _run

    a = {k: _np.asarray(v) for k, v in inputs.items()}
    n, c, l, h = a["x"].shape
    tok, att, ffn = "L0_tok_", "L0_attn_", "L0_ffn_"
    host = {
        "x": a["x"].reshape(n, c, l * h),
        "wkv": _np.stack([a[tok + "Wk_w"].T, a[tok + "Wv_w"].T]), "wq": a[tok + "Wq_w"].T,
        "bkv": _np.stack([a[tok + "Wk_b"], a[tok + "Wv_b"]]), "bq_tok": a[tok + "Wq_b"],
        "w_bias_t": a[tok + "w_bias"].T, "mask_t": a[tok + "local_mask"].T,
        "out_w": a[tok + "out_w"], "out_b": a[tok + "out_b"], "ln_g": a[tok + "ln_g"], "ln_b": a[tok + "ln_b"],
        "wq_t": a[att + "Wq"].T, "bq": a[att + "bq"], "wk_t": a[att + "Wk"].T, "bk": a[att + "bk"],
        "wv_t": a[att + "Wv"].T, "bv": a[att + "bv"], "wo_t": a[att + "Wo"].T, "bo": a[att + "bo"],
        "beta": a[att + "beta"], "t_par": a[att + "t"], "ln_w": a[att + "ln_w"], "ln_b2": a[att + "ln_b"],
        "wg": a[ffn + "wg"], "w_gate": a[ffn + "w_gate"], "w_down": a[ffn + "w_down"],
    }
    nc = _bacc.Bacc("TRN2", target_bir_lowering=False, num_devices=1)
    arrays, args = {}, []
    for name in _NAMES:
        v = _np.ascontiguousarray(host[name])
        arrays[f"in_{name}"] = v
        args.append(nc.dram_tensor(f"in_{name}", v.shape, _mybir.dt.from_np(v.dtype), kind="ExternalInput").ap())
    args.append(nc.dram_tensor("out_0", (n, l, c * h), _mybir.dt.from_np(_np.dtype("float32")), kind="ExternalOutput").ap())
    tower_program(nc, *args)
    r = _run(nc, [arrays], core_ids=[0])
    return r.results[0]["out_0"]
```

```python
from contextlib import ExitStack

import concourse.bass as bass
from concourse import mybir

ALU = mybir.AluOpType
ACT = mybir.ActivationFunctionType
AX = mybir.AxisListType.X
F32 = mybir.dt.float32
BF16 = mybir.dt.bfloat16
U32 = mybir.dt.uint32
I32 = mybir.dt.int32
U8 = mybir.dt.uint8
F32R = mybir.dt.float32r

P = 128
EPS = 1e-5
PARTS_Q = (0, 0, 0, 1, 1, 2)
PARTS_K = (0, 1, 2, 0, 1, 0)
RUNS_Q = ((0, 1, 3), (1, 1, 2), (2, 1, 1))
RUNS_K = ((0, 3, 1), (0, 2, 1), (0, 1, 1))
STACK_DMAS = len(RUNS_Q + RUNS_K)
SPLIT_DMAS = 2 * 3
SROWS = 16 * len(PARTS_Q)
NPART = 3
VW = 32
LOOP_FIRST = 4


class Batch:

    def __init__(self, c, reg=None):
        self.c, self.reg = c, reg

    def __add__(self, d):
        return Batch(self.c + d, self.reg)

    def before(self, per=1, k=0):
        return self.c * per + k if self.reg is None else self.reg * (2 * per) + (self.c * per + k)

    def landed(self, per=16):
        rounds = self.c // 2 + 1
        return rounds * per if self.reg is None else self.reg * per + rounds * per

    @property
    def par(self):
        return self.c % 2


def need(eng, sem, value):
    if isinstance(value, int) and value <= 0:
        return
    eng.wait_ge(sem, value)


def need_alone(eng, passed, sem, value):
    if isinstance(value, int) and value <= 0:
        return
    eng.wait_ge(sem, value)
    if not isinstance(value, int):
        eng.sem_inc(passed, 1)


def turns(eng, nb, step, ahead=3):
    last_full = nb - 1 - ahead
    trips = (last_full - LOOP_FIRST + 1) // 2
    for i in range(-3, LOOP_FIRST):
        step(Batch(i), nb)
    with eng.Fori(0, trips) as j:
        for c in range(2):
            step(Batch(LOOP_FIRST + c, j), nb)
    for i in range(LOOP_FIRST + 2 * trips, nb + 2):
        step(Batch(i), nb)


def pool_turns(eng, nb, step):
    last_full = nb - 4
    trips = (last_full - LOOP_FIRST + 1) // 2
    for i in range(-3, LOOP_FIRST):
        step(Batch(i), nb, i % 4)
    with eng.Fori(0, trips // 2) as j:
        for c in range(4):
            step(Batch4(LOOP_FIRST + c, j), nb, (LOOP_FIRST + c) % 4)
    first = LOOP_FIRST + 4 * (trips // 2)
    for i in range(first, nb + 2):
        step(Batch(i), nb, i % 4)


class Batch4(Batch):

    def __add__(self, d):
        return Batch4(self.c + d, self.reg)

    def before(self, per=1, k=0):
        return self.reg * (4 * per) + (self.c * per + k)

    def landed(self, per=16):
        return self.reg * (2 * per) + (self.c // 2 + 1) * per


def slot(h):
    return 2 * (h % 8) + h // 8


def has(n, nb):
    return n.reg is not None or 0 <= n.c < nb


def tower_program(nc, **g):
    x, wg = g["x"], g["wg"]
    nb, ltok = x.shape[0], 256
    dm = 256
    nh, dh = 16, 16
    ne, ff = wg.shape[1], 1024
    tokens = nb * ltok
    cap = 2 * tokens // ne
    tiles = tokens // P
    g.update(nb=nb, ltok=ltok, dm=dm, nh=nh, dh=dh, ne=ne, ff=ff, cap=cap, tiles=tiles, SC=1.0 / dh ** 0.5)

    h2_dram = nc.dram_tensor("h2_dram", (tokens, dm), F32, kind="Internal").ap()
    x2_dram = nc.dram_tensor("x2_dram", (tokens, dm), F32, kind="Internal").ap()
    eo_dram = nc.dram_tensor("eo_dram", (ne * cap, dm), F32, kind="Internal").ap()
    qk_dram = [nc.dram_tensor(f"qk_dram{b}", (2, NPART, dh, nh * ltok), BF16, kind="Internal").ap() for b in range(2)]
    slot_dram = [nc.dram_tensor(f"slot_dram{c}", (ne * 2 * cap, 1), U32, kind="Internal").ap() for c in range(2)]

    g.update(h2_dram=h2_dram, x2_dram=x2_dram, eo_dram=eo_dram, qk_dram=qk_dram, slot_dram=slot_dram)

    outer = ExitStack()
    with outer:
        def keep(name, shape, dt=F32):
            return outer.enter_context(nc.sbuf_tensor(name, shape, dt))

        passed = {k: outer.enter_context(nc.semaphore(f"passed_{k}")) for k in ("sp", "pe", "dve", "pool")}
        scat_out, rows_in, got_in = ([outer.enter_context(nc.semaphore(f"{k}{b}")) for b in range(2)]
                                     for k in ("scat_out", "rows_in", "got_in"))

        ident = keep("ident", [P, P])
        routes = keep("routes", [P, 2, tiles], U32)
        gates = keep("gates", [P, 2, tiles])
        slot_tok = keep("slot_tok", [P, ne, cap // P], U32)
        g.update(passed=passed, scat_out=scat_out, rows_in=rows_in, got_in=got_in,
                 ident=ident, routes=routes, gates=gates, slot_tok=slot_tok)
        with ExitStack() as until_routed:
            def sb(name, shape):
                return until_routed.enter_context(nc.sbuf_tensor(name, shape, F32))

            logits_all = sb("logits_all", [P, tiles, ne])
            top_all = sb("top_all", [P, tiles, 2])
            expert_all = sb("expert_all", [P, tiles, 2])
            place_all = sb("place_all", [P, tiles, 2])
            filled = sb("filled", [P, 2, 2, ne])
            iota_e = sb("iota_e", [P, ne])
            g.update(logits_all=logits_all, top_all=top_all, expert_all=expert_all, place_all=place_all,
                     filled=filled, iota_e=iota_e)
            tower(nc, g)
            finish_routes(nc, g)
        experts(nc, g)
        combine(nc, g)


def tower(nc, g):
    x, out_w, wg = g["x"], g["out_w"], g["wg"]
    nb, ltok, dm, nh, dh, ne, cap, tiles, SC = (g[k] for k in "nb ltok dm nh dh ne cap tiles SC".split())
    qk_dram, slot_dram = g["qk_dram"], g["slot_dram"]
    ident, iota_e, filled = g["ident"], g["iota_e"], g["filled"]
    logits_all, top_all, expert_all, place_all = (g[k] for k in ("logits_all", "top_all", "expert_all", "place_all"))
    h2_dram = g["h2_dram"].rearrange("(n lt p) d -> n p lt d", p=P, lt=2)
    x2_dram = g["x2_dram"].rearrange("(n lt p) d -> n p lt d", p=P, lt=2)

    ctx = ExitStack()
    with ctx:
        def sb(name, shape, dt=F32):
            return ctx.enter_context(nc.sbuf_tensor(name, shape, dt))

        def bank(name, shape, dt=F32):
            return ctx.enter_context(nc.psum_tensor(name, shape, dt))

        def sem(name):
            return ctx.enter_context(nc.semaphore(name))

        wkv_sb = sb("wkv_sb", [65, 2, 64])
        wq_sb = sb("wq_sb", [65, 64])
        xid = sb("xid", [65, 4, 64])
        ew_t = sb("ew_t", [P, 2, 256])
        mask_sb = sb("mask_sb", [P, 2, 256], U8)
        outw_sb = sb("outw_sb", [P, 2, 256])
        wqa = sb("wqa", [P, 2, 256])
        wka = sb("wka", [P, 2, 256])
        wva = sb("wva", [P, 2, 256])
        woa = sb("woa", [P, 2, 256])
        wg_sb = sb("wg_sb", [P, 2, ne])
        rows = {k: sb(f"row_{k}", [P, 256]) for k in ("ln_g", "ln_b", "bv", "bo", "ln_w", "ln_b2")}
        bqk = sb("bqk", [P, 4])
        beta_sb = sb("beta_sb", [P, nh])
        t_sb = sb("t_sb", [P, nh])
        b8 = sb("b8", [P, nh])
        b4 = sb("b4", [P, nh])
        c16t = sb("c16t", [P, nh])
        c16 = sb("c16", [P, nh])
        eps = sb("eps", [P, 1])
        identb = sb("identb", [P, P], BF16)
        before_b = sb("before_b", [P, P], BF16)
        ones_b = sb("ones_b", [P, P], BF16)
        tok_ids = sb("tok_ids", [P, tiles], I32)
        iota_i = sb("iota_i", [P, ne], I32)
        zero_i = sb("zero_i", [P, 2 * ne * cap // P], U32)

        xb = [sb(f"xb{b}", [65, ltok * 4]) for b in range(2)]
        ek = sb("ek", [P, 2, 256])
        ekv = sb("ekv", [P, 2, 256])
        eq = sb("eq", [P, 2, 256])
        dn = sb("dn", [P, 2, 256])
        rec = sb("rec", [P, 2, 256])
        y_t = sb("y_t", [P, 2, 256])
        hn = sb("hn", [P, 2, 256])
        hg = sb("hg", [P, 2, 256])
        h1 = sb("h1", [P, 2, 256])
        x1 = sb("x1", [P, 2, 256])
        hx0 = sb("hx0", [P, 2, 256])
        hx = [sb(f"hxr{b}", [P, 2, 256]) for b in range(4)]
        x1_t = [sb(f"x1_t{b}", [P, 2, 256]) for b in range(2)]
        stat = [sb(f"stat{k}", [P, 2, 6]) for k in range(4)]
        mv = [sb(f"mv{k}", [P, 2, 2]) for k in range(4)]
        lnv = [sb(f"lnv{k}", [P, 2]) for k in range(4)]
        rs = [sb(f"rs{k}", [P, 2]) for k in range(4)]
        qkf = sb("qkf", [P, 4, 256])
        qkr = sb("qkr", [P, 4, 256])
        qkp = sb("qkp", [P, NPART, 4, 256], BF16)
        q_stack = [sb(f"q_stack{b}", [P, nh, ltok], BF16) for b in range(2)]
        k_stack = [sb(f"k_stack{b}", [P, nh, ltok], BF16) for b in range(2)]
        v_sb = [sb(f"v_sb{b}", [P, 2, nh, VW]) for b in range(2)]
        rmax = sb("rmax", [P, nh, 2])
        nmx = sb("nmx", [P, nh, 2])
        nmr = sb("nmr", [P, nh, 2])
        mparts = sb("mparts", [P, 2, NPART, nh], BF16)
        mrow = sb("mrow", [NPART * nh, ltok], BF16)
        z_sb = [sb(f"z_sb{b}", [P, 2, 512]) for b in range(2)]
        u_sb = [sb(f"u_sb{b}", [P, 2, 512]) for b in range(2)]
        zb = sb("zb", [P, 512])
        p_sb = [sb(f"p_sb{b}", [P, 4, 2, 256]) for b in range(2)]
        g_sb = [sb(f"g_sb{b}", [P, 4, 2, 256]) for b in range(2)]
        f_sb = sb("f_sb", [P, 512])
        rc = sb("rc", [P, 16])
        ntv = sb("ntv", [P, 2, 2, 4, 16])
        f_n = sb("f_n", [P, 2, 256])
        f_t = sb("f_t", [P, 2, 256])
        yb = sb("yb", [P, 2, 256])
        yn = sb("yn", [P, 2, 256])
        yw = sb("yw", [P, 2, 256])
        h2 = [sb(f"h2_{b}", [P, 2, 256]) for b in range(2)]
        x2 = [sb(f"x2_{b}", [P, 2, 256]) for b in range(2)]
        x2_t = sb("x2_t", [P, 2, 256])
        lgt = sb("lgt", [P, 2, ne])
        top8 = sb("top8", [P, 2, 8])
        idx8 = sb("idx8", [P, 2, 8], U32)
        idxf = sb("idxf", [P, 2, 2])
        hot = sb("hot", [P, 2, 2, ne], BF16)
        locb = sb("locb", [P, 2, 2, ne])
        lsel = sb("lsel", [P, 2, 2, ne])
        loc = sb("loc", [P, 2, 2])
        over = sb("over", [P, 2, 2])
        flat = sb("flat", [P, 2, 2])
        flat2 = sb("flat2", [P, 2, 2])
        slot_u = [sb(f"slot_u{b}", [P, 4], U32) for b in range(2)]
        tok_u = [sb(f"tok_u{b}", [P, 2], U32) for b in range(2)]

        raw_ps = bank("raw_ps", [P, 2, 2, 256])
        sh_ps = bank("sh_ps", [P, 2, 2, 256])
        pv_ps = bank("pv_ps", [P, 512])
        a_ps = bank("a_ps", [P, 512])
        b_ps = bank("b_ps", [P, 512])
        t_ps = bank("t_ps", [P, 512])
        b_bf = b_ps[:, :].bitcast(BF16)

        s_w = sem("s_w")
        s_c0 = sem("s_c0")
        s_c1 = sem("s_c1")
        s_d = sem("s_d")
        s_z = sem("s_z")
        s_zd = sem("s_zd")
        s_i = sem("s_i")
        with nc.Block() as block:
            @block.sync
            def _(sp):
                loads = [
                    (wkv_sb[0:64, :, :], g["wkv"].rearrange("k c d -> c k d")), (wkv_sb[64:65, :, :], g["bkv"].rearrange("k (a d) -> a k d", a=1)),
                    (wq_sb[0:64, :], g["wq"]), (wq_sb[64:65, :], g["bq_tok"].rearrange("(a d) -> a d", a=1)),
                    (xid[64:65, :, :], g["out_b"].rearrange("(a h c) -> a h c", a=1, c=64)),
                    (ew_t[:, :, :], g["w_bias_t"].rearrange("(s p) t -> p s t", p=P)),
                    (mask_sb[:, :, :], g["mask_t"].rearrange("(s p) t -> p s t", p=P)),
                    (wg_sb[:, :, :], wg.rearrange("(k p) e -> p k e", p=P)),
                    (bqk[:, 0:2], g["bq"].rearrange("(m p) -> p m", p=P)),
                    (bqk[:, 2:4], g["bk"].rearrange("(m p) -> p m", p=P)),
                    (beta_sb[:, :], g["beta"].partition_broadcast(P)),
                    (t_sb[:, :], g["t_par"].partition_broadcast(P)),
                ]
                loads += [(w[:, :, :], d.rearrange("(k p) n -> p k n", p=P)) for w, d in
                          ((outw_sb, out_w), (wqa, g["wq_t"]), (wka, g["wk_t"]), (wva, g["wv_t"]), (woa, g["wo_t"]))]
                loads += [(r[:, :], g[k].partition_broadcast(P)) for k, r in rows.items()]
                for dst, src in loads:
                    sp.dma_start(dst, src, allow_slow_non_contiguous=True).then_inc(s_w, 16)
                sp.wait_ge(s_w, 16 * len(loads))
                sp.wait_ge(s_z, 1)
                for c in range(2):
                    sp.dma_start(slot_dram[c].rearrange("(p m) o -> p (m o)", p=P), zero_i[:, :]).then_inc(s_zd, 16)
                sp.wait_ge(s_zd, 32)

            @block.gpsimd
            def _(pool):
                pool.memset(ident[:, :], 0.0).then_inc(s_c0, 1)
                pool.memset(before_b[:, :], 1.0).then_inc(s_c0, 1)
                pool.iota(iota_i[:, :], pattern=[[1, ne]], base=0, channel_multiplier=0).then_inc(s_c0, 1)
                pool.iota(tok_ids[:, :], pattern=[[P, tiles]], base=0, channel_multiplier=1).then_inc(s_c0, 1)
                pool.wait_ge(s_c0, 4)
                pool.affine_select(out=ident[:, :], in_=ident[:, :], compare_op=ALU.not_equal, fill=1.0,
                                   base=0, pattern=[[-1, P]], channel_multiplier=1).then_inc(s_c1, 1)
                pool.affine_select(out=before_b[:, :], in_=before_b[:, :], compare_op=ALU.is_ge, fill=0.0,
                                   base=-1, pattern=[[1, P]], channel_multiplier=-1).then_inc(s_c1, 1)

            @block.vector
            def _(dve):
                fills = [(zero_i[:, :], 0), (ones_b[:, :], 1.0), (eps[:, :], EPS), (filled[:, :, :, :], 0.0)]
                fills += [(v[:, :, :, :], 0.0) for v in v_sb]
                for b in range(2):
                    fills += [(xb[b][64:65, :], 1.0), (k_stack[b][96:128, :, :], 1.0), (q_stack[b][96:128, :, :], 0.0)]
                for n, (dst, value) in enumerate(fills):
                    dve.memset(dst, value).then_inc(s_z if n == 0 else s_i, 1)
                done = len(fills) - 1
                dve.wait_ge(s_i, done)
                for v in v_sb:
                    dve.memset(v[:, :, :, 16:17], 2.0).then_inc(s_d, 1)
                dve.wait_ge(s_c1, 2)
                dve.tensor_copy(identb[:, :], ident[:, :]).then_inc(s_d, 1)
                for h in range(4):
                    dve.tensor_copy(xid[0:64, h, :], ident[0:64, 0:64]).then_inc(s_d, 1)
                dve.tensor_copy(iota_e[:, :], iota_i[:, :]).then_inc(s_d, 1)
                dve.wait_ge(s_w, 16 * (12 + 5 + len(rows)))
                dve.tensor_tensor(ew_t[:, :, :], ew_t[:, :, :], mask_sb[:, :, :], ALU.mult).then_inc(s_d, 1)
                dve.tensor_scalar(b8[:, :], beta_sb[:, :], 8.0, None, ALU.mult).then_inc(s_d, 1)
                dve.tensor_scalar(b4[:, :], beta_sb[:, :], 4.0, None, ALU.mult).then_inc(s_d, 1)
                dve.wait_ge(s_d, 11)
                dve.tensor_tensor(c16t[:, :], b4[:, :], t_sb[:, :], ALU.mult).then_inc(s_d, 1)
                dve.tensor_tensor(c16[:, :], b4[:, :], b4[:, :], ALU.mult).then_inc(s_d, 1)
                dve.wait_ge(s_d, 13)
                dve.tensor_tensor(c16t[:, :], c16t[:, :], c16t[:, :], ALU.mult).then_inc(s_d, 1)
                dve.wait_ge(s_d, 14)
                dve.tensor_tensor(c16[:, :], c16[:, :], c16t[:, :], ALU.add).then_inc(s_d, 1)

            @block.scalar
            def _(act):
                nc.scalar.preload_act_table_set("natural_log_exp_and_others")
                act.wait_ge(s_d, 15)
                act.activation(ew_t[:, :, :], ew_t[:, :, :], ACT.Exp).then_inc(s_c1, 1)

        names = """kv_full ek_ready ekv_ready q_full eq_ready den_full dn_ready ldn_ready rec_ready num_full yt_ready
            mix_full st0 ag0 lv0 rs0 hn_ready hg_ready h1_ready st1 ag1 lv1 rs1 x1_ready hx0_ready hx_ready
            x1t_full x1t_ready qk_full qk_copied part_h part_r part_m part_l v_full v_ready
            mx_full mx_ready nm_neg nm_h nm_r nm_m nm_r2 mparts_ready mt_full mt_ready
            raw_full z_ready sq_ready zb_ready u_pool l_ready g_ready sh_full p_ready
            pv_full f_ready tr_full rc_ready nt_ready fn_ready
            ft_full ft_ready y_full yb_ready st2 ag2 lv2 rs2 yn_ready yw_ready h2_ready st3 ag3 lv3 rs3 x2_ready
            x2t_full x2t_ready lg_full lg_copied lg_kept top_ready idx_ready idxf_ready hot_ready kept
            lc_full locb_ready fill_ready lsel_ready loc_ready over_ready flat_ready flat2_ready slot_ready""".split()
        s = {k: sem(k) for k in names}
        passed = g["passed"]
        x_in = [sem(f"x_in{b}") for b in range(2)]
        qk_out = [sem(f"qk_out{b}") for b in range(2)]
        stack_in = [sem(f"stack_in{b}") for b in range(2)]
        maxrow_in = [sem(f"maxrow_in{b}") for b in range(2)]
        h2_out = [sem(f"h2_out{b}") for b in range(2)]
        x2_out = [sem(f"x2_out{b}") for b in range(2)]
        scat_out = g["scat_out"]

        def dyn(n, mul=1):
            return bass.ds(n.before(mul), mul)

        with nc.Block() as block:
            @block.sync
            def _(sp):
                def load_x(n):
                    b = n.par
                    need_alone(sp, passed["sp"], s["mix_full"], n.before(1, -1))
                    sp.dma_start(xb[b][0:64, :], x[dyn(n)].rearrange("a c m -> (a c) m")).then_inc(x_in[b], 16)

                def store_qk(n):
                    need_alone(sp, passed["sp"], s["part_l"], n.before(1, 1))
                    need_alone(sp, passed["sp"], stack_in[n.par], (n + -2).landed(16 * STACK_DMAS) if has(n + -2, nb) else 0)
                    for c in range(2):
                        for part in range(NPART):
                            sp.dma_start(qk_dram[n.par][c, part].rearrange("r (h m) -> h r m", h=8), qkp[:, part, 2 * c:2 * c + 2, :])\
                                .then_inc(qk_out[n.par], 16)

                def load_stacks(n):
                    b = n.par
                    need_alone(sp, passed["sp"], qk_out[b], n.landed(16 * SPLIT_DMAS))
                    need_alone(sp, passed["sp"], s["sh_full"], (n + -1).before(8))
                    for c, (stack, runs) in enumerate(((q_stack[b], RUNS_Q), (k_stack[b], RUNS_K))):
                        row = 0
                        for part, parts, times in runs:
                            src = qk_dram[b][c, part:part + parts].rearrange("a r m -> (a r) m")
                            if times > 1:
                                src = src.rearrange("(t r) m -> t r m", t=1).broadcast_to((times, dh, nh * ltok))
                            width = dh * parts * times
                            sp.dma_start(stack[row:row + width, :, :].rearrange("r h n -> r (h n)"), src).then_inc(stack_in[b], 16)
                            row += width

                def load_maxrow(n):
                    need_alone(sp, passed["sp"], s["mt_ready"], n.before(1, 1))
                    for part in range(NPART):
                        sp.dma_start(q_stack[n.par][SROWS + part:SROWS + part + 1, :, :],
                                     mrow[part * nh:part * nh + nh, :]).then_inc(maxrow_in[n.par], 16)

                def store_h2(n):
                    need_alone(sp, passed["sp"], s["h2_ready"], n.before(1, 1))
                    sp.dma_start(h2_dram[dyn(n)].rearrange("a p l d -> (a p) l d"), h2[n.par][:, :, :]).then_inc(h2_out[n.par], 16)

                def store_x2(n):
                    need_alone(sp, passed["sp"], s["x2_ready"], n.before(2, 2))
                    sp.dma_start(x2_dram[dyn(n)].rearrange("a p l d -> (a p) l d"), x2[n.par][:, :, :]).then_inc(x2_out[n.par], 16)

                def step(i, nb):
                    if has(i + 1, nb):
                        load_stacks(i + 1)
                    if has(i + 4, nb) and i.c + 4 >= 2:
                        load_x(i + 4)
                    if has(i + 2, nb):
                        store_qk(i + 2)
                    if has(i + -1, nb):
                        store_h2(i + -1)
                    if has(i + 1, nb):
                        load_maxrow(i + 1)
                    if has(i + -1, nb):
                        store_x2(i + -1)

                load_x(Batch(0))
                load_x(Batch(1))
                turns(sp, nb, step, ahead=4)
                for sems in (h2_out, x2_out):
                    for b in range(2):
                        sp.wait_ge(sems[b], 16 * (nb // 2))

            @block.tensor
            def _(pe):
                def kv(n, lt):
                    if lt == 0:
                        pe.wait_ge(x_in[n.par], n.landed())
                        need(pe, s["hn_ready"], n.before(2))
                    else:
                        need(pe, s["ekv_ready"], n.before(2, 1))
                        need(pe, s["x1t_ready"], n.before(1))
                    xv = xb[n.par][:, :].rearrange("c (l h) -> c l h", h=4)
                    for h in range(4):
                        mm = pe.matmul(a_ps[:, h * P:(h + 1) * P], xv[:, lt * P:lt * P + P, h],
                                       wkv_sb[:, :, :].rearrange("c k d -> c (k d)"), start=True, stop=True)
                    mm.then_inc(s["kv_full"], 1)

                def q_tok(n):
                    need(pe, s["ekv_ready"], n.before(2, 2))
                    xv = xb[n.par][:, :].rearrange("c (l h) -> c l h", h=4)
                    for h in range(4):
                        mm = pe.matmul(a_ps[64 * (h % 2):64 * (h % 2) + 64, (h // 2) * 256:(h // 2) * 256 + 256],
                                       wq_sb[:, :], xv[:, :, h], start=True, stop=True)
                    mm.then_inc(s["q_full"], 1)

                def den(n, m):
                    if m == 0:
                        need(pe, s["ek_ready"], n.before(2, 2))
                        need(pe, s["eq_ready"], n.before(1, 1))
                    for st in range(2):
                        mm = pe.matmul(a_ps[:, m * 256:m * 256 + 256], ek[:, st, m * P:m * P + P], ew_t[:, st, :],
                                       start=(st == 0), stop=(st == 1))
                    if m == 1:
                        mm.then_inc(s["den_full"], 1)

                def num(n, m):
                    if m == 0:
                        need(pe, s["ekv_ready"], n.before(2, 2))
                        need(pe, s["dn_ready"], n.before(1, 1))
                    for st in range(2):
                        mm = pe.matmul(a_ps[:, m * 256:m * 256 + 256], ekv[:, st, m * P:m * P + P], ew_t[:, st, :],
                                       start=(st == 0), stop=(st == 1))
                    if m == 1:
                        mm.then_inc(s["num_full"], 1)

                def mix_out(n, lt):
                    if lt == 0:
                        need(pe, s["yt_ready"], n.before(1, 1))
                    xv = xb[n.par][:, :].rearrange("c (l h) -> c l h", h=4)
                    for h in range(4):
                        pe.matmul(a_ps[:, lt * 256 + h * 64:lt * 256 + h * 64 + 64], xv[:, lt * P:lt * P + P, h],
                                  xid[:, h, :], start=(h == 0), stop=False)
                    for m in range(2):
                        mm = pe.matmul(a_ps[:, lt * 256:lt * 256 + 256], y_t[:, m, lt * P:lt * P + P], outw_sb[:, m, :],
                                       start=False, stop=(m == 1))
                    if lt == 1:
                        mm.then_inc(s["mix_full"], 1)

                def transposed(n, src, ps, full):
                    for dk in range(2):
                        for lt in range(2):
                            mm = pe.transpose(ps[:, dk * 256 + lt * P:dk * 256 + lt * P + P], src[:, lt, dk * P:dk * P + P],
                                              ident[:, :])
                    mm.then_inc(s[full], 1)

                def x1_transposed(n):
                    need(pe, s["x1_ready"], n.before(2, 2))
                    if has(n + 1, nb):
                        need(pe, s["ekv_ready"], (n + 1).before(2, 1))
                    transposed(n, x1, a_ps, "x1t_full")

                def project(n, c):
                    if c == 0:
                        need(pe, s["x1t_ready"], n.before(1, 1))
                        if has(n + -4, nb):
                            need(pe, s["locb_ready"], (n + -3).before(1))
                            need(pe, s["fill_ready"], (n + -3).before(1))
                        else:
                            need(pe, s["qk_copied"], n.before(4))
                    else:
                        need(pe, s["qk_copied"], n.before(4, 2))
                    w = (wqa, wka)[c]
                    for m in range(2):
                        for dk in range(2):
                            mm = pe.matmul(t_ps[:, m * 256:m * 256 + 256], w[:, dk, m * P:m * P + P], x1_t[n.par][:, dk, :],
                                           start=(dk == 0), stop=(dk == 1))
                    mm.then_inc(s["qk_full"], 1)

                def project_v(n):
                    need(pe, s["mt_ready"], n.before(1))
                    for lt in range(2):
                        for dk in range(2):
                            mm = pe.matmul(b_ps[:, lt * 256:lt * 256 + 256], x1_t[n.par][:, dk, lt * P:lt * P + P], wva[:, dk, :],
                                           start=(dk == 0), stop=(dk == 1))
                    mm.then_inc(s["v_full"], 1)

                def max_scores(n, h):
                    b = n.par
                    if h == 0:
                        pe.wait_ge(stack_in[b], n.landed(16 * STACK_DMAS))
                        need(pe, s["v_ready"], n.before(1, 1))
                    else:
                        need(pe, s["mx_ready"], n.before(nh, h))
                    for lt in range(2):
                        mm = pe.matmul(b_ps[:, lt * 256:lt * 256 + 256], q_stack[b][0:SROWS, slot(h), lt * P:lt * P + P],
                                       k_stack[b][0:SROWS, slot(h), :], start=True, stop=True)
                    mm.then_inc(s["mx_full"], 1)

                def max_transposed(n):
                    need_alone(pe, passed["pe"], s["mparts_ready"], n.before(1, 1))
                    for lt in range(2):
                        mm = pe.transpose(b_bf[0:NPART * nh, lt * P:lt * P + P],
                                          mparts[:, lt, :, :].rearrange("p a h -> p (a h)"), identb[:, :])
                    mm.then_inc(s["mt_full"], 1)

                def scores(n, pair, ps, nrows, bank_sem, full):
                    b = n.par
                    need(pe, s[bank_sem], n.before(8, pair))
                    if nrows > SROWS and pair == 0:
                        pe.wait_ge(maxrow_in[b], n.landed(16 * NPART))
                    if nrows == SROWS and pair == 0:
                        pe.wait_ge(stack_in[b], n.landed(16 * STACK_DMAS))
                    for j in range(2):
                        for mt in range(2):
                            mm = pe.matmul(ps[:, j, mt, :], k_stack[b][0:nrows, slot(2 * pair + j), mt * P:mt * P + P],
                                           q_stack[b][0:nrows, slot(2 * pair + j), :], start=True, stop=True)
                    mm.then_inc(s[full], 1)

                def weighted(n, t, kind):
                    if kind == 0:
                        need(pe, s["p_ready"], n.before(8, 2 * t + 2))
                        need(pe, s["v_ready"], n.before(1, 1))
                        need(pe, s["nt_ready"], n.before(4, t))
                    else:
                        need(pe, s["g_ready"], n.before(8, 2 * t + 2))
                    w = (p_sb, g_sb)[kind][t % 2]
                    for mt in range(2):
                        for q in range(4):
                            mm = pe.matmul(pv_ps[32 * q:32 * q + 32, kind * 256:kind * 256 + 256],
                                           v_sb[n.par][:, mt, 4 * t + q, :], w[:, q, mt, :],
                                           start=(mt == 0), stop=(mt == 1))
                    if kind == 1:
                        mm.then_inc(s["pv_full"], 1)

                def weighted_transposed(n, t):
                    need(pe, s["f_ready"], n.before(4, t + 1))
                    for lt in range(2):
                        for kind in range(2):
                            mm = pe.transpose(pv_ps[:, (lt * 2 + kind) * P:(lt * 2 + kind) * P + P],
                                              f_sb[:, kind * 256 + lt * P:kind * 256 + lt * P + P], ident[:, :])
                    mm.then_inc(s["tr_full"], 1)

                def f_transposed(n):
                    need(pe, s["fn_ready"], n.before(4, 4))
                    if has(n + 3, nb):
                        need(pe, s["qk_copied"], (n + 3).before(4, 4))
                    else:
                        need(pe, s["locb_ready"], n.before(1))
                        need(pe, s["fill_ready"], n.before(1))
                    transposed(n, f_n, t_ps, "ft_full")

                def y_proj(n, lt):
                    if lt == 0:
                        need(pe, s["ft_ready"], n.before(1, 1))
                    for dk in range(2):
                        mm = pe.matmul(t_ps[:, lt * 256:lt * 256 + 256], f_t[:, dk, lt * P:lt * P + P], woa[:, dk, :],
                                       start=(dk == 0), stop=(dk == 1))
                    if lt == 1:
                        mm.then_inc(s["y_full"], 1)

                def x2_transposed(n):
                    need(pe, s["x2_ready"], n.before(2, 2))
                    transposed(n, x2[n.par], t_ps, "x2t_full")

                def logits(n):
                    need(pe, s["x2t_ready"], n.before(1, 1))
                    for lt in range(2):
                        for dk in range(2):
                            mm = pe.matmul(t_ps[:, lt * ne:lt * ne + ne], x2_t[:, dk, lt * P:lt * P + P], wg_sb[:, dk, :],
                                           start=(dk == 0), stop=(dk == 1))
                    mm.then_inc(s["lg_full"], 1)

                def positions(n):
                    need(pe, s["hot_ready"], n.before(1, 1))
                    c = 2 * ne
                    h0 = hot[:, 0, :, :].rearrange("p c e -> p (c e)")
                    h1_ = hot[:, 1, :, :].rearrange("p c e -> p (c e)")
                    pe.matmul(t_ps[:, 0:c], before_b[:, :], h0, start=True, stop=True)
                    pe.matmul(t_ps[:, c:2 * c], before_b[:, :], h1_, start=True, stop=False)
                    pe.matmul(t_ps[:, c:2 * c], ones_b[:, :], h0, start=False, stop=True)
                    pe.matmul(t_ps[:, 2 * c:3 * c], ones_b[:, :], h0, start=True, stop=False)
                    pe.matmul(t_ps[:, 2 * c:3 * c], ones_b[:, :], h1_, start=False, stop=True).then_inc(s["lc_full"], 1)

                def step(i, nb):
                    A, B, X, M, C, D = (has(i + d, nb) for d in (3, 2, 1, 0, -1, -2))

                    def maxima(*heads):
                        for h in heads:
                            if X:
                                max_scores(i + 1, h)

                    def raw(pair):
                        if M:
                            scores(i, pair, raw_ps, SROWS, "z_ready", "raw_full")

                    def raw_ahead():
                        if X:
                            scores(i + 1, 0, raw_ps, SROWS, "z_ready", "raw_full")

                    def shifted(pair):
                        if M:
                            scores(i, pair, sh_ps, SROWS + NPART, "p_ready", "sh_full")

                    def on(there, d, what, *args):
                        if there:
                            what(i + d, *args)

                    on(C, -1, weighted_transposed, 2)
                    on(X, 1, project_v)
                    on(D, -2, x2_transposed)
                    raw(1)
                    shifted(0)
                    on(A, 3, kv, 0)
                    on(C, -1, weighted, 3, 0)
                    on(C, -1, weighted, 3, 1)
                    on(D, -2, logits)
                    on(C, -1, weighted_transposed, 3)
                    on(B, 2, x1_transposed)
                    raw(2)
                    shifted(1)
                    maxima(0)
                    shifted(2)
                    on(A, 3, kv, 1)
                    maxima(1)
                    on(D, -2, positions)
                    maxima(2)
                    on(B, 2, project, 0)
                    raw(3)
                    maxima(3)
                    on(A, 3, q_tok)
                    maxima(4)
                    on(B, 2, project, 1)
                    shifted(3)
                    maxima(5)
                    on(A, 3, den, 0)
                    on(A, 3, den, 1)
                    raw(4)
                    on(M, 0, weighted, 0, 0)
                    maxima(6)
                    on(M, 0, weighted, 0, 1)
                    maxima(7)
                    on(C, -1, f_transposed)
                    shifted(4)
                    maxima(8)
                    on(M, 0, weighted_transposed, 0)
                    on(C, -1, y_proj, 0)
                    raw(5)
                    maxima(9)
                    on(C, -1, y_proj, 1)
                    maxima(10)
                    on(A, 3, num, 0)
                    shifted(5)
                    maxima(11)
                    on(A, 3, num, 1)
                    raw(6)
                    on(M, 0, weighted, 1, 0)
                    maxima(12)
                    on(M, 0, weighted, 1, 1)
                    maxima(13)
                    shifted(6)
                    raw(7)
                    maxima(14)
                    on(M, 0, weighted_transposed, 1)
                    on(A, 3, mix_out, 0)
                    maxima(15)
                    on(A, 3, mix_out, 1)
                    on(X, 1, max_transposed)
                    shifted(7)
                    on(M, 0, weighted, 2, 0)
                    raw_ahead()
                    on(M, 0, weighted, 2, 1)

                turns(pe, nb, step)

            @block.scalar
            def _(act):
                def ek_tile(n, lt):
                    need(act, s["kv_full"], n.before(2, lt + 1))
                    if lt == 0:
                        need(act, s["den_full"], n.before(1))
                    kvv = a_ps[:, :].rearrange("p (h k d) -> p h k d", h=4, k=2)
                    act.activation(ek[:, lt, :].rearrange("p (h d) -> p h d", h=4), kvv[:, :, 0, :], ACT.Exp)\
                        .then_inc(s["ek_ready"], 1)

                def exp_minus_q(n):
                    need(act, s["q_full"], n.before(1, 1))
                    need(act, s["dn_ready"], n.before(1))
                    act.activation(eq[:, :, :].rearrange("p m t -> p (m t)"), a_ps[:, :], ACT.Exp, scale=-1.0)\
                        .then_inc(s["eq_ready"], 1)

                def rsqrt(n, k, used, per):
                    need(act, s[f"ag{k}"], n.before(2, 2))
                    act.activation(lnv[k][:, :], mv[k][:, :, 1], ACT.Ln, bias=eps[:, 0:1]).then_inc(s[f"lv{k}"], 1)
                    need(act, s[f"lv{k}"], n.before(1, 1))
                    need(act, s[used], n.before(per))
                    act.activation(rs[k][:, :], lnv[k][:, :], ACT.Exp, scale=-0.5).then_inc(s[f"rs{k}"], 1)

                def copy_out(n, ps, dst, full, ready, used):
                    need(act, s[full], n.before(1, 1))
                    for sem_name, back in used:
                        need(act, s[sem_name], (n + back).before(1))
                    act.activation(dst[:, :, :].rearrange("p a n -> p (a n)"), ps[:, :], ACT.Copy).then_inc(s[ready], 1)

                def reciprocal(n):
                    need(act, s["dn_ready"], n.before(1, 1))
                    act.activation(dn[:, :, :], dn[:, :, :], ACT.Ln).then_inc(s["ldn_ready"], 1)
                    need(act, s["ldn_ready"], n.before(1, 1))
                    need(act, s["yt_ready"], n.before(1))
                    act.activation(rec[:, :, :], dn[:, :, :], ACT.Exp, scale=-1.0).then_inc(s["rec_ready"], 1)

                def qk_bias(n, c):
                    need(act, s["qk_full"], n.before(2, c + 1))
                    if c == 0:
                        need(act, s["part_h"], n.before(1))
                        need(act, s["part_r"], n.before(1))
                    for m in range(2):
                        act.activation(qkf[:, 2 * c + m, :], t_ps[:, m * 256:m * 256 + 256], ACT.Identity,
                                       bias=bqk[:, 2 * c + m:2 * c + m + 1]).then_inc(s["qk_copied"], 1)

                def maxrow_copy(n):
                    need(act, s["mt_full"], n.before(1, 1))
                    if has(n + -1, nb):
                        act.wait_ge(maxrow_in[(n.par + 1) % 2], (n + -1).landed(16 * NPART))
                    act.activation(mrow[:, :], b_bf[0:NPART * nh, 0:ltok], ACT.Copy).then_inc(s["mt_ready"], 1)

                def softmax_weights(n, pair):
                    need(act, s["sh_full"], n.before(8, pair + 1))
                    if pair % 2 == 0:
                        need(act, s["pv_full"], n.before(4, pair // 2 - 1))
                    dst = p_sb[(pair // 2) % 2][:, 2 * (pair % 2):2 * (pair % 2) + 2, :, :]
                    act.activation(dst.rearrange("p j m n -> p (j m n)"), sh_ps[:, :, :, :].rearrange("p j m n -> p (j m n)"),
                                   ACT.Exp, scale=SC).then_inc(s["p_ready"], 1)

                def cauchy_weights(n, pair):
                    b, h = pair % 2, 2 * pair
                    need(act, s["z_ready"], n.before(8, pair + 1))
                    need(act, s["g_ready"], n.before(8, pair - 1))
                    act.activation(u_sb[b][:, 0, :], z_sb[b][:, 0, :], ACT.Square, bias=b4[:, h:h + 1])\
                        .then_inc(s["sq_ready"], 1)
                    need(act, s["u_pool"], n.before(8, pair + 1))
                    act.activation(u_sb[b][:, 1, :], u_sb[b][:, 1, :], ACT.Ln, bias=c16[:, h + 1:h + 2])\
                        .then_inc(s["l_ready"], 1)
                    need(act, s["sq_ready"], n.before(8, pair + 1))
                    act.activation(u_sb[b][:, 0, :], u_sb[b][:, 0, :], ACT.Ln, bias=c16t[:, h:h + 1])\
                        .then_inc(s["l_ready"], 1)
                    need(act, s["l_ready"], n.before(16, 2 * pair + 2))
                    if pair % 2 == 0:
                        need(act, s["pv_full"], n.before(4, pair // 2 - 1))
                    dst = g_sb[(pair // 2) % 2][:, 2 * (pair % 2):2 * (pair % 2) + 2, :, :]
                    act.activation(dst.rearrange("p j m n -> p (j m n)"), u_sb[b][:, :, :].rearrange("p j n -> p (j n)"),
                                   ACT.Exp, scale=-1.0).then_inc(s["g_ready"], 1)

                def weighted_copy(n, t):
                    need(act, s["pv_full"], n.before(4, t + 1))
                    need(act, s["tr_full"], n.before(4, t))
                    act.activation(f_sb[:, :], pv_ps[:, :], ACT.Copy).then_inc(s["f_ready"], 1)

                def step(i, nb):
                    A, B, X, M, C, D = (has(i + d, nb) for d in (3, 2, 1, 0, -1, -2))

                    def on(there, d, what, *args):
                        if there:
                            what(i + d, *args)

                    on(C, -1, cauchy_weights, 7)
                    on(A, 3, ek_tile, 0)
                    on(M, 0, softmax_weights, 0)
                    if D:
                        copy_out(i + -2, t_ps, x2_t, "x2t_full", "x2t_ready", (("lg_full", 0),))
                    on(B, 2, rsqrt, 1, "x1_ready", 2)
                    on(C, -1, weighted_copy, 3)
                    if B:
                        copy_out(i + 2, a_ps, x1_t[i.par], "x1t_full", "x1t_ready", (("v_full", -1),))
                    on(M, 0, softmax_weights, 1)
                    on(M, 0, cauchy_weights, 0)
                    on(M, 0, softmax_weights, 2)
                    on(A, 3, ek_tile, 1)
                    on(M, 0, cauchy_weights, 1)
                    on(B, 2, qk_bias, 0)
                    on(A, 3, exp_minus_q)
                    on(M, 0, softmax_weights, 3)
                    on(B, 2, qk_bias, 1)
                    on(M, 0, cauchy_weights, 2)
                    on(M, 0, weighted_copy, 0)
                    on(M, 0, softmax_weights, 4)
                    if C:
                        copy_out(i + -1, t_ps, f_t, "ft_full", "ft_ready", (("y_full", 0),))
                    on(M, 0, cauchy_weights, 3)
                    on(A, 3, reciprocal)
                    on(M, 0, softmax_weights, 5)
                    on(M, 0, cauchy_weights, 4)
                    on(C, -1, rsqrt, 2, "yn_ready", 2)
                    on(M, 0, weighted_copy, 1)
                    on(M, 0, softmax_weights, 6)
                    on(M, 0, cauchy_weights, 5)
                    on(X, 1, maxrow_copy)
                    on(M, 0, softmax_weights, 7)
                    on(A, 3, rsqrt, 0, "hn_ready", 2)
                    on(M, 0, weighted_copy, 2)
                    on(C, -1, rsqrt, 3, "x2_ready", 2)
                    on(M, 0, cauchy_weights, 6)

                nc.scalar.preload_act_table_set("natural_log_exp_and_others")
                turns(act, nb, step)

            @block.vector
            def _(dve):
                def ekv_tile(n, lt):
                    need(dve, s["ek_ready"], n.before(2, lt + 1))
                    if lt == 0:
                        need(dve, s["num_full"], n.before(1))
                    kvv = a_ps[:, :].rearrange("p (h k d) -> p h k d", h=4, k=2)
                    dve.tensor_tensor(ekv[:, lt, :].rearrange("p (h d) -> p h d", h=4), kvv[:, :, 1, :],
                                      ek[:, lt, :].rearrange("p (h d) -> p h d", h=4), ALU.mult).then_inc(s["ekv_ready"], 1)

                def fold(t):
                    return t[:, :, :].rearrange("p a n -> p (a n)")

                def denominators(n):
                    need(dve, s["den_full"], n.before(1, 1))
                    need(dve, s["rec_ready"], n.before(1))
                    dve.scalar_tensor_tensor(out=fold(dn), in0=fold(eq), scalar=1.0, in1=a_ps[:, :],
                                             op0=ALU.add, op1=ALU.mult).then_inc(s["dn_ready"], 1)

                def mixed_values(n):
                    need(dve, s["rec_ready"], n.before(1, 1))
                    need(dve, s["num_full"], n.before(1, 1))
                    need(dve, s["mix_full"], n.before(1))
                    dve.tensor_tensor(fold(y_t), a_ps[:, :], fold(rec), ALU.mult).then_inc(s["yt_ready"], 1)

                def stats(n, k, src, ready, per, incs):
                    need(dve, s[ready], n.before(per, incs))
                    for lt in range(2):
                        dve.bn_stats(stat[k][:, lt, :], src(lt)).then_inc(s[f"st{k}"], 1)
                    need(dve, s[f"lv{k}"], n.before(1))
                    for lt in range(2):
                        need_alone(dve, passed["dve"], s[f"st{k}"], n.before(2, lt + 1))
                        dve.bn_aggr(mv[k][:, lt, :], stat[k][:, lt, :]).then_inc(s[f"ag{k}"], 1)

                def normalise(n, k, src, dst, ready, used):
                    need(dve, s[f"rs{k}"], n.before(1, 1))
                    for f in used:
                        need(dve, s[f], n.before(1))
                    for lt in range(2):
                        dve.tensor_scalar(dst[:, lt, :], src(lt), mv[k][:, lt, 0:1], rs[k][:, lt:lt + 1],
                                          ALU.subtract, ALU.mult).then_inc(s[ready], 1)

                def a_half(lt):
                    return a_ps[:, lt * 256:lt * 256 + 256]

                def part_high(n):
                    need(dve, s["qk_copied"], n.before(4, 4))
                    if has(n + -1, nb):
                        dve.wait_ge(qk_out[(n.par + 1) % 2], (n + -1).landed(16 * SPLIT_DMAS))
                    dve.tensor_copy(qkp[:, 0, :, :], qkf[:, :, :]).then_inc(s["part_h"], 1)

                def part_mid(n):
                    need(dve, s["part_r"], n.before(1, 1))
                    dve.tensor_copy(qkp[:, 1, :, :], qkr[:, :, :]).then_inc(s["part_m"], 1)

                def v_bias(n):
                    need(dve, s["v_full"], n.before(1, 1))
                    need(dve, s["pv_full"], (n + -1).before(4))
                    for_v = rows["bv"][:, :].rearrange("p (a h d) -> p a h d", a=1, d=dh).broadcast_to((P, 2, nh, dh))
                    dve.tensor_tensor(v_sb[n.par][:, :, :, 0:dh], b_ps[:, :].rearrange("p (l h d) -> p l h d", l=2, d=dh),
                                      for_v, ALU.add).then_inc(s["v_ready"], 1)

                def head_max(n, h):
                    need(dve, s["mx_full"], n.before(nh, h + 1))
                    if h == 0:
                        need(dve, s["nm_neg"], n.before(1))
                    dve.tensor_reduce(rmax[:, slot(h), :], b_ps[:, :].rearrange("p (l m) -> p l m", l=2), AX, ALU.max)\
                        .then_inc(s["mx_ready"], 1)

                def max_parts(n):
                    def part(k):
                        return mparts[:, :, k, :].rearrange("p l h -> p h l")
                    need(dve, s["mx_ready"], n.before(nh, nh))
                    need(dve, s["mparts_ready"], n.before(1))
                    dve.tensor_scalar(nmx[:, :, :], rmax[:, :, :], -1.0, None, ALU.mult).then_inc(s["nm_neg"], 1)
                    need(dve, s["nm_neg"], n.before(1, 1))
                    need(dve, s["mt_full"], n.before(1))
                    dve.tensor_copy(part(0), nmx[:, :, :]).then_inc(s["nm_h"], 1)
                    need(dve, s["nm_h"], n.before(1, 1))
                    dve.tensor_tensor(nmr[:, :, :], nmx[:, :, :], part(0), ALU.subtract).then_inc(s["nm_r"], 1)
                    need(dve, s["nm_r"], n.before(1, 1))
                    dve.tensor_copy(part(1), nmr[:, :, :]).then_inc(s["nm_m"], 1)
                    need(dve, s["nm_m"], n.before(1, 1))
                    dve.tensor_tensor(part(2), nmr[:, :, :], part(1), ALU.subtract).then_inc(s["mparts_ready"], 1)

                def magnitudes(n, pair):
                    b = pair % 2
                    need(dve, s["raw_full"], n.before(8, pair + 1))
                    need(dve, s["sq_ready"], n.before(8, pair - 1))
                    need(dve, s["u_pool"], n.before(8, pair - 1))
                    dve.tensor_scalar(z_sb[b][:, :, :].rearrange("p j n -> p (j n)").bitcast(I32),
                                      raw_ps[:, :, :, :].rearrange("p j m n -> p (j m n)").bitcast(I32),
                                      0x7FFFFFFF, None, ALU.bitwise_and).then_inc(s["z_ready"], 1)

                def norm_quad(n, t):
                    need(dve, s["tr_full"], n.before(4, t + 1))
                    need(dve, s["nt_ready"], n.before(4, t))
                    v = pv_ps[:, :].rearrange("p (g d) -> p g d", d=VW)
                    dve.reciprocal(rc[:, :], v[:, :, dh]).then_inc(s["rc_ready"], 1)
                    need(dve, s["rc_ready"], n.before(4, t + 1))
                    need(dve, s["fn_ready"], n.before(4, t))
                    dve.tensor_tensor(ntv[:, :, :, :, :].rearrange("p l k h d -> p (l k h) d"), v[:, :, 0:dh],
                                      rc[:, :].rearrange("p (g a) -> p g a", a=1).broadcast_to((P, 16, dh)), ALU.mult)\
                        .then_inc(s["nt_ready"], 1)
                    need(dve, s["nt_ready"], n.before(4, t + 1))
                    if t == 0:
                        need(dve, s["ft_full"], n.before(1))
                    nv = ntv[:, :, :, :, :].rearrange("p l k h d -> p l k (h d)")
                    dve.tensor_tensor(f_n[:, :, t * 64:t * 64 + 64], nv[:, :, 0, :], nv[:, :, 1, :], ALU.add)\
                        .then_inc(s["fn_ready"], 1)

                def y_bias(n):
                    need(dve, s["y_full"], n.before(1, 1))
                    dve.tensor_tensor(yb[:, :, :], t_ps[:, :].rearrange("p (l d) -> p l d", l=2),
                                      rows["bo"][:, :].rearrange("p (a d) -> p a d", a=1).broadcast_to((P, 2, dm)), ALU.add)\
                        .then_inc(s["yb_ready"], 1)

                def choose(n):
                    need(dve, s["lg_full"], n.before(1, 1))
                    dve.tensor_copy(fold(lgt), t_ps[:, 0:2 * ne]).then_inc(s["lg_copied"], 1)
                    need(dve, s["lg_copied"], n.before(1, 1))
                    dve.tensor_copy(logits_all[:, dyn(n, 2), :], lgt[:, :, :]).then_inc(s["lg_kept"], 1)
                    for lt in range(2):
                        need_alone(dve, passed["dve"], s["idx_ready"], n.before(2))
                        dve.max(top8[:, lt, :], lgt[:, lt, :]).then_inc(s["top_ready"], 1)
                    for lt in range(2):
                        need_alone(dve, passed["dve"], s["top_ready"], n.before(2, lt + 1))
                        dve.max_index(idx8[:, lt, :], top8[:, lt, :], lgt[:, lt, :]).then_inc(s["idx_ready"], 1)
                    need(dve, s["idx_ready"], n.before(2, 2))
                    dve.tensor_copy(top_all[:, dyn(n, 2), :], top8[:, :, 0:2]).then_inc(s["kept"], 1)
                    dve.tensor_copy(idxf[:, :, :], idx8[:, :, 0:2]).then_inc(s["idxf_ready"], 1)
                    need(dve, s["idxf_ready"], n.before(1, 1))
                    dve.tensor_copy(expert_all[:, dyn(n, 2), :], idxf[:, :, :]).then_inc(s["kept"], 1)
                    dve.tensor_tensor(hot[:, :, :, :].rearrange("p l c e -> p (l c) e"),
                                      idxf[:, :, :].rearrange("p l (c a) -> p (l c) a", a=1).broadcast_to((P, 4, ne)),
                                      iota_e[:, :].rearrange("p (a e) -> p a e", a=1).broadcast_to((P, 4, ne)), ALU.is_equal)\
                        .then_inc(s["hot_ready"], 1)

                def count(n):
                    b, c = n.par, 2 * ne
                    need(dve, s["lc_full"], n.before(1, 1))
                    need(dve, s["fill_ready"], n.before(1))
                    run = filled[:, b, :, :].rearrange("p c e -> p (c e)")
                    dve.tensor_tensor(locb[:, :, :, :].rearrange("p l c e -> p l (c e)"),
                                      t_ps[:, 0:2 * c].rearrange("p (l k) -> p l k", l=2),
                                      run.rearrange("p (a k) -> p a k", a=1).broadcast_to((P, 2, c)), ALU.add)\
                        .then_inc(s["locb_ready"], 1)
                    dve.tensor_tensor(filled[:, 1 - b, :, :].rearrange("p c e -> p (c e)"), t_ps[:, 2 * c:3 * c], run, ALU.add)\
                        .then_inc(s["fill_ready"], 1)

                def place(n):
                    b = n.par
                    need(dve, s["locb_ready"], n.before(1, 1))
                    dve.tensor_tensor(lsel[:, :, :, :].rearrange("p l c e -> p (l c e)"),
                                      locb[:, :, :, :].rearrange("p l c e -> p (l c e)"),
                                      hot[:, :, :, :].rearrange("p l c e -> p (l c e)"), ALU.mult).then_inc(s["lsel_ready"], 1)
                    need(dve, s["lsel_ready"], n.before(1, 1))
                    dve.tensor_reduce(loc[:, :, :].rearrange("p l c -> p (l c)"),
                                      lsel[:, :, :, :].rearrange("p l c e -> p (l c) e"), AX, ALU.add).then_inc(s["loc_ready"], 1)
                    need(dve, s["loc_ready"], n.before(1, 1))
                    dve.tensor_copy(place_all[:, dyn(n, 2), :], loc[:, :, :]).then_inc(s["kept"], 1)
                    dve.tensor_scalar(fold(over), fold(loc), float(cap), float(4 * ne * cap), ALU.is_ge, ALU.mult)\
                        .then_inc(s["over_ready"], 1)
                    dve.scalar_tensor_tensor(out=fold(flat), in0=fold(idxf), scalar=float(2 * cap), in1=fold(loc),
                                             op0=ALU.mult, op1=ALU.add).then_inc(s["flat_ready"], 1)
                    need(dve, s["over_ready"], n.before(1, 1))
                    need(dve, s["flat_ready"], n.before(1, 1))
                    dve.tensor_tensor(fold(flat2), fold(flat), fold(over), ALU.add).then_inc(s["flat2_ready"], 1)
                    need(dve, s["flat2_ready"], n.before(1, 1))
                    if has(n + -2, nb):
                        dve.wait_ge(scat_out[b], (n + -2).landed(64))
                    dve.tensor_copy(slot_u[b][:, :], fold(flat2)).then_inc(s["slot_ready"], 1)
                    dve.tensor_copy(tok_u[b][:, :], tok_ids[:, dyn(n, 2)]).then_inc(s["slot_ready"], 1)

                def step(i, nb):
                    A, B, X, M, C, D = (has(i + d, nb) for d in (3, 2, 1, 0, -1, -2))
                    last = (i.par + 1) % 2

                    def maxima(*heads):
                        for h in heads:
                            if X:
                                head_max(i + 1, h)

                    def on(there, d, what, *args):
                        if there:
                            what(i + d, *args)

                    on(M, 0, magnitudes, 0)
                    on(C, -1, norm_quad, 2)
                    on(M, 0, magnitudes, 1)
                    on(A, 3, ekv_tile, 0)
                    on(B, 2, stats, 1, lambda lt: h1[:, lt, :], "h1_ready", 1, 1)
                    if B:
                        normalise(i + 2, 1, lambda lt: h1[:, lt, :], x1, "x1_ready", ("hx0_ready", "x1t_full"))

                    on(X, 1, v_bias)
                    on(C, -1, norm_quad, 3)
                    on(D, -2, choose)
                    maxima(0)

                    on(M, 0, magnitudes, 2)
                    maxima(1)
                    on(D, -2, count)
                    on(A, 3, ekv_tile, 1)
                    maxima(2, 3)

                    on(M, 0, magnitudes, 3)
                    maxima(4)
                    maxima(5)
                    on(D, -2, place)
                    on(B, 2, part_high)
                    maxima(6)

                    on(M, 0, magnitudes, 4)
                    on(A, 3, denominators)
                    maxima(7)
                    maxima(8)
                    on(M, 0, norm_quad, 0)
                    maxima(9)

                    on(M, 0, magnitudes, 5)
                    maxima(10)
                    on(C, -1, y_bias)
                    maxima(11)
                    if C:
                        stats(i + -1, 2, lambda lt: yb[:, lt, :], "yb_ready", 1, 1)
                    on(B, 2, part_mid)
                    maxima(12)

                    on(M, 0, magnitudes, 6)
                    maxima(13)
                    on(A, 3, mixed_values)
                    maxima(14)
                    if C:
                        normalise(i + -1, 2, lambda lt: yb[:, lt, :], yn, "yn_ready", ("yw_ready",))
                    on(M, 0, norm_quad, 1)
                    maxima(15)
                    on(X, 1, max_parts)

                    on(M, 0, magnitudes, 7)
                    on(A, 3, stats, 0, a_half, "mix_full", 1, 1)
                    if C:
                        stats(i + -1, 3, lambda lt: h2[last][:, lt, :], "h2_ready", 1, 1)
                    on(A, 3, normalise, 0, a_half, hn, "hn_ready", ("hg_ready",))
                    if C:
                        if has(i + -3, nb):
                            dve.wait_ge(x2_out[last], (i + -3).landed())
                        normalise(i + -1, 3, lambda lt: h2[last][:, lt, :], x2[last], "x2_ready", ("x2t_full",))

                turns(dve, nb, step)

            @block.gpsimd
            def _(pool):
                def over_rows(dst, a, row):
                    r = rows[row][:, :].rearrange("p (a d) -> p a d", a=1).broadcast_to((P, 2, dm))
                    return a[:, :, :], r

                def scale_row(n, dst, src, row, op, ready, per, k, done, free=()):
                    need_alone(pool, passed["pool"], s[ready], n.before(per, k))
                    for f in free:
                        need_alone(pool, passed["pool"], s[f], n.before(1))
                    a, r = over_rows(dst, src, row)
                    pool.tensor_tensor(dst[:, :, :], a, r, op).then_inc(s[done], 1)

                def sum_rows(n, dst, a, b_, done):
                    pool.tensor_tensor(dst[:, :, :], a[:, :, :], b_[:, :, :], ALU.add).then_inc(s[done], 1)

                def mixer_norm(n):
                    scale_row(n, hg, hn, "ln_g", ALU.mult, "hn_ready", 2, 2, "hg_ready", ("h1_ready",))
                    need_alone(pool, passed["pool"], s["x1_ready"], n.before(2))
                    scale_row(n, h1, hg, "ln_b", ALU.add, "hg_ready", 1, 1, "h1_ready", ("hx0_ready",))

                def residual(n, b):
                    need_alone(pool, passed["pool"], s["x1_ready"], n.before(2, 2))
                    need_alone(pool, passed["pool"], s["hx_ready"], n.before(1))
                    sum_rows(n, hx0, h1, x1, "hx0_ready")
                    need_alone(pool, passed["pool"], s["h2_ready"], (n + -3).before(1) if has(n + -4, nb) else 0)
                    scale_row(n, hx[b], hx0, "ln_b2", ALU.add, "hx0_ready", 1, 1, "hx_ready")

                def remainder(n):
                    need_alone(pool, passed["pool"], s["part_h"], n.before(1, 1))
                    need_alone(pool, passed["pool"], s["part_l"], n.before(1))
                    pool.tensor_tensor(qkr[:, :, :], qkf[:, :, :], qkp[:, 0, :, :], ALU.subtract).then_inc(s["part_r"], 1)

                def part_low(n):
                    need_alone(pool, passed["pool"], s["part_m"], n.before(1, 1))
                    if has(n + -1, nb):
                        need_alone(pool, passed["pool"], qk_out[(n.par + 1) % 2], (n + -1).landed(16 * SPLIT_DMAS))
                    pool.tensor_tensor(qkp[:, 2, :, :], qkr[:, :, :], qkp[:, 1, :, :], ALU.subtract).then_inc(s["part_l"], 1)

                def polynomial(n, pair):
                    b, h = pair % 2, 2 * pair + 1
                    need_alone(pool, passed["pool"], s["z_ready"], n.before(8, pair + 1))
                    need_alone(pool, passed["pool"], s["u_pool"], n.before(8, pair))
                    pool.tensor_tensor(zb[:, :], z_sb[b][:, 1, :], b8[:, h:h + 1].broadcast_to((P, 512)), ALU.add)\
                        .then_inc(s["zb_ready"], 1)
                    need_alone(pool, passed["pool"], s["zb_ready"], n.before(8, pair + 1))
                    need_alone(pool, passed["pool"], s["g_ready"], n.before(8, pair - 1))
                    pool.tensor_tensor(u_sb[b][:, 1, :], zb[:, :], z_sb[b][:, 1, :], ALU.mult).then_inc(s["u_pool"], 1)

                def attention_norm(n, b):
                    scale_row(n, yw, yn, "ln_w", ALU.mult, "yn_ready", 2, 2, "yw_ready", ("h2_ready",))
                    need_alone(pool, passed["pool"], s["yw_ready"], n.before(1, 1))
                    need_alone(pool, passed["pool"], s["x2_ready"], (n + -1).before(2) if has(n + -2, nb) else 0)
                    if has(n + -2, nb):
                        need_alone(pool, passed["pool"], h2_out[n.par], (n + -2).landed())
                    sum_rows(n, h2[n.par], yw, hx[b], "h2_ready")

                def scatter(n):
                    b = n.par
                    need_alone(pool, passed["pool"], s["slot_ready"], n.before(2, 2))
                    for lt in range(2):
                        for c in range(2):
                            pool.indirect_dma_start(
                                out=slot_dram[c], out_offset=bass.IndirectOffsetOnAxis(ap=slot_u[b][:, 2 * lt + c:2 * lt + c + 1], axis=0),
                                in_=tok_u[b][:, lt:lt + 1], in_offset=None,
                                bounds_check=2 * ne * cap - 1, oob_is_err=False).then_inc(scat_out[b], 16)

                def step4(i, nb, ring):
                    A, B, M, C, D = (has(i + d, nb) for d in (3, 2, 0, -1, -2))
                    for pair in range(nh // 2):
                        if M:
                            polynomial(i, pair)
                        if pair == 0 and B:
                            residual(i + 2, (ring + 2) % 4)
                        if pair == 3 and B:
                            remainder(i + 2)
                        if pair == 4 and D:
                            scatter(i + -2)
                        if pair == 5 and B:
                            part_low(i + 2)
                        if pair == 6 and C:
                            attention_norm(i + -1, (ring + 3) % 4)
                        if pair == 7 and A:
                            mixer_norm(i + 3)

                pool_turns(pool, nb, step4)
                for b in range(2):
                    pool.wait_ge(scat_out[b], 64 * (nb // 2))


def finish_routes(nc, g):
    ne, cap, tiles = g["ne"], g["cap"], g["tiles"]
    filled, iota_e = g["filled"], g["iota_e"]
    logits_all, top_all, expert_all, place_all = (g[k] for k in ("logits_all", "top_all", "expert_all", "place_all"))
    routes, gates, slot_tok, slot_dram = g["routes"], g["gates"], g["slot_tok"], g["slot_dram"]
    with ExitStack() as ctx:
        def sb(name, shape, dt=F32):
            return ctx.enter_context(nc.sbuf_tensor(name, shape, dt))

        def sem(name):
            return ctx.enter_context(nc.semaphore(name))

        big = [sb(f"big{b}", [P, tiles, ne]) for b in range(2)]
        soft = sb("soft", [P, tiles, ne])
        n1f = sb("n1f", [P, ne])
        n1i = sb("n1i", [P, ne], I32)
        col = {k: sb(f"col_{k}", [P, tiles]) for k in "off pos kept0 kept1 posm row z rz d2 e2 g2 sum rd w".split()}
        r_chain = sem("r_chain")
        r_counts = sem("r_counts")
        r_shift = sem("r_shift")
        r_exp = sem("r_exp")
        r_joined = sem("r_joined")
        r_table = sem("r_table")
        n1 = filled[:, 0, 0, :]

        def wide(a):
            return a.rearrange("p (t a) -> p t a", a=1).broadcast_to((P, tiles, ne))

        def tall(a):
            return a.rearrange("p (a e) -> p a e", a=1).broadcast_to((P, tiles, ne))

        with nc.Block() as block:
            @block.vector
            def _(dve):
                count = [0]

                def link(ins):
                    count[0] += 1
                    ins.then_inc(r_chain, 1)
                    dve.wait_ge(r_chain, count[0])

                link(dve.tensor_scalar(n1f[:, :], n1, float(cap), None, ALU.min))
                dve.tensor_copy(n1i[:, :], n1f[:, :]).then_inc(r_counts, 1)
                dve.tensor_tensor(soft[:, :, :], logits_all[:, :, :], wide(top_all[:, :, 0]), ALU.subtract).then_inc(r_shift, 1)
                dve.tensor_tensor(col["d2"][:, :], top_all[:, :, 1], top_all[:, :, 0], ALU.subtract).then_inc(r_shift, 1)
                link(dve.tensor_tensor(big[0][:, :, :], wide(expert_all[:, :, 1]), tall(iota_e[:, :]), ALU.is_equal))
                link(dve.tensor_tensor(big[1][:, :, :], big[0][:, :, :], tall(n1), ALU.mult))
                link(dve.tensor_reduce(col["off"][:, :], big[1][:, :, :], AX, ALU.add))
                link(dve.tensor_tensor(place_all[:, :, 1], place_all[:, :, 1], col["off"][:, :], ALU.add))
                for c in range(2):
                    link(dve.tensor_scalar(col[f"kept{c}"][:, :], place_all[:, :, c], float(cap), None, ALU.is_lt))
                    link(dve.tensor_scalar(col["posm"][:, :], place_all[:, :, c], float(cap - 1), None, ALU.min))
                    link(dve.scalar_tensor_tensor(out=col["row"][:, :], in0=expert_all[:, :, c], scalar=float(cap),
                                                  in1=col["posm"][:, :], op0=ALU.mult, op1=ALU.add))
                    link(dve.tensor_copy(routes[:, c, :], col["row"][:, :]))
                dve.wait_ge(r_exp, 2)
                link(dve.tensor_reduce(col["z"][:, :], soft[:, :, :], AX, ALU.add))
                link(dve.reciprocal(col["rz"][:, :], col["z"][:, :]))
                link(dve.tensor_tensor(col["g2"][:, :], col["e2"][:, :], col["rz"][:, :], ALU.mult))
                link(dve.tensor_tensor(col["sum"][:, :], col["g2"][:, :], col["rz"][:, :], ALU.add))
                link(dve.tensor_scalar(col["w"][:, :], col["sum"][:, :], 1e-9, None, ALU.max))
                link(dve.reciprocal(col["rd"][:, :], col["w"][:, :]))
                for c, gate in enumerate((col["rz"], col["g2"])):
                    link(dve.tensor_tensor(col["sum"][:, :], gate[:, :], col["rd"][:, :], ALU.mult))
                    link(dve.tensor_tensor(gates[:, c, :], col["sum"][:, :], col[f"kept{c}"][:, :], ALU.mult))

            @block.scalar
            def _(act):
                act.wait_ge(r_shift, 2)
                act.activation(soft[:, :, :], soft[:, :, :], ACT.Exp).then_inc(r_exp, 1)
                act.activation(col["e2"][:, :], col["d2"][:, :], ACT.Exp).then_inc(r_exp, 1)

            @block.sync
            def _(sp):
                sp.wait_ge(r_counts, 1)
                for e in range(ne):
                    n = sp.value_load(n1i[0:1, e:e + 1], min_val=0, max_val=cap)
                    base = e * 2 * cap
                    sp.dma_start(slot_dram[0][bass.ds(n + base, cap), :].rearrange("(a m) o -> a (m o)", a=16),
                                 slot_dram[1][base:base + cap, :].rearrange("(a m) o -> a (m o)", a=16)).then_inc(r_joined, 16)
                sp.wait_ge(r_joined, 16 * ne)
                for e in range(ne):
                    base = e * 2 * cap
                    sp.dma_start(slot_tok[:, e, :], slot_dram[0][base:base + cap, :].rearrange("(p j) o -> p (j o)", p=P))\
                        .then_inc(r_table, 16)
                sp.wait_ge(r_table, 16 * ne)


def experts(nc, g):
    ne, cap, ff = g["ne"], g["cap"], g["ff"]
    x2_dram, w_experts = g["x2_dram"], g["w_experts"]
    ident, slot_tok = g["ident"], g["slot_tok"]
    gpe = cap // (4 * P)
    fts = ff // P
    pieces, width = w_experts.shape[2], w_experts.shape[3]
    eo_view = g["eo_dram"].rearrange("(e p j) d -> e p j d", e=ne, p=P)
    with ExitStack() as ctx:
        def sb(name, shape, dt=F32):
            return ctx.enter_context(nc.sbuf_tensor(name, shape, dt))

        def bank(name, shape, dt=F32):
            return ctx.enter_context(nc.psum_tensor(name, shape, dt))

        def sem(name):
            return ctx.enter_context(nc.semaphore(name))

        w_raw = [sb(f"w_raw{b}", [P, pieces, width]) for b in range(2)]
        w_hi = [sb(f"w_hi{b}", [P, pieces, width], F32R) for b in range(2)]
        w_lo = [sb(f"w_lo{b}", [P, pieces, width], F32R) for b in range(2)]
        idc = [sb(f"idc{b}", [P, 4], U32) for b in range(2)]
        xg = [sb(f"xg{b}", [P, 4, 256]) for b in range(2)]
        xt_hi = [sb(f"xt_hi{b}", [P, 2, 512], F32R) for b in range(2)]
        xt_lo = [sb(f"xt_lo{b}", [P, 2, 512], F32R) for b in range(2)]
        h_f = [sb(f"h_f{k}", [P, 512]) for k in range(2)]
        ht_hi = [sb(f"ht_hi{b}", [P, fts, 512], F32R) for b in range(2)]
        ht_lo = [sb(f"ht_lo{b}", [P, fts, 512], F32R) for b in range(2)]
        eo = [sb(f"eo{b}", [P, 4, 256]) for b in range(2)]
        tr_ps = [bank(f"tr_ps{k}", [P, 512]) for k in range(2)]
        h_ps = [bank(f"h_ps{k}", [P, 512]) for k in range(4)]
        o_ps = bank("o_ps", [P, 4, 256])
        w_in = [sem(f"w_in{b}") for b in range(2)]
        rows_in = g["rows_in"]
        eo_out = [sem(f"eo_out{b}") for b in range(2)]
        ids_ready = sem("ids_ready")
        xtr_full = sem("xtr_full")
        xt_hi_ready = sem("xt_hi_ready")
        xt_ready = sem("xt_ready")
        h_full = sem("h_full")
        gelu_ready = sem("gelu_ready")
        ht_hi_ready = sem("ht_hi_ready")
        ht_ready = sem("ht_ready")
        o_full = sem("o_full")
        eo_ready = sem("eo_ready")
        eo_free = sem("eo_free")
        w_hi_ready = sem("w_hi_ready")
        w_lo_ready = sem("w_lo_ready")
        passed = g["passed"]
        PER = {ids_ready: 1, xtr_full: 2, xt_hi_ready: 2, xt_ready: 2, h_full: fts, gelu_ready: fts,
               ht_hi_ready: fts, ht_ready: fts, o_full: 4, eo_ready: 2, eo_free: 1}

        class Group:

            def __init__(self, ep, par, gi, b, last=False):
                self.e, self.par, self.b, self.last = ep * 2 + par, par, b, last
                self.piece = gi * 2 + b
                self.j = gi * 8 + b * 4
                self.ep, self.gi = ep, gi

            def number(self, mul, add=0):
                return self.ep * (2 * gpe * mul) + self.gi * (2 * mul) + ((self.par * gpe + self.b) * mul + add)

            def past(self, sem_, k=0):
                per = PER[sem_]
                return self.number(per, 2 * per + k)

            def landed(self, per, extra=0):
                return self.ep * (gpe * per) + self.gi * per + (self.par * gpe // 2 + 1 + extra) * per

        class First(Group):

            def __init__(self):
                super().__init__(0, 0, 0, 1)

            def number(self, mul, add=0):
                return add - mul

            def landed(self, per, extra=0):
                return extra * per

        def groups(eng, body, tail=None):
            with eng.Fori(0, ne // 2 - 1) as ep:
                for par in range(2):
                    with eng.Fori(0, gpe // 2) as gi:
                        for b in range(2):
                            body(Group(ep, par, gi, b), True)
                    if tail:
                        tail(ep, par)
            ep = ne // 2 - 1
            with eng.Fori(0, gpe // 2) as gi:
                for b in range(2):
                    body(Group(ep, 0, gi, b), True)
            if tail:
                tail(ep, 0)
            with eng.Fori(0, gpe // 2 - 1) as gi:
                for b in range(2):
                    body(Group(ep, 1, gi, b), False)
            for b in range(2):
                body(Group(ep, 1, gpe // 2 - 1, b, last=b == 1), False)

        def start_past(eng, sem_):
            eng.sem_inc(sem_, 2 * PER[sem_])

        with nc.Block() as block:
            @block.sync
            def _(sp):
                def load_weights(e, par):
                    sp.dma_start(w_raw[par][:, :, :], w_experts[bass.ds(e, 1)].rearrange("a p k n -> (a p) k n"))\
                        .then_inc(w_in[par], 16)

                def store(q, split):
                    need_alone(sp, passed["sp"], eo_ready, q.past(eo_ready, 2))
                    sp.dma_start(eo_view[bass.ds(q.e, 1), :, bass.ds(q.j, 4), :].rearrange("a p j d -> (a p) j d"),
                                 eo[q.b][:, :, :]).then_inc(eo_out[q.b], 16)
                    sp.wait_ge(eo_out[q.b], q.landed(16))
                    sp.sem_inc(eo_free, 1)

                def reload(ep, par):
                    if isinstance(ep, int) and ep * 2 + par + 3 >= ne:
                        return
                    e = ep * 2 + par
                    need_alone(sp, passed["sp"], w_lo_ready, e * pieces + 2 * pieces)
                    load_weights(e + 3, 1 - par)

                load_weights(0, 0)
                load_weights(1, 1)
                sp.wait_ge(w_lo_ready, pieces)
                load_weights(2, 0)
                with sp.Fori(0, ne // 2 - 2) as ep:
                    for par in range(2):
                        with sp.Fori(0, gpe // 2) as gi:
                            for b in range(2):
                                store(Group(ep, par, gi, b), True)
                        reload(ep, par)
                for ep in range(ne // 2 - 2, ne // 2):
                    for par in range(2):
                        with sp.Fori(0, gpe // 2) as gi:
                            for b in range(2):
                                store(Group(ep, par, gi, b), True)
                        reload(ep, par)
                for b in range(2):
                    sp.wait_ge(eo_out[b], 16 * ne * gpe // 2)

            @block.gpsimd
            def _(pool):
                ids = slot_tok[:, :, :].rearrange("p e j -> p (e j)")

                def gather(q):
                    b = 1 - q.b
                    need_alone(pool, passed["pool"], xtr_full, q.past(xtr_full, 0))
                    pool.tensor_copy(idc[b][:, :], ids[:, bass.ds(q.number(4, 4), 4)]).then_inc(ids_ready, 1)
                    need_alone(pool, passed["pool"], ids_ready, q.past(ids_ready, 2))
                    for j in range(4):
                        pool.indirect_dma_start(out=xg[b][:, j, :], out_offset=None, in_=x2_dram,
                                                in_offset=bass.IndirectOffsetOnAxis(ap=idc[b][:, j:j + 1], axis=0))\
                            .then_inc(rows_in[b], 16)

                def split_low(par, piece):
                    pool.tensor_tensor(w_lo[par][:, piece, :].rearrange("p a n -> p (a n)"),
                                       w_raw[par][:, piece, :].rearrange("p a n -> p (a n)"),
                                       w_hi[par][:, piece, :].rearrange("p a n -> p (a n)"), ALU.subtract).then_inc(w_lo_ready, 1)

                def body(q, split):
                    if not q.last:
                        gather(q)
                    if split:
                        need_alone(pool, passed["pool"], w_hi_ready, q.number(1, pieces + 1))
                        split_low(1 - q.par, bass.ds(q.piece, 1))

                start_past(pool, ids_ready)
                gather(First())
                for piece in range(pieces):
                    pool.wait_ge(w_hi_ready, piece + 1)
                    split_low(0, bass.ds(piece, 1))
                groups(pool, body)

            @block.tensor
            def _(pe):
                def transposes(q):
                    b = 1 - q.b
                    pe.wait_ge(rows_in[b], q.landed(64, q.b))
                    for dk in range(2):
                        pe.wait_ge(xt_ready, q.past(xt_ready, dk + 1))
                        for j in range(4):
                            mm = pe.transpose(tr_ps[dk][:, j * P:j * P + P], xg[b][:, j, dk * P:dk * P + P], ident[:, :])
                        mm.then_inc(xtr_full, 1)

                def body(q, split):
                    hi, lo = w_hi[q.par], w_lo[q.par]
                    pe.wait_ge(w_lo_ready, q.e * pieces + pieces)
                    pe.wait_ge(xt_ready, q.past(xt_ready, 2))
                    for f in range(fts):
                        pe.wait_ge(gelu_ready, q.past(gelu_ready, f - 3))
                        for dk in range(2):
                            piece, col = 2 * dk + f // 4, (f % 4) * P
                            for n, (w, v) in enumerate(((hi, xt_hi), (hi, xt_lo), (lo, xt_hi))):
                                mm = pe.matmul(h_ps[f % 4][:, :], w[:, piece, col:col + P], v[q.b][:, dk, :],
                                               start=(dk == 0 and n == 0), stop=(dk == 1 and n == 2))
                        mm.then_inc(h_full, 1)
                    if not q.last:
                        transposes(q)
                    for j in range(4):
                        pe.wait_ge(eo_ready, q.past(eo_ready, j // 2 - 1))
                        for f in range(fts):
                            if j == 0:
                                pe.wait_ge(ht_ready, q.past(ht_ready, f + 1))
                            piece, col = 4 + f // 2, (f % 2) * 256
                            for n, (v, w) in enumerate(((ht_hi, hi), (ht_lo, hi), (ht_hi, lo))):
                                mm = pe.matmul(o_ps[:, j, :], v[q.b][:, f, j * P:j * P + P], w[:, piece, col:col + 256],
                                               start=(f == 0 and n == 0), stop=(f == fts - 1 and n == 2))
                        mm.then_inc(o_full, 1)

                start_past(pe, xtr_full)
                start_past(pe, h_full)
                start_past(pe, o_full)
                transposes(First())
                groups(pe, body)

            @block.scalar
            def _(act):
                def split_high(par, piece):
                    act.activation(w_hi[par][:, piece, :].rearrange("p a n -> p (a n)"),
                                   w_raw[par][:, piece, :].rearrange("p a n -> p (a n)"), ACT.Copy).then_inc(w_hi_ready, 1)

                def body(q, split):
                    for f in range(fts):
                        act.wait_ge(h_full, q.past(h_full, f + 1))
                        act.wait_ge(ht_ready, q.past(ht_ready, f - 1))
                        act.activation(h_f[f % 2][:, :], h_ps[f % 4][:, :], ACT.Gelu).then_inc(gelu_ready, 1)
                    if split:
                        act.wait_ge(w_in[1 - q.par], q.ep * 16 + 16 * (1 + q.par))
                        split_high(1 - q.par, bass.ds(q.piece, 1))

                start_past(act, gelu_ready)
                act.wait_ge(w_in[0], 16)
                for piece in range(pieces):
                    split_high(0, bass.ds(piece, 1))
                groups(act, body)

            @block.vector
            def _(dve):
                def split_xt(q):
                    b = 1 - q.b
                    for dk in range(2):
                        dve.wait_ge(xtr_full, q.past(xtr_full, dk + 3))
                        if dk == 0:
                            dve.wait_ge(h_full, q.past(h_full, 0))
                        dve.tensor_copy(xt_hi[b][:, dk, :], tr_ps[dk][:, :]).then_inc(xt_hi_ready, 1)
                        dve.wait_ge(xt_hi_ready, q.past(xt_hi_ready, dk + 3))
                        dve.tensor_tensor(xt_lo[b][:, dk, :], tr_ps[dk][:, :], xt_hi[b][:, dk, :], ALU.subtract)\
                            .then_inc(xt_ready, 1)

                def body(q, split):
                    for f in range(fts):
                        dve.wait_ge(gelu_ready, q.past(gelu_ready, f + 1))
                        if f == 0:
                            dve.wait_ge(o_full, q.past(o_full, -4))
                        dve.tensor_copy(ht_hi[q.b][:, f, :], h_f[f % 2][:, :]).then_inc(ht_hi_ready, 1)
                        dve.wait_ge(ht_hi_ready, q.past(ht_hi_ready, f + 1))
                        dve.tensor_tensor(ht_lo[q.b][:, f, :], h_f[f % 2][:, :], ht_hi[q.b][:, f, :], ALU.subtract)\
                            .then_inc(ht_ready, 1)
                    if not q.last:
                        split_xt(q)
                    for half in range(2):
                        dve.wait_ge(o_full, q.past(o_full, 2 * half + 2))
                        if half == 0:
                            dve.wait_ge(eo_free, q.past(eo_free, -1))
                        dve.tensor_copy(eo[q.b][:, 2 * half:2 * half + 2, :], o_ps[:, 2 * half:2 * half + 2, :]).then_inc(eo_ready, 1)

                for s_ in (xt_hi_ready, xt_ready, ht_hi_ready, ht_ready, eo_ready, eo_free):
                    start_past(dve, s_)
                split_xt(First())
                groups(dve, body)


def combine(nc, g):
    tiles, routes, gates = g["tiles"], g["routes"], g["gates"]
    eo_dram = g["eo_dram"]
    h2_dram = g["h2_dram"].rearrange("(q l p) d -> q p l d", l=2, p=P)
    out = g["out"].rearrange("q (l p) d -> q p l d", l=2)
    with ExitStack() as ctx:
        def sb(name, shape, dt=F32):
            return ctx.enter_context(nc.sbuf_tensor(name, shape, dt))

        def sem(name):
            return ctx.enter_context(nc.semaphore(name))

        idx = [sb(f"cidx{b}", [P, 2, 2], U32) for b in range(2)]
        gate = [sb(f"cgate{b}", [P, 2, 2]) for b in range(2)]
        got = [sb(f"got{b}", [P, 2, 2, 256]) for b in range(2)]
        res = [sb(f"res{b}", [P, 2, 256]) for b in range(2)]
        acc = [sb(f"acc{b}", [P, 2, 256]) for b in range(2)]
        sums = [sb(f"sums{b}", [P, 2, 256]) for b in range(2)]
        got_in = g["got_in"]
        res_in = [sem(f"res_in{b}") for b in range(2)]
        sum_out = [sem(f"sum_out{b}") for b in range(2)]
        idx_ready = sem("idx2_ready")
        gate_ready = sem("gate_ready")
        first_done = sem("first_done")
        sums_done = sem("sums_done")
        sums_free = sem("sums_free")
        passed = g["passed"]
        rounds = tiles // 4

        with nc.Block() as block:
            @block.sync
            def _(sp):
                def load(j, b):
                    sp.dma_start(res[b][:, :, :], h2_dram[bass.ds(j * 2 + b, 1)].rearrange("a p l d -> (a p) l d")).then_inc(res_in[b], 16)

                for b in range(2):
                    load(0, b)
                with sp.Fori(0, rounds - 1) as j:
                    for b in range(2):
                        need_alone(sp, passed["sp"], sums_done, j * 4 + (2 * b + 6))
                        sp.dma_start(out[bass.ds(j * 2 + b, 1)].rearrange("a p l d -> (a p) l d"), sums[b][:, :, :]).then_inc(sum_out[b], 16)
                        load(j + 1, b)
                        sp.wait_ge(sum_out[b], j * 16 + 16)
                        sp.sem_inc(sums_free, 1)
                for b in range(2):
                    sp.wait_ge(sums_done, (rounds - 1) * 4 + 2 * b + 6)
                    sp.dma_start(out[2 * rounds - 2 + b], sums[b][:, :, :]).then_inc(sum_out[b], 16)
                for b in range(2):
                    sp.wait_ge(sum_out[b], 16 * rounds)

            @block.gpsimd
            def _(pool):
                with pool.Fori(0, rounds) as j:
                    for b in range(2):
                        need_alone(pool, passed["pool"], sums_done, j * 4 + (2 * b + 2))
                        pool.tensor_copy(idx[b][:, :, :], routes[:, :, bass.ds(j * 4 + 2 * b, 2)]).then_inc(idx_ready, 1)
                        need_alone(pool, passed["pool"], idx_ready, j * 2 + (b + 1))
                        for c in range(2):
                            for l in range(2):
                                pool.indirect_dma_start(out=got[b][:, c, l, :], out_offset=None, in_=eo_dram,
                                                        in_offset=bass.IndirectOffsetOnAxis(ap=idx[b][:, c, l:l + 1], axis=0))\
                                    .then_inc(got_in[b], 16)

            @block.vector
            def _(dve):
                dve.sem_inc(sums_done, 4)
                dve.sem_inc(sums_free, 2)
                with dve.Fori(0, rounds) as j:
                    for b in range(2):
                        dve.tensor_copy(gate[b][:, :, :], gates[:, :, bass.ds(j * 4 + 2 * b, 2)]).then_inc(gate_ready, 1)
                        dve.wait_ge(gate_ready, j * 2 + (b + 1))
                        dve.wait_ge(got_in[b], j * 64 + 64)
                        dve.wait_ge(res_in[b], j * 16 + 16)
                        for l in range(2):
                            dve.scalar_tensor_tensor(out=acc[b][:, l, :], in0=got[b][:, 0, l, :], scalar=gate[b][:, 0, l:l + 1],
                                                     in1=res[b][:, l, :], op0=ALU.mult, op1=ALU.add).then_inc(first_done, 1)
                        dve.wait_ge(sums_free, j * 2 + (b + 1))
                        for l in range(2):
                            dve.wait_ge(first_done, j * 4 + (2 * b + l + 1))
                            dve.scalar_tensor_tensor(out=sums[b][:, l, :], in0=got[b][:, 1, l, :], scalar=gate[b][:, 1, l:l + 1],
                                                     in1=acc[b][:, l, :], op0=ALU.mult, op1=ALU.add).then_inc(sums_done, 1)


def _pieces(gate, down):
    import numpy as _np

    e, d, f = gate.shape
    gate = gate.reshape(e, d // P, P, f // 512, 512).transpose(0, 2, 1, 3, 4).reshape(e, P, -1, 512)
    down = down.reshape(e, f // (2 * P), 2, P, d).transpose(0, 3, 1, 2, 4).reshape(e, P, -1, 512)
    return _np.concatenate([gate, down], axis=2)


def kernel(**inputs):
    import numpy as _np
    import concourse.bacc as _bacc
    from concourse import mybir as _mybir
    from concourse.bass_utils import run_bass_kernel_spmd as _run

    a = {k: _np.asarray(v) for k, v in inputs.items()}
    n, c, l, h = a["x"].shape
    tok, att, ffn = "L0_tok_", "L0_attn_", "L0_ffn_"
    host = {
        "x": a["x"].reshape(n, c, l * h),
        "wkv": _np.stack([a[tok + "Wk_w"].T, a[tok + "Wv_w"].T]), "wq": a[tok + "Wq_w"].T,
        "bkv": _np.stack([a[tok + "Wk_b"], a[tok + "Wv_b"]]), "bq_tok": a[tok + "Wq_b"],
        "w_bias_t": a[tok + "w_bias"].T, "mask_t": a[tok + "local_mask"].T,
        "out_w": a[tok + "out_w"], "out_b": a[tok + "out_b"], "ln_g": a[tok + "ln_g"], "ln_b": a[tok + "ln_b"],
        "wq_t": a[att + "Wq"].T, "bq": a[att + "bq"], "wk_t": a[att + "Wk"].T, "bk": a[att + "bk"],
        "wv_t": a[att + "Wv"].T, "bv": a[att + "bv"], "wo_t": a[att + "Wo"].T, "bo": a[att + "bo"],
        "beta": a[att + "beta"], "t_par": a[att + "t"], "ln_w": a[att + "ln_w"], "ln_b2": a[att + "ln_b"],
        "wg": a[ffn + "wg"], "w_experts": _pieces(a[ffn + "w_gate"], a[ffn + "w_down"]),
    }
    nc = _bacc.Bacc("TRN2", target_bir_lowering=False, num_devices=1)
    arrays, dram = {}, {}
    for name in host:
        v = _np.ascontiguousarray(host[name])
        arrays[f"in_{name}"] = v
        dram[name] = nc.dram_tensor(f"in_{name}", v.shape, _mybir.dt.from_np(v.dtype), kind="ExternalInput").ap()
    dram["out"] = nc.dram_tensor("out_0", (n, l, c * h), _mybir.dt.from_np(_np.dtype("float32")), kind="ExternalOutput").ap()
    tower_program(nc, **dram)
    r = _run(nc, [arrays], core_ids=[0])
    return r.results[0]["out_0"]
```
